# Optimizing a Trainium2 kernel written in Bass

```python
import numpy as np
import jax
import jax.numpy as jnp

def _softmax(x, axis=-1):
    return jax.nn.softmax(x, axis=axis)

def _gelu(x):
    return jax.nn.gelu(x, approximate=True)

def _silu(x):
    return jax.nn.silu(x)

def _sigmoid(x):
    return jax.nn.sigmoid(x)

def _layernorm(x, axis=-1, eps=1e-05):
    m = jnp.mean(x, axis=axis, keepdims=True)
    v = jnp.var(x, axis=axis, keepdims=True)
    return (x - m) / jnp.sqrt(v + eps)

def _scatter_add(tgt, idx, src, axis=0):
    return tgt.at[idx].add(src)

def _segment_sum(src, seg, n):
    return jax.ops.segment_sum(src, seg, n)
kernel_name = 'mk_prb_d2_jaxref_r4_83c490'

def setup_inputs(seed: int=0):
    np.random.seed(seed)
    _w = jnp.asarray

    def _L0_attn_setup():
        import jax, jax.numpy as jnp
        import numpy as np
        B, N, D = (2, 512, 256)
        H = 16
        DH = D // H
        WINDOW = 64
        SCALE = 1.0 / np.sqrt(DH).astype(np.float32)

        def _causal_window_mask(n: int) -> jnp.ndarray:
            pos = jnp.arange(n)
            diff = pos[:, None] - pos[None, :]
            return (diff >= 0) & (diff < WINDOW)
        key = jax.random.key(seed)
        k1, k2, k3 = jax.random.split(key, 3)
        lim_qkv = np.sqrt(6.0 / (D + 3 * D)).astype(np.float32)
        lim_out = np.sqrt(6.0 / (D + D)).astype(np.float32)
        x = jax.random.normal(k1, (B, N, D), dtype=jnp.float32)
        Wqkv = jax.random.uniform(k2, (3 * D, D), dtype=jnp.float32, minval=-lim_qkv, maxval=lim_qkv)
        bqkv = jnp.zeros((3 * D,), dtype=jnp.float32)
        Wout = jax.random.uniform(k3, (D, D), dtype=jnp.float32, minval=-lim_out, maxval=lim_out)
        bout = jnp.zeros((D,), dtype=jnp.float32)
        return {'x': x, 'Wqkv': Wqkv, 'bqkv': bqkv, 'Wout': Wout, 'bout': bout}
    _L0_attn_in = _L0_attn_setup()

    def _L0_ffn_setup():
        import jax, jax.numpy as jnp
        import numpy as np
        D_MODEL = 256
        key = jax.random.key(seed)
        k_x, k_w, k_a1, k_a2 = jax.random.split(key, 4)
        x = jax.random.normal(k_x, (4, 512, D_MODEL), dtype=jnp.float32)
        weight = jax.random.normal(k_w, (D_MODEL, D_MODEL), dtype=jnp.float32) * 0.02
        aux_weight1 = jax.random.normal(k_a1, (D_MODEL, D_MODEL), dtype=jnp.float32) * 0.02
        aux_weight2 = jax.random.normal(k_a2, (D_MODEL, D_MODEL), dtype=jnp.float32) * 0.02
        bias = jnp.zeros((D_MODEL,), dtype=jnp.float32)
        return {'x': x, 'weight': weight, 'aux_weight1': aux_weight1, 'aux_weight2': aux_weight2, 'bias': bias}
    _L0_ffn_in = _L0_ffn_setup()

    def _L1_attn_setup():
        import jax, jax.numpy as jnp
        import numpy as np
        DT_RANK = 64
        N_STATES = 16

        def selective_scan(u, delta, A, B, C, D):
            dA = jnp.einsum('bld,dn->bldn', delta, A)
            dB_u = jnp.einsum('bld,bld,bln->bldn', delta, u, B)
            dA_shift = jnp.concatenate([dA[:, 1:], jnp.zeros_like(dA[:, :1])], axis=1)
            dA_cumsum = jnp.exp(jnp.flip(jnp.cumsum(jnp.flip(dA_shift, axis=1), axis=1), axis=1))
            xs = jnp.cumsum(dB_u * dA_cumsum, axis=1) / (dA_cumsum + 1e-12)
            y = jnp.einsum('bldn,bln->bld', xs, C)
            return y + u * D
        key = jax.random.key(seed)
        ks = jax.random.split(key, 6)
        b, l, d = (2, 256, 256)
        dt_rank, n = (DT_RANK, N_STATES)
        x = jax.random.normal(ks[0], (b, l, d), dtype=jnp.float32)
        W_x = jax.random.normal(ks[1], (d, dt_rank + 2 * n), dtype=jnp.float32) * (1.0 / np.sqrt(d))
        W_dt = jax.random.normal(ks[2], (dt_rank, d), dtype=jnp.float32) * (1.0 / np.sqrt(dt_rank))
        b_dt = jnp.zeros((d,), dtype=jnp.float32)
        A_log = jnp.log(jnp.tile(jnp.arange(1, n + 1, dtype=jnp.float32)[None, :], (d, 1)))
        D = jnp.ones((d,), dtype=jnp.float32)
        W_out = jax.random.normal(ks[3], (d, d), dtype=jnp.float32) * (1.0 / np.sqrt(d))
        b_out = jnp.zeros((d,), dtype=jnp.float32)
        return {'x': x, 'W_x': W_x, 'W_dt': W_dt, 'b_dt': b_dt, 'A_log': A_log, 'D': D, 'W_out': W_out, 'b_out': b_out}
    _L1_attn_in = _L1_attn_setup()

    def _L1_ffn_setup():
        import jax, jax.numpy as jnp
        import numpy as np
        D_MODEL = 256
        HIDDEN = 512
        MOE_DIM = 64
        N_EXPERTS = 8
        TOP_K = 2
        EXP_HIDDEN = HIDDEN // 2
        B, S = (4, 512)
        key = jax.random.key(seed)
        ks = jax.random.split(key, 20)

        def w(k, shape, fan_in):
            return (jax.random.normal(k, shape, dtype=jnp.float32) / np.sqrt(fan_in)).astype(jnp.float32)
        return {'inputs_embeds': jax.random.normal(ks[0], (B, S, D_MODEL), dtype=jnp.float32), 'enc_w': w(ks[1], (D_MODEL, HIDDEN), D_MODEL), 'enc_b': jnp.zeros((HIDDEN,), jnp.float32), 's2c_w': w(ks[2], (HIDDEN, MOE_DIM), HIDDEN), 's2c_b': jnp.zeros((MOE_DIM,), jnp.float32), 'r_w1': w(ks[3], (MOE_DIM, 64), MOE_DIM), 'r_b1': jnp.zeros((64,), jnp.float32), 'r_w2': w(ks[4], (64, N_EXPERTS), 64), 'r_b2': jnp.zeros((N_EXPERTS,), jnp.float32), 'e_w1': w(ks[5], (N_EXPERTS, MOE_DIM, EXP_HIDDEN), MOE_DIM), 'e_b1': jnp.zeros((N_EXPERTS, EXP_HIDDEN), jnp.float32), 'e_w2': w(ks[6], (N_EXPERTS, EXP_HIDDEN, MOE_DIM), EXP_HIDDEN), 'e_b2': jnp.zeros((N_EXPERTS, MOE_DIM), jnp.float32), 'c2s_w': w(ks[7], (MOE_DIM, HIDDEN), MOE_DIM), 'c2s_b': jnp.zeros((HIDDEN,), jnp.float32), 'dec_w': w(ks[8], (HIDDEN, D_MODEL), HIDDEN), 'dec_b': jnp.zeros((D_MODEL,), jnp.float32), 'ln_g': jnp.ones((D_MODEL,), jnp.float32), 'ln_b': jnp.zeros((D_MODEL,), jnp.float32)}
    _L1_ffn_in = _L1_ffn_setup()
    _d = {'L0_attn_x': _L0_attn_in['x'], 'L0_attn_Wqkv': _L0_attn_in['Wqkv'], 'L0_attn_bqkv': _L0_attn_in['bqkv'], 'L0_attn_Wout': _L0_attn_in['Wout'], 'L0_attn_bout': _L0_attn_in['bout'], 'L0_ffn_weight': _L0_ffn_in['weight'], 'L0_ffn_aux_weight1': _L0_ffn_in['aux_weight1'], 'L0_ffn_aux_weight2': _L0_ffn_in['aux_weight2'], 'L0_ffn_bias': _L0_ffn_in['bias'], 'L1_attn_W_x': _L1_attn_in['W_x'], 'L1_attn_W_dt': _L1_attn_in['W_dt'], 'L1_attn_b_dt': _L1_attn_in['b_dt'], 'L1_attn_A_log': _L1_attn_in['A_log'], 'L1_attn_D': _L1_attn_in['D'], 'L1_attn_W_out': _L1_attn_in['W_out'], 'L1_attn_b_out': _L1_attn_in['b_out'], 'L1_ffn_enc_w': _L1_ffn_in['enc_w'], 'L1_ffn_enc_b': _L1_ffn_in['enc_b'], 'L1_ffn_s2c_w': _L1_ffn_in['s2c_w'], 'L1_ffn_s2c_b': _L1_ffn_in['s2c_b'], 'L1_ffn_r_w1': _L1_ffn_in['r_w1'], 'L1_ffn_r_b1': _L1_ffn_in['r_b1'], 'L1_ffn_r_w2': _L1_ffn_in['r_w2'], 'L1_ffn_r_b2': _L1_ffn_in['r_b2'], 'L1_ffn_e_w1': _L1_ffn_in['e_w1'], 'L1_ffn_e_b1': _L1_ffn_in['e_b1'], 'L1_ffn_e_w2': _L1_ffn_in['e_w2'], 'L1_ffn_e_b2': _L1_ffn_in['e_b2'], 'L1_ffn_c2s_w': _L1_ffn_in['c2s_w'], 'L1_ffn_c2s_b': _L1_ffn_in['c2s_b'], 'L1_ffn_dec_w': _L1_ffn_in['dec_w'], 'L1_ffn_dec_b': _L1_ffn_in['dec_b'], 'L1_ffn_ln_g': _L1_ffn_in['ln_g'], 'L1_ffn_ln_b': _L1_ffn_in['ln_b']}
    _x0 = _d['L0_attn_x']
    _d['L0_attn_x'] = jax.random.normal(jax.random.fold_in(jax.random.key(seed), 1), (32, 512, 256), dtype=_x0.dtype)
    del _x0
    return _d

def reference(L0_attn_x, L0_attn_Wqkv, L0_attn_bqkv, L0_attn_Wout, L0_attn_bout, L0_ffn_weight, L0_ffn_aux_weight1, L0_ffn_aux_weight2, L0_ffn_bias, L1_attn_W_x, L1_attn_W_dt, L1_attn_b_dt, L1_attn_A_log, L1_attn_D, L1_attn_W_out, L1_attn_b_out, L1_ffn_enc_w, L1_ffn_enc_b, L1_ffn_s2c_w, L1_ffn_s2c_b, L1_ffn_r_w1, L1_ffn_r_b1, L1_ffn_r_w2, L1_ffn_r_b2, L1_ffn_e_w1, L1_ffn_e_b1, L1_ffn_e_w2, L1_ffn_e_b2, L1_ffn_c2s_w, L1_ffn_c2s_b, L1_ffn_dec_w, L1_ffn_dec_b, L1_ffn_ln_g, L1_ffn_ln_b):

    def _L0_attn_ref(x, Wqkv, bqkv, Wout, bout):
        import jax, jax.numpy as jnp
        import numpy as np
        B, N, D = (2, 512, 256)
        H = 16
        DH = D // H
        WINDOW = 64
        SCALE = 1.0 / np.sqrt(DH).astype(np.float32)

        def _causal_window_mask(n: int) -> jnp.ndarray:
            pos = jnp.arange(n)
            diff = pos[:, None] - pos[None, :]
            return (diff >= 0) & (diff < WINDOW)
        b, n, d = x.shape
        qkv = x @ Wqkv.T + bqkv
        qkv = qkv.reshape(b, n, 3, H, DH)
        qkv = jnp.transpose(qkv, (2, 0, 3, 1, 4))
        q, k, v = (qkv[0], qkv[1], qkv[2])
        scores = jnp.einsum('bhqd,bhkd->bhqk', q, k) * SCALE
        mask = _causal_window_mask(n)
        neg_inf = jnp.asarray(-jnp.inf, dtype=scores.dtype)
        scores = jnp.where(mask[None, None], scores, neg_inf)
        attn = jax.nn.softmax(scores, axis=-1)
        out = jnp.einsum('bhqk,bhkd->bhqd', attn, v)
        out = jnp.transpose(out, (0, 2, 1, 3)).reshape(b, n, d)
        return out @ Wout.T + bout

    def _L0_ffn_ref(x, weight, aux_weight1, aux_weight2, bias):
        import jax, jax.numpy as jnp
        import numpy as np
        D_MODEL = 256
        h = jnp.einsum('btc,cd->btd', x, weight)
        h = jnp.einsum('btc,cd->btd', h, aux_weight1)
        h = jnp.einsum('btc,cd->btd', h, aux_weight2)
        return jnp.tanh(h + bias)

    def _L1_attn_ref(x, W_x, W_dt, b_dt, A_log, D, W_out, b_out):
        import jax, jax.numpy as jnp
        import numpy as np
        DT_RANK = 64
        N_STATES = 16

        def selective_scan(u, delta, A, B, C, D):
            dA = jnp.einsum('bld,dn->bldn', delta, A)
            dB_u = jnp.einsum('bld,bld,bln->bldn', delta, u, B)
            dA_shift = jnp.concatenate([dA[:, 1:], jnp.zeros_like(dA[:, :1])], axis=1)
            dA_cumsum = jnp.exp(jnp.flip(jnp.cumsum(jnp.flip(dA_shift, axis=1), axis=1), axis=1))
            xs = jnp.cumsum(dB_u * dA_cumsum, axis=1) / (dA_cumsum + 1e-12)
            y = jnp.einsum('bldn,bln->bld', xs, C)
            return y + u * D
        n = A_log.shape[1]
        A = -jnp.exp(A_log)
        x_dbl = jnp.einsum('bld,de->ble', x, W_x)
        delta = x_dbl[..., :DT_RANK]
        B = x_dbl[..., DT_RANK:DT_RANK + n]
        C = x_dbl[..., DT_RANK + n:]
        delta = jax.nn.softplus(jnp.einsum('blr,rd->bld', delta, W_dt) + b_dt)
        y = selective_scan(x, delta, A, B, C, D)
        return jnp.einsum('bld,de->ble', y, W_out) + b_out

    def _L1_ffn_ref(inputs_embeds, enc_w, enc_b, s2c_w, s2c_b, r_w1, r_b1, r_w2, r_b2, e_w1, e_b1, e_w2, e_b2, c2s_w, c2s_b, dec_w, dec_b, ln_g, ln_b):
        import jax, jax.numpy as jnp
        import numpy as np
        D_MODEL = 256
        HIDDEN = 512
        MOE_DIM = 64
        N_EXPERTS = 8
        TOP_K = 2
        EXP_HIDDEN = HIDDEN // 2
        B, S = (4, 512)
        b, s, _ = inputs_embeds.shape
        spikes = jax.nn.sigmoid(inputs_embeds @ enc_w + enc_b)
        cont = spikes.reshape(b * s, -1) @ s2c_w + s2c_b
        rh = jax.nn.relu(cont @ r_w1 + r_b1)
        probs = jax.nn.softmax(rh @ r_w2 + r_b2, axis=-1)
        topw, topi = jax.lax.top_k(probs, TOP_K)
        topw = topw / jnp.sum(topw, axis=-1, keepdims=True)
        comb = jnp.sum(jax.nn.one_hot(topi, N_EXPERTS, dtype=cont.dtype) * topw[..., None], axis=1)
        eh = jax.nn.relu(jnp.einsum('nd,edh->neh', cont, e_w1) + e_b1)
        eo = jnp.einsum('neh,ehd->ned', eh, e_w2) + e_b2
        moe_out = jnp.einsum('ned,ne->nd', eo, comb)
        rates = jax.nn.sigmoid(moe_out @ c2s_w + c2s_b)
        x = rates.reshape(b, s, -1)
        dec = jax.nn.sigmoid(x @ dec_w + dec_b)
        mu = jnp.mean(dec, axis=-1, keepdims=True)
        var = jnp.var(dec, axis=-1, keepdims=True)
        return (dec - mu) * jax.lax.rsqrt(var + 1e-05) * ln_g + ln_b
    x = L0_attn_x
    xn = _layernorm(x, axis=-1)
    x = x + _L0_attn_ref(xn, L0_attn_Wqkv, L0_attn_bqkv, L0_attn_Wout, L0_attn_bout) + _L0_ffn_ref(xn, L0_ffn_weight, L0_ffn_aux_weight1, L0_ffn_aux_weight2, L0_ffn_bias)
    xn = _layernorm(x, axis=-1)
    x = x + _L1_attn_ref(xn, L1_attn_W_x, L1_attn_W_dt, L1_attn_b_dt, L1_attn_A_log, L1_attn_D, L1_attn_W_out, L1_attn_b_out) + _L1_ffn_ref(xn, L1_ffn_enc_w, L1_ffn_enc_b, L1_ffn_s2c_w, L1_ffn_s2c_b, L1_ffn_r_w1, L1_ffn_r_b1, L1_ffn_r_w2, L1_ffn_r_b2, L1_ffn_e_w1, L1_ffn_e_b1, L1_ffn_e_w2, L1_ffn_e_b2, L1_ffn_c2s_w, L1_ffn_c2s_b, L1_ffn_dec_w, L1_ffn_dec_b, L1_ffn_ln_g, L1_ffn_ln_b)
    return x

_drawn_inputs = setup_inputs


def setup_inputs(seed=0):
    import zlib

    import numpy as np

    out = dict(_drawn_inputs(seed))
    spreads = {'L0_attn_bqkv': (0.0, 0.1),
     'L0_attn_bout': (0.0, 0.1),
     'L0_ffn_bias': (0.0, 0.1),
     'L1_attn_b_dt': (0.0, 0.1),
     'L1_attn_D': (1.0, 0.2),
     'L1_attn_b_out': (0.0, 0.1),
     'L1_ffn_enc_b': (0.0, 0.397),
     'L1_ffn_s2c_b': (0.0, 0.1),
     'L1_ffn_r_b1': (0.0, 0.1),
     'L1_ffn_r_b2': (0.0, 0.1),
     'L1_ffn_e_b1': (0.0, 0.661),
     'L1_ffn_e_b2': (0.0, 0.418),
     'L1_ffn_c2s_b': (0.0, 0.289),
     'L1_ffn_dec_b': (0.0, 0.1),
     'L1_ffn_ln_g': (1.0, 0.2),
     'L1_ffn_ln_b': (0.0, 0.1)}
    factors = {}
    for name, (base, spread) in spreads.items():
        noise = np.random.default_rng([zlib.crc32(name.encode()), seed]).standard_normal(out[name].shape)
        drawn = base * np.exp(spread * noise) if base else spread * noise
        out[name] = jnp.asarray(drawn.astype(out[name].dtype))
    for name, factor in factors.items():
        out[name] = (out[name] * factor).astype(out[name].dtype)
    return out
```

```python
from contextlib import ExitStack

import concourse.bass as bass
from concourse import mybir


def layered_kernel(nc, x_in, w, out):
    F32 = mybir.dt.float32
    BF16 = mybir.dt.bfloat16
    ALU = mybir.AluOpType
    ACT = mybir.ActivationFunctionType
    AX = mybir.AxisListType

    B, L, D = x_in.shape
    P = 128
    T = L // P
    KC = D // P
    H, WINDOW = 16, 64
    DH = D // H
    HH = P // DH
    G = 4
    KW = P + WINDOW
    NEG = -1e30
    N_STATES = w["L1_attn_A_log"].shape[1]
    RANK = w["L1_attn_W_dt"].shape[0]
    XD = RANK + 2 * N_STATES
    HID = w["L1_ffn_enc_w"].shape[1]
    MH = HID // P
    E, MD, EH = w["L1_ffn_e_w1"].shape
    EK = EH // P
    Q = 4
    NQ = N_STATES // Q
    LN_EPS = 1e-5
    SCAN_EPS = 1e-12
    UNITS = [(hf, a, t) for hf in range(KC) for a in range(HH // G) for t in range(T)]
    NU = len(UNITS)
    ZERO_FROM = 110.0

    ctx = ExitStack()
    with ctx:
        def sb(name, shape, dt=F32):
            return ctx.enter_context(nc.sbuf_tensor(name, shape, dt))

        ident = sb("ident", [P, P])
        ident16 = sb("ident16", [P, P], BF16)
        ones = sb("ones", [P, P])
        ones16 = sb("ones16", [P, P], BF16)
        upto = sb("upto", [P, P])
        after = sb("after", [P, P])
        mask = sb("mask", [P, 2, KW], BF16)
        mask0 = sb("mask0", [P, 2, KW], BF16)
        headsel = sb("headsel", [P, HH])
        lower = sb("lower", [P, T * E, E])
        eps1 = sb("eps1", [P, T])
        eps4 = sb("eps4", [P, T])
        mhalf = sb("mhalf", [P, T])
        wqkvT = sb("wqkvT", [P, KC, 3 * D])
        woaT = sb("woaT", [P, 2, KC, D])
        wfused = sb("wfused", [P, KC, D])
        wx = sb("wx", [P, KC, XD])
        wdt = sb("wdt", [RANK, D])
        wo1 = sb("wo1", [P, KC, D])
        wenc = sb("wenc", [P, KC, HID])
        ws2c = sb("ws2c", [P, MH, 2, MD])
        wr1 = sb("wr1", [P, MD])
        wr2 = sb("wr2", [MD + 1, E])
        we1 = sb("we1", [P, E, EH])
        we2 = sb("we2", [P, E, EK, MD])
        wc2s = sb("wc2s", [P, HID])
        wdec = sb("wdec", [P, MH, D])
        decay = sb("decay", [P, N_STATES, D])
        d_all = sb("d_all", [P, D])
        lng_all = sb("lng_all", [P, D])
        bqk = sb("bqk", [P, 2, KC])
        benc = sb("benc", [P, MH])
        bs2c = sb("bs2c", [P, 1])
        br1 = sb("br1", [MD, 1])
        be1 = sb("be1", [P, E, EK])
        bc2s = sb("bc2s", [P, MH])
        BV, BFFN, BDT, BOUT, BOUT1, BDEC, BE2 = range(7)
        biasrow = sb("biasrow", [P, 7, 512], BF16)

        xb = sb("xb", [P, T, D])
        xn = sb("xn", [P, T, D])
        xnT = sb("xnT", [P, KC, L])
        qT = sb("qT", [P, KC, L])
        kT = sb("kT", [P, KC, WINDOW + L])
        vh = sb("vh", [P, T, H, 2 * DH])
        th = sb("th", [P, T, D])
        pr = [sb(f"pr{i}", [P, G, 2 * P]) for i in range(2)]
        prT = [sb(f"prT{i}", [P, G, 2, P]) for i in range(2)]
        aT = sb("aT", [P, KC, L])
        x1 = sb("x1", [P, T, D])
        big = sb("big", [P, 8 * 1024])
        qm = big[:, :].rearrange("p (h l) -> p h l", h=HH * KC)
        tmp = [big[:, 1024 * i:1024 * (i + 1)].rearrange("p (q d) -> p q d", q=Q) for i in range(8)]
        e_t, ee_t = tmp[0:NQ], tmp[NQ:2 * NQ]
        x_t = [p[:, :, :, :].rearrange("p q w l -> p q (w l)") for p in prT]
        f_later = th[:, :, :]
        x_later = qT[:, :, :].rearrange("p k (a d) -> p (k a) d", d=D)
        least_a = sb("least_a", [P, NQ])
        least_t = sb("least_t", [P, T - 1])
        past = sb("past", [P, NQ, T - 1])
        first_c = sb("first_c", [P, NQ], mybir.dt.int32)
        stat = sb("stat", [P, T, 6])
        mv = sb("mv", [P, T, 2])
        rstd = sb("rstd", [P, T])
        nmax = sb("nmax", [P, 2, G])
        psm = sb("psm", [P, 2, G])
        prc = sb("prc", [P, 2, G])
        xdT = sb("xdT", [XD, L])
        bc = sb("bc", [P, T, 2 * N_STATES])
        z = sb("z", [P, T, D])
        az = sb("az", [P, T, D])
        delta, gg = az, z
        dsum = sb("dsum", [P, 2, D])
        tail = sb("tail", [P, T, D])
        fsum = sb("fsum", [P, NQ, Q * D])
        ysum = sb("ysum", [P, T, D])
        hidT = big[:, 0:MH * L].rearrange("p (m l) -> p m l", m=MH)
        contT = sb("contT", [P, L])
        rhT = sb("rhT", [MD + 1, L])
        rt = sb("rt", [P, 8, T * E])
        pair = sb("pair", [P, 2, T * E * E])
        rs = sb("rs", [P, 4, T])
        eh = [big[:, (MH + EK * i) * L:(MH + EK * (i + 1)) * L].rearrange("p (k l) -> p k l", k=EK) for i in range(2)]
        moe = sb("moe", [P, T, MD])
        moeT = sb("moeT", [P, L])
        ob = tail
        xn2, xn2T, yT, td = xn, xnT, aT, th
        m1 = z[:, :, :].rearrange("p (a t) d -> p a (t d)", a=2)

        ps = [ctx.enter_context(nc.psum_tensor(f"ps{i}", [P, 1024], F32)) for i in range(4)]

        s_slot = [(2, 0, 1)[u % 3] for u in range(NU)]
        W_LOADS = 76
        C_ALL = 33
        WT_ALL = 83
        PER = {}

        def sem(name, per):
            s = ctx.enter_context(nc.semaphore(name))
            PER[id(s)] = per
            return s

        w_in = sem("w_in", 0)
        cdone = sem("cdone", 0)
        const = sem("const", 0)
        wt_ps = sem("wt_ps", 0)
        wt = sem("wt", 0)
        x_in_s = sem("x_loaded", 16)
        stored = sem("stored", 16)
        passed = sem("passed", 0)
        stats = [sem(f"stats{i}", T) for i in range(3)]
        aggr = [sem(f"aggr{i}", T) for i in range(3)]
        var = [sem(f"var{i}", 1) for i in range(3)]
        rstd_s = [sem(f"rstd{i}", 1) for i in range(3)]
        xn_s = [sem(f"xnorm{i}", T) for i in range(2)]
        xnT_ps = [sem(f"xnT_ps{i}", 1) for i in range(2)]
        xnT_s = [sem(f"xnT{i}", 1) for i in range(2)]
        q_ps = sem("q_ps", 1)
        k_ps = sem("k_ps", 1)
        v_ps = sem("v_ps", 1)
        h_ps = sem("h_ps", 1)
        q_s = sem("q", KC)
        k_s = sem("k", KC)
        v_s = sem("v", 2)
        th_s = sem("th", 1)
        qm_s = sem("qm", 4)
        s_ps = sem("score_ps", NU)
        nmax_s = sem("nmax", NU)
        pexp = sem("pexp", NU * G)
        prc_s = sem("prc", NU)
        pn = sem("pnorm", NU)
        pT_ps = sem("pT_ps", NU)
        pT_s = sem("pT", NU)
        pv = sem("pv", NU)
        aT_s = sem("aT", 1)
        y0_ps = sem("y0_ps", 1)
        xth = sem("x_plus_tanh", 1)
        x1_s = sem("x1", 1)
        xd_ps = sem("xd_ps", 1)
        xd_s = sem("xd", 1)
        dt_ps = sem("dt_ps", 1)
        bc_ps = sem("bc_ps", 1)
        bc_s = sem("bc", 1)
        z_s = sem("z", 1)
        az_s = sem("az", 1)
        ez_s = sem("ez", 1)
        lz_s = sem("lz", 1)
        delta_s = sem("delta", 1)
        g_s = sem("g", 1)
        dsum_s = sem("dsum", 2)
        yu = sem("yu", 1)
        tail_ps = sem("tail_ps", 1)
        tail_s = sem("tail", 1)
        first_s = sem("first", 6)
        et = sem("et", NQ)
        ee1 = sem("e", NQ)
        ee2 = sem("e_eps", NQ)
        f_s = sem("f", NQ)
        rc_s = sem("rc", NQ)
        sc_ps = sem("scan_ps", NQ)
        xx = sem("xx", NQ)
        ya = sem("yadd", NQ * 3)
        et_l = sem("et_later", 0)
        e_l = sem("e_later", 0)
        ln_l = sem("e_eps_later", 0)
        rc_l = sem("rc_later", 0)
        f_l = sem("f_later", 0)
        ps_l = sem("scan_ps_later", 0)
        x_l = sem("xx_later", 0)
        fs_l = sem("fsum_later", 0)
        y_l = sem("yadd_later", 0)
        yT_ps = sem("yT_ps", 1)
        yT_s = sem("yT", 1)
        y1_ps = sem("y1_ps", 1)
        x2_s = sem("x2", 1)
        enc_ps = sem("enc_ps", 2)
        ts = sem("spikes", MH)
        cont_ps = sem("cont_ps", 1)
        cont_s = sem("cont", 1)
        rh_ps = sem("rh_ps", 1)
        rh_s = sem("rh", 1)
        lg_ps = sem("lg_ps", 1)
        route = sem("route", 11)
        rexp = sem("rexp", 1)
        e1_ps = sem("e1_ps", E)
        eha = sem("eh_a", E)
        ehv = sem("eh_v", E)
        e2_ps = sem("e2_ps", E)
        m1_s = sem("m1", T)
        moe_s = sem("moe", T)
        mT_ps = sem("mT_ps", 1)
        mT_s = sem("mT", 1)
        c2s_ps = sem("c2s_ps", 2)
        tr = sem("rates", MH)
        dec_ps = sem("dec_ps", 1)
        td_s = sem("td", 1)
        n3 = sem("n3", T)
        out_s = sem("out_ready", T)

        block = ctx.enter_context(nc.Block())

        x_v = x_in.rearrange("b (t p) d -> b p t d", p=P)
        o_v = out.rearrange("b (t p) d -> b p t d", p=P)

        wqkv_n = big[:, 0:6 * D].rearrange("p (m c) -> p m c", m=6)
        wo_n = big[:, 6 * D:8 * D].rearrange("p (m c) -> p m c", m=2)
        a1_n = big[:, 8 * D:10 * D].rearrange("p (m c) -> p m c", m=2)
        w_n = big[:, 10 * D:12 * D].rearrange("p (m c) -> p m c", m=2)
        a2_n = big[:, 12 * D:14 * D].rearrange("p (m c) -> p m c", m=2)
        wT = big[:, 14 * D:16 * D].rearrange("p (k c) -> p k c", k=2)
        a12 = big[:, 16 * D:18 * D].rearrange("p (k c) -> p k c", k=2)
        alog = big[:, 18 * D:18 * D + 32].rearrange("p (k n) -> p k n", k=2)
        aexp = big[:, 18 * D + 32:18 * D + 64].rearrange("p (k n) -> p k n", k=2)
        aT16 = big[0:N_STATES, 19 * D:20 * D]
        nsel = big[0:N_STATES, 20 * D:20 * D + N_STATES * P].rearrange("p (n m) -> p n m", n=N_STATES)
        br = fsum[:, :, :].rearrange("p a b -> p (a b)")[:, 0:7 * 512].rearrange("p (k c) -> p k c", k=7)

        ROWS = (0, 32, 64)

        def first_tiles(eng, n):
            eng.wait_ge(first_s, n(first_s, 6))
            eng.sem_inc(passed, 1)
            return [eng.value_load(first_c[P - 1:P, q:q + 1], min_val=0, max_val=T - 1) for q in range(NQ)]

        def later_tiles(eng, c0, done, unit):
            for q in range(NQ):
                with eng.If(c0[q] < T - 1):
                    with eng.Fori(c0[q] + 1, T) as c:
                        unit(q, c, eng.snap(done))
                        eng.reg_add(done, done, 1)
            k = eng.snap(done)
            return k

        @block.sync
        def _(sp):
            def col(v):
                return v.rearrange("(m p) -> p m", p=P)

            def row(v):
                return v.rearrange("(a n) -> a n", a=1)

            sp.wait_ge(const, 7)
            loads = [
                (wqkv_n, w["L0_attn_Wqkv"].rearrange("(m p) c -> p m c", p=P)),
                (wo_n, w["L0_attn_Wout"].rearrange("(m p) c -> p m c", p=P)),
                (a1_n, w["L0_ffn_aux_weight1"].rearrange("(m p) c -> p m c", p=P)),
                (w_n, w["L0_ffn_weight"].rearrange("(m p) c -> p m c", p=P)),
                (a2_n, w["L0_ffn_aux_weight2"].rearrange("(m p) c -> p m c", p=P)),
                (alog, w["L1_attn_A_log"].rearrange("(m p) n -> p m n", p=P)),
                (wx[:, :, :], w["L1_attn_W_x"].rearrange("(k p) n -> p k n", p=P)),
                (wdt[:, :], w["L1_attn_W_dt"]),
                (wo1[:, :, :], w["L1_attn_W_out"].rearrange("(k p) n -> p k n", p=P)),
                (wenc[:, :, :], w["L1_ffn_enc_w"].rearrange("(k p) n -> p k n", p=P)),
                (ws2c[:, :, 0, :], w["L1_ffn_s2c_w"].rearrange("(k p) n -> p k n", p=P)),
                (ws2c[:, :, 1, :], w["L1_ffn_s2c_w"].rearrange("(k p) n -> p k n", p=P)),
                (wr1[0:MD, :], w["L1_ffn_r_w1"]),
                (wr2[0:MD, :], w["L1_ffn_r_w2"]),
                (wr2[MD:MD + 1, :], row(w["L1_ffn_r_b2"])),
                (we1[0:MD, :, :], w["L1_ffn_e_w1"].rearrange("e d h -> d e h")),
                (wc2s[0:MD, :], w["L1_ffn_c2s_w"]),
                (wdec[:, :, :], w["L1_ffn_dec_w"].rearrange("(k p) n -> p k n", p=P)),
                (d_all[:, :], w["L1_attn_D"].partition_broadcast(P)),
                (lng_all[:, :], w["L1_ffn_ln_g"].partition_broadcast(P)),
                (bqk[:, 0, :], col(w["L0_attn_bqkv"][0:D])),
                (bqk[:, 1, :], col(w["L0_attn_bqkv"][D:2 * D])),
                (benc[:, :], col(w["L1_ffn_enc_b"])),
                (bs2c[0:MD, :], w["L1_ffn_s2c_b"].rearrange("(p a) -> p a", a=1)),
                (bs2c[MD:P, :], w["L1_ffn_s2c_b"].rearrange("(p a) -> p a", a=1)),
                (br1[:, :], w["L1_ffn_r_b1"].rearrange("(p a) -> p a", a=1)),
                (bc2s[:, :], col(w["L1_ffn_c2s_b"])),
            ]
            for k in range(EK):
                loads.append((we2[:, :, k, :], w["L1_ffn_e_w2"][:, k * P:(k + 1) * P, :].rearrange("e p d -> p e d")))
                loads.append((be1[:, :, k], w["L1_ffn_e_b1"][:, k * P:(k + 1) * P].rearrange("e p -> p e")))
            for r in ROWS:
                for k, v in ((BV, w["L0_attn_bqkv"][2 * D:3 * D]), (BFFN, w["L0_ffn_bias"]), (BDT, w["L1_attn_b_dt"]),
                             (BOUT, w["L0_attn_bout"]), (BOUT1, w["L1_attn_b_out"]), (BDEC, w["L1_ffn_dec_b"])):
                    for i in range(2):
                        loads.append((br[r:r + 1, k, i * D:(i + 1) * D], row(v)))
                loads.append((br[r:r + 1, BE2, :], w["L1_ffn_e_b2"].rearrange("(a e) d -> a (e d)", a=1)))
                for i in range(2):
                    loads.append((ob[r:r + 1, i, :], row(w["L1_ffn_ln_b"])))
            with nc.allow_non_contiguous_dma("small vectors, once"):
                for dst, src in loads:
                    sp.dma_start(dst, src).then_inc(w_in, 16)
            assert len(loads) == W_LOADS
            sp.sem_inc(stored, 16)
            sp.dma_start(xb[:, :, :], x_v[0]).then_inc(x_in_s, 16)
            with sp.Fori(0, B - 1) as it:
                def n(s, k):
                    return it * PER[id(s)] + k

                after_it = sp.snap(it + 1)
                nxt = x_v[bass.ds(after_it, 1)].rearrange("o p t d -> p (o t) d")
                dst = o_v[bass.ds(it, 1)].rearrange("o p t d -> p (o t) d")
                sp.wait_ge(xth, n(xth, 1))
                sp.sem_inc(passed, 1)
                sp.dma_start(xb[:, :, :], nxt).then_inc(x_in_s, 16)
                sp.wait_ge(out_s, n(out_s, T))
                sp.sem_inc(passed, 1)
                sp.dma_start(dst, ob[:, :, :]).then_inc(stored, 16)
            sp.wait_ge(out_s, B * T)
            sp.dma_start(o_v[B - 1], ob[:, :, :]).then_inc(stored, 16)
            sp.wait_ge(stored, 16 * (B + 1))

        @block.gpsimd
        def _(pool):
            def keep(t, pattern, base, mult, fill, last=const):
                pool.affine_select(out=t, in_=t, compare_op=ALU.is_ge, fill=fill, base=base,
                                   pattern=pattern, channel_multiplier=mult).then_inc(cdone, 1)

            for t in (wr1[:, :], we1[:, :, :], wc2s[:, :], br, kT[:, :, :], vh[:, :, :, :], ob[:, 0:2, :]):
                pool.memset(t, 0.0).then_inc(const, 1)
            sets = ((ident[:, :], 0.0), (ident16[:, :], 0.0), (ones[:, :], 1.0), (ones16[:, :], 1.0), (upto[:, :], 1.0),
                    (after[:, :], 1.0), (mask[:, :, :], 0.0), (mask0[:, :, :], 0.0), (headsel[:, :], 1.0),
                    (lower[:, :, :], 1.0), (eps1[:, :], LN_EPS), (eps4[:, :], 4 * LN_EPS), (mhalf[:, :], -0.5),
                    (biasrow[:, :, :], 0.0), (pr[0][:, :, 0:WINDOW], 0.0), (pr[1][:, :, 0:WINDOW], 0.0),
                    (moeT[:, :], 0.0), (nsel, 1.0), (rhT[:, :], 1.0))
            for t, v in sets:
                pool.memset(t, v).then_inc(cdone, 1)
            pool.wait_ge(cdone, len(sets))
            for m in (ident, ident16):
                pool.affine_select(out=m[:, :], in_=m[:, :], compare_op=ALU.not_equal, fill=1.0, base=0,
                                   pattern=[[-1, P]], channel_multiplier=1).then_inc(cdone, 1)
            keep(upto[:, :], [[1, P]], 0, -1, 0.0)
            keep(after[:, :], [[-1, P]], -1, 1, 0.0)
            keep(lower[:, :, :].rearrange("p (t i) j -> p t i j", t=T), [[0, T], [1, E], [-1, E]], -1, 0, 0.0)
            keep(mask[:, :, :], [[0, 2], [1, KW]], -1, -1, NEG)
            keep(mask0[:, :, :], [[0, 2], [1, KW]], -1, -1, NEG)
            keep(headsel[:, :], [[-DH, HH]], 0, 1, 0.0)
            keep(nsel, [[-1, N_STATES], [0, P]], 0, 1, 0.0)
            c = len(sets) + 9
            pool.wait_ge(cdone, c)
            keep(mask[:, :, :], [[0, 2], [-1, KW]], WINDOW, 1, NEG)
            keep(mask0[:, :, :], [[0, 2], [-1, KW]], WINDOW, 1, NEG)
            keep(headsel[:, :], [[DH, HH]], DH - 1, -1, 0.0)
            keep(nsel, [[1, N_STATES], [0, P]], 0, -1, 0.0)
            pool.wait_ge(cdone, c + 4)
            keep(mask0[:, :, :], [[0, 2], [1, KW]], -WINDOW, 0, NEG)

            pool.wait_ge(w_in, 16 * W_LOADS)
            pool.wait_ge(wt, WT_ALL)
            pool.sem_inc(y_l, 3)
            done = pool.alloc_register("later_pool")
            pool.reg_mov(done, 0)
            with pool.Fori(0, B) as it:
                def n(s, k):
                    return it * PER[id(s)] + k

                def norm(i, eps):
                    pool.wait_ge(aggr[i], n(aggr[i], T))
                    pool.tensor_tensor(rstd[:, :], mv[:, :, 1], eps[:, :], ALU.add).then_inc(var[i], 1)
                    pool.wait_ge(var[i], n(var[i], 1))
                    pool.tensor_tensor(rstd[:, :], rstd[:, :], mhalf[:, :], ALU.pow).then_inc(rstd_s[i], 1)

                norm(0, eps1)
                for hf in range(KC):
                    for a in range(HH // G):
                        pool.wait_ge(q_s, n(q_s, hf + 1))
                        pool.tensor_tensor(qm[:, hf * HH + a * G:hf * HH + (a + 1) * G, :],
                                           qT[:, hf:hf + 1, :].to_broadcast([P, G, L]),
                                           headsel[:, a * G:(a + 1) * G].unsqueeze(2).to_broadcast([P, G, L]),
                                           ALU.mult).then_inc(qm_s, 1)
                for u, (hf, a, t) in enumerate(UNITS):
                    pool.wait_ge(prc_s, n(prc_s, u + 1))
                    p = pr[u % 2][:, :, WINDOW:2 * P]
                    pool.tensor_tensor(p, p, prc[:, u % 2, :].unsqueeze(2).to_broadcast([P, G, KW]),
                                       ALU.mult).then_inc(pn, 1)
                pool.wait_ge(th_s, n(th_s, 1))
                pool.tensor_tensor(x1[:, :, :], xb[:, :, :], th[:, :, :], ALU.add).then_inc(xth, 1)
                norm(1, eps1)
                pool.wait_ge(xn_s[1], n(xn_s[1], T))
                pool.tensor_tensor(ysum[:, :, :], xn2[:, :, :], d_all[:, :].unsqueeze(1).to_broadcast([P, T, D]),
                                   ALU.mult).then_inc(yu, 1)
                pool.wait_ge(delta_s, n(delta_s, 1))
                pool.tensor_tensor(dsum[:, 1, :], delta[:, 2, :], delta[:, 3, :], ALU.add).then_inc(dsum_s, 1)
                pool.wait_ge(dsum_s, n(dsum_s, 1))
                pool.tensor_tensor(dsum[:, 0, :], delta[:, 1, :], dsum[:, 1, :], ALU.add).then_inc(dsum_s, 1)
                pool.tensor_tensor(gg[:, :, :], delta[:, :, :], xn2[:, :, :], ALU.mult).then_inc(g_s, 1)
                c0 = first_tiles(pool, n)
                for q in range(NQ):
                    X = x_t[q % 2]
                    pool.wait_ge(xx, n(xx, q + 1))
                    pool.tensor_tensor(X[:, 0:2, :], X[:, 0:2, :], X[:, 2:4, :], ALU.add).then_inc(ya, 1)
                    pool.wait_ge(ya, n(ya, 3 * q + 1))
                    pool.tensor_tensor(X[:, 0, :], X[:, 0, :], X[:, 1, :], ALU.add).then_inc(ya, 1)
                    pool.wait_ge(ya, n(ya, 3 * q + 2))
                    pool.sem_inc(passed, 1)
                    y = ysum[:, bass.ds(c0[q], 1), :]
                    pool.tensor_tensor(y, y, X[:, 0:1, :], ALU.add).then_inc(ya, 1)

                def later(q, c, k):
                    X = x_later
                    pool.wait_ge(ps_l, k + 1)
                    pool.tensor_tensor(fsum[:, q, :].rearrange("p (a d) -> p a d", a=Q),
                                       fsum[:, q, :].rearrange("p (a d) -> p a d", a=Q), f_later, ALU.add).then_inc(fs_l, 1)
                    pool.wait_ge(x_l, k + 1)
                    pool.tensor_tensor(X[:, 0:2, :], X[:, 0:2, :], X[:, 2:4, :], ALU.add).then_inc(y_l, 1)
                    pool.wait_ge(y_l, k * 3 + 4)
                    pool.tensor_tensor(X[:, 0, :], X[:, 0, :], X[:, 1, :], ALU.add).then_inc(y_l, 1)
                    pool.wait_ge(y_l, k * 3 + 5)
                    pool.sem_inc(passed, 1)
                    y = ysum[:, bass.ds(c, 1), :]
                    pool.tensor_tensor(y, y, X[:, 0:1, :], ALU.add).then_inc(y_l, 1)

                later_tiles(pool, c0, done, later)
                norm(2, eps4)

        @block.scalar
        def _(act):
            act.wait_ge(w_in, 16 * W_LOADS)
            act.activation(aexp, alog, ACT.Exp).then_inc(wt, 1)
            act.mul(benc[:, :], benc[:, :], 0.5).then_inc(wt, 1)
            act.mul(bc2s[:, :], bc2s[:, :], 0.5).then_inc(wt, 1)
            act.mul(bqk[:, 0, :], bqk[:, 0, :], DH ** -0.5).then_inc(wt, 1)
            act.wait_ge(wt, WT_ALL)
            done = act.alloc_register("later_act")
            act.reg_mov(done, 0)
            with act.Fori(0, B) as it:
                def n(s, k):
                    return it * PER[id(s)] + k

                act.wait_ge(xnT_ps[0], n(xnT_ps[0], 1))
                act.activation(xnT[:, :, :].rearrange("p k l -> p (k l)"), ps[0][:, :], ACT.Copy).then_inc(xnT_s[0], 1)
                for hf in range(KC):
                    act.wait_ge(q_ps, n(q_ps, 1))
                    act.activation(qT[:, hf, :], ps[1][:, hf * L:(hf + 1) * L], ACT.Identity, bias=bqk[:, 0, hf:hf + 1],
                                   scale=DH ** -0.5).then_inc(q_s, 1)
                for hf in range(KC):
                    act.wait_ge(k_ps, n(k_ps, 1))
                    act.activation(kT[:, hf, WINDOW:WINDOW + L], ps[2][:, hf * L:(hf + 1) * L], ACT.Identity,
                                   bias=bqk[:, 1, hf:hf + 1]).then_inc(k_s, 1)
                act.wait_ge(h_ps, n(h_ps, 1))
                act.activation(th[:, :, :].rearrange("p t d -> p (t d)"), ps[1][:, :], ACT.Tanh).then_inc(th_s, 1)
                for u, (hf, a, t) in enumerate(UNITS):
                    act.wait_ge(nmax_s, n(nmax_s, u + 1))
                    if u >= 2:
                        act.wait_ge(pT_ps, n(pT_ps, u - 1))
                    for i in range(G):
                        src = ps[s_slot[u]][:, 512 * (i // 2) + KW * (i % 2):512 * (i // 2) + KW * (i % 2) + KW]
                        act.activation(pr[u % 2][:, i, WINDOW:2 * P], src, ACT.Exp, bias=nmax[:, u % 2, i:i + 1],
                                       accum_out=psm[:, u % 2, i:i + 1]).then_inc(pexp, 1)
                act.wait_ge(pv, n(pv, NU))
                act.activation(aT[:, :, :].rearrange("p k l -> p (k l)"), ps[3][:, :], ACT.Copy).then_inc(aT_s, 1)

                act.wait_ge(xnT_ps[1], n(xnT_ps[1], 1))
                act.activation(xn2T[:, :, :].rearrange("p k l -> p (k l)"), ps[0][:, :], ACT.Copy).then_inc(xnT_s[1], 1)
                act.wait_ge(xd_ps, n(xd_ps, 1))
                act.activation(xdT[:, :], ps[1][0:XD, 0:L], ACT.Copy).then_inc(xd_s, 1)
                act.wait_ge(bc_ps, n(bc_ps, 1))
                act.activation(bc[:, :, :].rearrange("p t n -> p (t n)"), ps[1][:, 0:T * 2 * N_STATES], ACT.Copy).then_inc(bc_s, 1)
                act.wait_ge(z_s, n(z_s, 1))
                act.activation(az[:, :, :], z[:, :, :], ACT.Abs).then_inc(az_s, 1)
                act.wait_ge(az_s, n(az_s, 1))
                act.activation(az[:, :, :], az[:, :, :], ACT.Exp, scale=-1.0).then_inc(ez_s, 1)
                act.wait_ge(ez_s, n(ez_s, 1))
                act.activation(az[:, :, :], az[:, :, :], ACT.Ln, bias=1.0).then_inc(lz_s, 1)
                act.wait_ge(tail_ps, n(tail_ps, 1))
                act.wait_ge(stored, n(stored, 16))
                act.activation(tail[:, :, :].rearrange("p t d -> p (t d)"), ps[0][:, :], ACT.Copy).then_inc(tail_s, 1)
                c0 = first_tiles(act, n)
                for q in range(NQ):
                    act.wait_ge(et, n(et, q + 1))
                    act.activation(e_t[q], e_t[q], ACT.Exp, scale=-1.0).then_inc(ee1, 1)
                for q in range(NQ):
                    act.wait_ge(ee1, n(ee1, q + 1))
                    act.activation(ee_t[q], e_t[q], ACT.Ln, bias=SCAN_EPS).then_inc(ee2, 1)
                for q in range(NQ):
                    act.wait_ge(ee2, n(ee2, q + 1))
                    act.activation(ee_t[q], ee_t[q], ACT.Exp, scale=-1.0).then_inc(rc_s, 1)

                def later(q, c, k):
                    act.wait_ge(et_l, k + 1)
                    act.activation(e_t[q], e_t[q], ACT.Exp, scale=-1.0).then_inc(e_l, 1)
                    act.wait_ge(e_l, k + 1)
                    act.activation(ee_t[q], e_t[q], ACT.Ln, bias=SCAN_EPS).then_inc(ln_l, 1)
                    act.wait_ge(ln_l, k + 1)
                    act.activation(ee_t[q], ee_t[q], ACT.Exp, scale=-1.0).then_inc(rc_l, 1)

                later_tiles(act, c0, done, later)
                act.wait_ge(yT_ps, n(yT_ps, 1))
                act.activation(yT[:, :, :].rearrange("p k l -> p (k l)"), ps[0][:, :], ACT.Copy).then_inc(yT_s, 1)

                for m in range(MH):
                    act.wait_ge(enc_ps, n(enc_ps, m // 2 + 1))
                    act.activation(hidT[:, m, :], ps[1 + m // 2][:, 512 * (m % 2):512 * (m % 2) + L], ACT.Tanh,
                                   bias=benc[:, m:m + 1], scale=0.5).then_inc(ts, 1)
                act.wait_ge(cont_ps, n(cont_ps, 1))
                act.activation(contT[:, :], ps[0][:, 0:L], ACT.Identity, bias=bs2c[:, :], scale=0.5).then_inc(cont_s, 1)
                act.wait_ge(rh_ps, n(rh_ps, 1))
                act.activation(rhT[0:MD, :], ps[0][0:MD, 512:512 + L], ACT.Relu, bias=br1[:, :]).then_inc(rh_s, 1)
                act.wait_ge(route, n(route, 2))
                act.activation(rt[:, 1, :], rt[:, 0, :], ACT.Exp).then_inc(rexp, 1)
                for e in range(E):
                    act.wait_ge(e1_ps, n(e1_ps, e + 1))
                    if e >= 2:
                        act.wait_ge(e2_ps, n(e2_ps, e - 1))
                    act.activation(eh[e % 2][:, 0, :], ps[e % 2][:, 0:L], ACT.Relu, bias=be1[:, e, 0:1]).then_inc(eha, 1)
                act.wait_ge(mT_ps, n(mT_ps, 1))
                act.activation(moeT[0:MD, :], ps[0][0:MD, 0:L], ACT.Copy).then_inc(mT_s, 1)
                for m in range(MH):
                    act.wait_ge(c2s_ps, n(c2s_ps, m // 2 + 1))
                    act.activation(hidT[:, m, :], ps[1 + m // 2][:, 512 * (m % 2):512 * (m % 2) + L], ACT.Tanh,
                                   bias=bc2s[:, m:m + 1], scale=0.5).then_inc(tr, 1)
                act.wait_ge(dec_ps, n(dec_ps, 1))
                act.activation(td[:, :, :].rearrange("p t d -> p (t d)"), ps[0][:, :], ACT.Tanh, scale=0.25).then_inc(td_s, 1)

        @block.vector
        def _(dve):
            dve.wait_ge(w_in, 16 * W_LOADS)
            dve.wait_ge(cdone, C_ALL)
            k = 4
            dve.wait_ge(wt, k)

            def prep(i, out_ap, in_ap):
                dve.wait_ge(wt_ps, i + 1)
                dve.tensor_copy(out_ap, in_ap).then_inc(wt, 1)

            prep(0, wqkvT[:, 0, :], ps[0][:, 0:768])
            prep(1, wqkvT[:, 1, :], ps[1][:, 0:768])
            prep(2, woaT[:, :, :, :].rearrange("p a k c -> p (a k c)"), ps[2][:, :])
            prep(3, wT.rearrange("p k c -> p (k c)"), ps[3][:, 0:512])
            prep(4, a12.rearrange("p k c -> p (k c)"), ps[0][:, 0:512])
            prep(5, wfused[:, :, :].rearrange("p k c -> p (k c)"), ps[1][:, 0:512])
            prep(6, aT16, ps[2][0:N_STATES, 0:D])
            for j in range(4):
                prep(7 + j, decay[:, 4 * j:4 * j + 4, :].rearrange("p n d -> p (n d)"), ps[3 if j % 2 else 0][:, :])
            dve.wait_ge(wt, 4 + 11)
            dve.tensor_reduce(least_a[:, :], decay[:, :, :].rearrange("p (q i) d -> p q (i d)", q=NQ), AX.X,
                              ALU.min).then_inc(wt, 1)
            dve.wait_ge(wt_ps, 12)
            dve.scalar_tensor_tensor(out=bs2c[:, :], in0=ps[1][:, 512:513], scalar=0.5, in1=bs2c[:, :],
                                     op0=ALU.mult, op1=ALU.add).then_inc(wt, 1)
            for i in range(2):
                dve.scalar_tensor_tensor(out=br[:, BDEC, i * D:(i + 1) * D], in0=br[:, BDEC, i * D:(i + 1) * D], scalar=2.0,
                                         in1=ps[1][:, 0:D], op0=ALU.mult, op1=ALU.add).then_inc(wt, 1)
            dve.tensor_tensor(br[:, BOUT1, :], br[:, BOUT1, :], ob[:, 0:2, :].rearrange("p a d -> p (a d)"),
                              ALU.add).then_inc(wt, 1)
            k = 4 + 11 + 5
            dve.wait_ge(wt, k)
            part = [qT[:, :, :].rearrange("p k l -> p (k l)")[:, 256 * i:256 * (i + 1)].bitcast(BF16) for i in range(2)]
            for kk in range(7):
                for j, r in enumerate(ROWS):
                    dve.tensor_copy(part[0], br[:, kk, :]).then_inc(wt, 1)
                    k += 1
                    dve.wait_ge(wt, k)
                    dve.tensor_copy(biasrow[r:r + 1, kk, :], part[0][r:r + 1, :]).then_inc(wt, 1)
                    dve.tensor_tensor(br[:, kk, :], br[:, kk, :], part[0], ALU.subtract).then_inc(wt, 1)
                    k += 2
                    dve.wait_ge(wt, k)
            assert k == WT_ALL, k

            done = dve.alloc_register("later_dve")
            dve.reg_mov(done, 0)
            with dve.Fori(0, B) as it:
                def n(s, k):
                    return it * PER[id(s)] + k

                def norm(i, src, ready, need):
                    for t in range(T):
                        dve.wait_ge(ready, need(t))
                        dve.bn_stats(stat[:, t, :], src[:, t, :]).then_inc(stats[i], 1)
                    for t in range(T):
                        dve.wait_ge(stats[i], n(stats[i], t + 1))
                        dve.sem_inc(passed, 1)
                        dve.bn_aggr(mv[:, t, :], stat[:, t, :]).then_inc(aggr[i], 1)

                norm(0, xb, x_in_s, lambda t: n(x_in_s, 16))
                dve.wait_ge(rstd_s[0], n(rstd_s[0], 1))
                for t in range(T):
                    dve.tensor_scalar(xn[:, t, :], xb[:, t, :], mv[:, t, 0:1], rstd[:, t:t + 1], ALU.subtract,
                                      ALU.mult).then_inc(xn_s[0], 1)
                dve.wait_ge(v_ps, n(v_ps, 1))
                for par in range(2):
                    vsrc = ps[0][:, :].rearrange("p (t g b d) -> p t g b d", t=T, g=H // 2, b=2)[:, :, :, par, :]
                    vdst = vh[:, :, :, :].rearrange("p t (g b) (c d) -> p t g b c d", b=2, c=2)[:, :, :, par, par, :]
                    dve.tensor_copy(vdst, vsrc).then_inc(v_s, 1)

                def row_max(u):
                    dve.wait_ge(s_ps, n(s_ps, u + 1))
                    src = ps[s_slot[u]][:, :].rearrange("p (b x) -> p b x", b=2)[:, :, 0:2 * KW]
                    dve.tensor_reduce(nmax[:, u % 2, :], src.rearrange("p b (i k) -> p b i k", i=2), AX.X, ALU.max,
                                      negate=True).then_inc(nmax_s, 1)

                row_max(0)
                row_max(1)
                for u, (hf, a, t) in enumerate(UNITS):
                    dve.wait_ge(pexp, n(pexp, G * (u + 1)))
                    dve.reciprocal(prc[:, u % 2, :], psm[:, u % 2, :]).then_inc(prc_s, 1)
                    dve.wait_ge(pT_ps, n(pT_ps, u + 1))
                    src = ps[s_slot[u]][:, :].rearrange("p (i w l) -> p i w l", i=G, w=2)
                    if u >= 2:
                        dve.wait_ge(pv, n(pv, u - 1))
                    w0 = 1 if t == 0 else 0
                    dve.tensor_copy(prT[u % 2][:, :, w0:2, :], src[:, :, w0:2, :]).then_inc(pT_s, 1)
                    if u + 2 < NU:
                        row_max(u + 2)
                dve.wait_ge(y0_ps, n(y0_ps, 1))
                dve.wait_ge(xth, n(xth, 1))
                dve.tensor_tensor(x1[:, :, :], x1[:, :, :], ps[0][:, :].rearrange("p (t d) -> p t d", t=T),
                                  ALU.add).then_inc(x1_s, 1)
                norm(1, x1, x1_s, lambda t: n(x1_s, 1))
                dve.wait_ge(rstd_s[1], n(rstd_s[1], 1))
                for t in range(T):
                    dve.tensor_scalar(xn2[:, t, :], x1[:, t, :], mv[:, t, 0:1], rstd[:, t:t + 1], ALU.subtract,
                                      ALU.mult).then_inc(xn_s[1], 1)
                dve.wait_ge(dt_ps, n(dt_ps, 1))
                dve.tensor_copy(z[:, :, :].rearrange("p t d -> p (t d)"), ps[2][:, :]).then_inc(z_s, 1)
                dve.wait_ge(lz_s, n(lz_s, 1))
                dve.scalar_tensor_tensor(out=delta[:, :, :], in0=z[:, :, :], scalar=0.0, in1=az[:, :, :], op0=ALU.max,
                                         op1=ALU.add).then_inc(delta_s, 1)

                rows = slice(P - 32, P)
                dve.wait_ge(tail_s, n(tail_s, 1))
                dve.tensor_reduce(least_t[rows, :], tail[rows, 0:T - 1, :], AX.X, ALU.min).then_inc(first_s, 1)
                for c in range(1, T - 1):
                    dve.wait_ge(first_s, n(first_s, c))
                    dve.tensor_tensor(least_t[rows, c:c + 1], least_t[rows, c:c + 1], least_t[rows, c - 1:c],
                                      ALU.min).then_inc(first_s, 1)
                dve.wait_ge(first_s, n(first_s, T - 1))
                dve.tensor_tensor(past[rows, :, :], least_t[rows, :].unsqueeze(1).to_broadcast([32, NQ, T - 1]),
                                  least_a[rows, :].unsqueeze(2).to_broadcast([32, NQ, T - 1]), ALU.mult).then_inc(first_s, 1)
                dve.wait_ge(first_s, n(first_s, T))
                dve.tensor_scalar(past[rows, :, :], past[rows, :, :], ZERO_FROM, None, ALU.is_gt).then_inc(first_s, 1)
                dve.wait_ge(first_s, n(first_s, T + 1))
                with nc.allow_low_precision("counts of at most three"):
                    dve.tensor_reduce(first_c[rows, :], past[rows, :, :], AX.X, ALU.add).then_inc(first_s, 1)
                c0 = first_tiles(dve, n)

                def exponents(q, c):
                    return dve.tensor_tensor(e_t[q], tail[:, bass.ds(c, 1), :].to_broadcast([P, Q, D]),
                                             decay[:, q * Q:(q + 1) * Q, :], ALU.mult)

                def inputs(q, c, dst):
                    for i in range(Q):
                        s = q * Q + i
                        last = dve.scalar_tensor_tensor(out=dst[:, i, :], in0=e_t[q][:, i, :],
                                                        scalar=bc[:, bass.ds(c, 1), s:s + 1].rearrange("p a n -> p (a n)"),
                                                        in1=gg[:, bass.ds(c, 1), :].rearrange("p a d -> p (a d)"),
                                                        op0=ALU.mult, op1=ALU.mult)
                    return last

                def outputs(q, c, slot, dst):
                    for i in range(Q):
                        s = N_STATES + q * Q + i
                        last = dve.scalar_tensor_tensor(out=dst[:, i, :], in0=ps[slot][:, i * D:(i + 1) * D],
                                                        scalar=bc[:, bass.ds(c, 1), s:s + 1].rearrange("p a n -> p (a n)"),
                                                        in1=ee_t[q][:, i, :], op0=ALU.mult, op1=ALU.mult)
                    return last

                dve.wait_ge(g_s, n(g_s, 1))
                dve.wait_ge(bc_s, n(bc_s, 1))
                for q in range(NQ):
                    exponents(q, c0[q]).then_inc(et, 1)
                f_q = [fsum[:, q, :].rearrange("p (i d) -> p i d", i=Q) for q in range(NQ)]

                def scan_out(q):
                    dve.wait_ge(rc_s, n(rc_s, q + 1))
                    dve.wait_ge(sc_ps, n(sc_ps, q + 1))
                    if q >= 2:
                        dve.wait_ge(ya, n(ya, 3 * (q - 1)))
                    outputs(q, c0[q], 1 + q % 2, x_t[q % 2]).then_inc(xx, 1)

                for q in range(NQ):
                    dve.wait_ge(ee1, n(ee1, q + 1))
                    inputs(q, c0[q], f_q[q]).then_inc(f_s, 1)
                for q in range(NQ):
                    scan_out(q)

                def later(q, c, k):
                    dve.wait_ge(y_l, k * 3 + 3)
                    exponents(q, c).then_inc(et_l, 1)
                    dve.wait_ge(e_l, k + 1)
                    inputs(q, c, f_later).then_inc(f_l, 1)
                    dve.wait_ge(rc_l, k + 1)
                    dve.wait_ge(ps_l, k + 1)
                    outputs(q, c, 1, x_later).then_inc(x_l, 1)

                later_tiles(dve, c0, done, later)
                dve.wait_ge(y1_ps, n(y1_ps, 1))
                dve.tensor_tensor(x1[:, :, :], x1[:, :, :], ps[3][:, :].rearrange("p (t d) -> p t d", t=T),
                                  ALU.add).then_inc(x2_s, 1)

                def step(k):
                    dve.wait_ge(route, n(route, k))

                lg = ps[0][:, 0:T * E].rearrange("p (t e) -> p t e", t=T)
                r3 = [rt[:, j, :].rearrange("p (t e) -> p t e", t=T) for j in range(8)]
                pr3 = [pair[:, j, :].rearrange("p (i e) -> p i e", e=E) for j in range(2)]
                dve.wait_ge(lg_ps, n(lg_ps, 1))
                dve.tensor_reduce(rs[:, 0, :], lg, AX.X, ALU.max).then_inc(route, 1)
                step(1)
                dve.tensor_tensor(r3[0], lg, rs[:, 0, :].unsqueeze(2).to_broadcast([P, T, E]), ALU.subtract).then_inc(route, 1)
                step(2)
                lj = r3[0].unsqueeze(2).to_broadcast([P, T, E, E])
                li = r3[0].unsqueeze(3).to_broadcast([P, T, E, E])
                p4 = [pair[:, j, :].rearrange("p (t i e) -> p t i e", t=T, e=E) for j in range(2)]
                dve.tensor_tensor(p4[0], lj, li, ALU.is_gt).then_inc(route, 1)
                dve.tensor_tensor(p4[1], lj, li, ALU.is_equal).then_inc(route, 1)
                step(4)
                dve.tensor_tensor(pr3[1], pr3[1], lower[:, :, :], ALU.mult).then_inc(route, 1)
                step(5)
                dve.tensor_tensor(pr3[0], pr3[0], pr3[1], ALU.add).then_inc(route, 1)
                step(6)
                dve.tensor_reduce(rt[:, 2, :], pr3[0], AX.X, ALU.add).then_inc(route, 1)
                step(7)
                dve.wait_ge(rexp, n(rexp, 1))
                dve.scalar_tensor_tensor(out=rt[:, 3, :], in0=rt[:, 2, :], scalar=2.0, in1=rt[:, 1, :], op0=ALU.is_lt,
                                         op1=ALU.mult).then_inc(route, 1)
                step(8)
                dve.tensor_reduce(rs[:, 1, :], r3[3], AX.X, ALU.add).then_inc(route, 1)
                step(9)
                dve.reciprocal(rs[:, 2, :], rs[:, 1, :]).then_inc(route, 1)
                step(10)
                dve.tensor_tensor(r3[4], r3[3], rs[:, 2, :].unsqueeze(2).to_broadcast([P, T, E]), ALU.mult).then_inc(route, 1)
                for e in range(E):
                    dve.wait_ge(e1_ps, n(e1_ps, e + 1))
                    if e >= 2:
                        dve.wait_ge(e2_ps, n(e2_ps, e - 1))
                    dve.tensor_scalar(eh[e % 2][:, 1, :], ps[e % 2][:, 512:512 + L], be1[:, e, 1:2], 0.0, ALU.add,
                                      ALU.max).then_inc(ehv, 1)
                dve.wait_ge(e2_ps, n(e2_ps, E))
                dve.wait_ge(route, n(route, 11))
                for t in range(T):
                    if t >= 2:
                        dve.wait_ge(moe_s, n(moe_s, t - 1))
                    dve.tensor_tensor(m1[:, t % 2, :].rearrange("p (e d) -> p e d", e=E),
                                      ps[2 + t // 2][:, 512 * (t % 2):512 * (t % 2) + 512].rearrange("p (e d) -> p e d", e=E),
                                      r3[4][:, t, :].unsqueeze(2).to_broadcast([P, E, MD]), ALU.mult).then_inc(m1_s, 1)
                    dve.wait_ge(m1_s, n(m1_s, t + 1))
                    dve.tensor_reduce(moe[:, t, :], m1[:, t % 2, :].rearrange("p (e d) -> p d e", e=E), AX.X,
                                      ALU.add).then_inc(moe_s, 1)
                norm(2, td, td_s, lambda t: n(td_s, 1))
                dve.wait_ge(rstd_s[2], n(rstd_s[2], 1))
                for t in range(T):
                    dve.scalar_tensor_tensor(out=td[:, t, :], in0=td[:, t, :], scalar=mv[:, t, 0:1], in1=lng_all[:, :],
                                             op0=ALU.subtract, op1=ALU.mult).then_inc(n3, 1)
                for t in range(T):
                    dve.wait_ge(n3, n(n3, t + 1))
                    dve.scalar_tensor_tensor(out=ob[:, t, :], in0=td[:, t, :], scalar=rstd[:, t:t + 1], in1=x1[:, t, :],
                                             op0=ALU.mult, op1=ALU.add).then_inc(out_s, 1)

        @block.tensor
        def _(pe):
            pe.wait_ge(w_in, 16 * W_LOADS)
            pe.wait_ge(cdone, C_ALL)
            for k in range(KC):
                for m in range(6):
                    mm = pe.transpose(ps[k][:, m * P:(m + 1) * P], wqkv_n[:, m, k * P:(k + 1) * P], ident[:, :])
                mm.then_inc(wt_ps, 1)
            for j, src in enumerate((wo_n, a1_n)):
                for k in range(KC):
                    for m in range(KC):
                        mm = pe.transpose(ps[2][:, 512 * j + k * D + m * P:512 * j + k * D + (m + 1) * P],
                                          src[:, m, k * P:(k + 1) * P], ident[:, :])
            mm.then_inc(wt_ps, 1)
            for k in range(KC):
                for m in range(KC):
                    mm = pe.transpose(ps[3][:, k * D + m * P:k * D + (m + 1) * P], w_n[:, m, k * P:(k + 1) * P], ident[:, :])
            mm.then_inc(wt_ps, 1)
            pe.wait_ge(wt, 4 + 3)
            for m in range(KC):
                for k in range(KC):
                    mm = pe.matmul(ps[0][:, m * D:(m + 1) * D], woaT[:, 1, k, m * P:(m + 1) * P], a2_n[:, k, :],
                                   start=k == 0, stop=k == KC - 1)
            mm.then_inc(wt_ps, 1)
            pe.wait_ge(wt, 4 + 5)
            for m in range(KC):
                for k in range(KC):
                    mm = pe.matmul(ps[1][:, m * D:(m + 1) * D], wT[:, k, m * P:(m + 1) * P], a12[:, k, :],
                                   start=k == 0, stop=k == KC - 1)
            mm.then_inc(wt_ps, 1)
            for k in range(KC):
                mm = pe.transpose(ps[2][0:N_STATES, k * P:(k + 1) * P], aexp[:, k, :], ident[:, :])
            mm.then_inc(wt_ps, 1)
            pe.wait_ge(wt, 4 + 7)
            for j in range(4):
                if j >= 2:
                    pe.wait_ge(wt, 4 + 7 + j - 1)
                for i in range(4):
                    mm = pe.matmul(ps[3 if j % 2 else 0][:, i * D:(i + 1) * D], nsel[:, 4 * j + i, :], aT16,
                                   start=True, stop=True)
                mm.then_inc(wt_ps, 1)
            for k in range(MH):
                pe.matmul(ps[1][:, 0:D], ones[:, :], wdec[:, k, :], start=k == 0, stop=k == MH - 1)
            for k in range(MH):
                mm = pe.matmul(ps[1][:, 512:513], ws2c[:, k, :, :].rearrange("p a d -> p (a d)"), ones[:, 0:1],
                               start=k == 0, stop=k == MH - 1)
            mm.then_inc(wt_ps, 1)
            pe.wait_ge(wt, WT_ALL)

            def bias(out_ap, k):
                pe.matmul(out_ap, ones16[:, :], biasrow[:, k, :], start=True, stop=False)

            def tiles(slot, lhsT, rhs, k_n, k):
                for t in range(T):
                    if t % 2 == 0:
                        bias(ps[slot][:, t * D:(t + 2) * D], k)
                    for c in range(k_n):
                        mm = pe.matmul(ps[slot][:, t * D:(t + 1) * D], lhsT[:, c, t * P:(t + 1) * P], rhs[:, c, :],
                                       start=False, stop=c == k_n - 1 and t % 2 == 1)
                return mm

            done = pe.alloc_register("later_pe")
            pe.reg_mov(done, 0)
            with pe.Fori(0, B) as it:
                def n(s, k):
                    return it * PER[id(s)] + k

                def turned(i, src):
                    for t in range(T):
                        pe.wait_ge(xn_s[i], n(xn_s[i], t + 1))
                        for c in range(KC):
                            mm = pe.transpose(ps[0][:, c * L + t * P:c * L + (t + 1) * P], src[:, t, c * P:(c + 1) * P],
                                              ident[:, :])
                    mm.then_inc(xnT_ps[i], 1)
                    pe.wait_ge(xnT_s[i], n(xnT_s[i], 1))

                turned(0, xn)
                for slot, c0, sig in ((1, 0, q_ps), (2, D, k_ps)):
                    for hf in range(KC):
                        for c in range(KC):
                            mm = pe.matmul(ps[slot][:, hf * L:(hf + 1) * L], wqkvT[:, c, c0 + hf * P:c0 + (hf + 1) * P],
                                           xnT[:, c, :], start=c == 0, stop=c == KC - 1)
                    mm.then_inc(sig, 1)
                tiles(0, xnT, wqkvT[:, :, 2 * D:3 * D], KC, BV).then_inc(v_ps, 1)
                pe.wait_ge(q_s, n(q_s, KC))
                tiles(1, xnT, wfused, KC, BFFN).then_inc(h_ps, 1)

                def scores(u):
                    hf, a, t = UNITS[u]
                    slot = s_slot[u]
                    pe.wait_ge(qm_s, n(qm_s, hf * 2 + a + 1))
                    if u == 0:
                        pe.wait_ge(k_s, n(k_s, KC))
                    elif u == 1:
                        pe.wait_ge(v_s, n(v_s, 2))
                    elif u == 2:
                        pe.wait_ge(th_s, n(th_s, 1))
                    elif u >= 3:
                        pe.wait_ge(pT_s, n(pT_s, u - 2))
                    for b in range(2):
                        pe.matmul(ps[slot][:, 512 * b:512 * b + 2 * KW], ident16[:, :],
                                  (mask if t else mask0)[:, :, :].rearrange("p a k -> p (a k)"), start=True, stop=False)
                    for i in range(G):
                        off = 512 * (i // 2) + KW * (i % 2)
                        mm = pe.matmul(ps[slot][:, off:off + KW], qm[:, hf * HH + a * G + i, t * P:(t + 1) * P],
                                       kT[:, hf, t * P:t * P + KW], start=False, stop=i % 2 == 1)
                    mm.then_inc(s_ps, 1)

                scores(0)
                scores(1)
                for u, (hf, a, t) in enumerate(UNITS):
                    pe.wait_ge(pn, n(pn, u + 1))
                    for i in range(G):
                        for v in range(0 if t else 1, 2):
                            mm = pe.transpose(ps[s_slot[u]][:, i * 2 * P + v * P:i * 2 * P + (v + 1) * P],
                                              pr[u % 2][:, i, v * P:(v + 1) * P], ident[:, :])
                    mm.then_inc(pT_ps, 1)
                    if u + 2 < NU:
                        scores(u + 2)
                    pe.wait_ge(pT_s, n(pT_s, u + 1))
                    for j in range(G // 2):
                        blk = a * G // 2 + j
                        todo = [(i, v) for i in range(2) for v in range(0 if t else 1, 2)]
                        for i, v in todo:
                            mm = pe.matmul(ps[3][32 * blk:32 * blk + 32, hf * L + t * P:hf * L + (t + 1) * P],
                                           vh[:, t - 1 + v, hf * HH + a * G + 2 * j + i, :], prT[u % 2][:, 2 * j + i, v, :],
                                           start=(i, v) == todo[0], stop=(i, v) == todo[-1])
                    mm.then_inc(pv, 1)
                pe.wait_ge(aT_s, n(aT_s, 1))
                tiles(0, aT, woaT[:, 0, :, :], KC, BOUT).then_inc(y0_ps, 1)
                pe.wait_ge(x1_s, n(x1_s, 1))

                turned(1, xn2)
                for c in range(KC):
                    mm = pe.matmul(ps[1][0:XD, 0:L], wx[:, c, :], xn2T[:, c, :], start=c == 0, stop=c == KC - 1)
                mm.then_inc(xd_ps, 1)
                pe.wait_ge(xd_s, n(xd_s, 1))
                for t in range(T):
                    if t % 2 == 0:
                        bias(ps[2][:, t * D:(t + 2) * D], BDT)
                    mm = pe.matmul(ps[2][:, t * D:(t + 1) * D], xdT[0:RANK, t * P:(t + 1) * P], wdt[:, :], start=False,
                                   stop=t % 2 == 1)
                mm.then_inc(dt_ps, 1)
                for t in range(T):
                    mm = pe.transpose(ps[1][:, t * 2 * N_STATES:(t + 1) * 2 * N_STATES], xdT[RANK:XD, t * P:(t + 1) * P],
                                      ident[RANK:XD, RANK:XD])
                mm.then_inc(bc_ps, 1)
                pe.wait_ge(dsum_s, n(dsum_s, 2))
                for c in range(T):
                    later = (dsum[:, 0, :], dsum[:, 1, :], delta[:, 3, :], None)[c]
                    mm = pe.matmul(ps[0][:, c * D:(c + 1) * D], after[:, :], delta[:, c, :], start=True, stop=later is None)
                    if later is not None:
                        mm = pe.matmul(ps[0][:, c * D:(c + 1) * D], ones[:, :], later, start=False, stop=True)
                mm.then_inc(tail_ps, 1)
                pe.wait_ge(bc_s, n(bc_s, 1))
                c0 = first_tiles(pe, n)
                for q in range(NQ):
                    pe.wait_ge(f_s, n(f_s, q + 1))
                    if q >= 2:
                        pe.wait_ge(xx, n(xx, q - 1))
                    for b in range(2):
                        mm = pe.matmul(ps[1 + q % 2][:, 512 * b:512 * (b + 1)], upto[:, :],
                                       fsum[:, q, 512 * b:512 * (b + 1)], start=True, stop=True)
                    mm.then_inc(sc_ps, 1)
                pe.wait_ge(xx, n(xx, NQ))
                pe.sem_inc(passed, 1)

                def later(q, c, k):
                    pe.wait_ge(f_l, k + 1)
                    for b in range(2):
                        pe.matmul(ps[1][:, 512 * b:512 * (b + 1)], ones[:, :], fsum[:, q, 512 * b:512 * (b + 1)],
                                  start=True, stop=False)
                        mm = pe.matmul(ps[1][:, 512 * b:512 * (b + 1)], upto[:, :],
                                       f_later.rearrange("p q d -> p (q d)")[:, 512 * b:512 * (b + 1)], start=False, stop=True)
                    mm.then_inc(ps_l, 1)

                k = later_tiles(pe, c0, done, later)
                pe.wait_ge(ya, n(ya, 3 * NQ))
                pe.wait_ge(y_l, k * 3 + 3)
                for t in range(T):
                    for c in range(KC):
                        mm = pe.transpose(ps[0][:, c * L + t * P:c * L + (t + 1) * P], ysum[:, t, c * P:(c + 1) * P],
                                          ident[:, :])
                mm.then_inc(yT_ps, 1)
                pe.wait_ge(yT_s, n(yT_s, 1))
                tiles(3, yT, wo1, KC, BOUT1).then_inc(y1_ps, 1)

                for m in range(MH):
                    for c in range(KC):
                        mm = pe.matmul(ps[1 + m // 2][:, 512 * (m % 2):512 * (m % 2) + L], wenc[:, c, m * P:(m + 1) * P],
                                       xn2T[:, c, :], start=c == 0, stop=c == KC - 1)
                    if m % 2:
                        mm.then_inc(enc_ps, 1)
                for m in range(MH):
                    pe.wait_ge(ts, n(ts, m + 1))
                    mm = pe.matmul(ps[0][:, 0:L], ws2c[:, m, :, :].rearrange("p a d -> p (a d)"), hidT[:, m, :],
                                   start=m == 0, stop=m == MH - 1)
                mm.then_inc(cont_ps, 1)
                pe.wait_ge(cont_s, n(cont_s, 1))
                pe.matmul(ps[0][0:MD, 512:512 + L], wr1[:, :], contT[:, :], start=True, stop=True).then_inc(rh_ps, 1)
                pe.wait_ge(rh_s, n(rh_s, 1))
                for t in range(T):
                    mm = pe.matmul(ps[0][:, t * E:(t + 1) * E], rhT[:, t * P:(t + 1) * P], wr2[:, :], start=True, stop=True)
                mm.then_inc(lg_ps, 1)

                def expert_in(e):
                    if e == 0:
                        pe.wait_ge(route, n(route, 2))
                    if e >= 2:
                        pe.wait_ge(eha, n(eha, e - 1))
                        pe.wait_ge(ehv, n(ehv, e - 1))
                    for k in range(EK):
                        mm = pe.matmul(ps[e % 2][:, 512 * k:512 * k + L], we1[:, e, k * P:(k + 1) * P], contT[:, :],
                                       start=True, stop=True)
                    mm.then_inc(e1_ps, 1)

                expert_in(0)
                pe.wait_ge(x2_s, n(x2_s, 1))
                for t in range(T):
                    bias(ps[2 + t // 2][:, 512 * (t % 2):512 * (t % 2) + 512], BE2)
                for e in range(E):
                    if e + 1 < E:
                        expert_in(e + 1)
                    pe.wait_ge(eha, n(eha, e + 1))
                    pe.wait_ge(ehv, n(ehv, e + 1))
                    for t in range(T):
                        for k in range(EK):
                            off = 512 * (t % 2) + e * MD
                            mm = pe.matmul(ps[2 + t // 2][:, off:off + MD], eh[e % 2][:, k, t * P:(t + 1) * P],
                                           we2[:, e, k, :], start=False, stop=e == E - 1 and k == EK - 1)
                    mm.then_inc(e2_ps, 1)
                for t in range(T):
                    pe.wait_ge(moe_s, n(moe_s, t + 1))
                    pe.sem_inc(passed, 1)
                    mm = pe.transpose(ps[0][0:MD, t * P:(t + 1) * P], moe[:, t, :], ident[:, :])
                mm.then_inc(mT_ps, 1)
                pe.wait_ge(mT_s, n(mT_s, 1))
                for m in range(MH):
                    mm = pe.matmul(ps[1 + m // 2][:, 512 * (m % 2):512 * (m % 2) + L], wc2s[:, m * P:(m + 1) * P],
                                   moeT[:, :], start=True, stop=True)
                    if m % 2:
                        mm.then_inc(c2s_ps, 1)
                pe.wait_ge(tr, n(tr, MH))
                tiles(0, hidT, wdec, MH, BDEC).then_inc(dec_ps, 1)


def kernel(**inputs):
    import numpy as _np
    import concourse.bacc as _bacc
    from concourse import mybir as _mybir
    from concourse.bass_utils import run_bass_kernel_spmd as _run

    nc = _bacc.Bacc("TRN2", target_bir_lowering=False, num_devices=1)
    arrays, args = {}, {}
    for name in inputs:
        a = _np.ascontiguousarray(inputs[name])
        arrays[f"in_{name}_dram"] = a
        args[name] = nc.dram_tensor(f"in_{name}_dram", a.shape, _mybir.dt.from_np(a.dtype), kind="ExternalInput").ap()
    x = args.pop("L0_attn_x")
    out = nc.dram_tensor("out_0_dram", x.shape, _mybir.dt.float32, kind="ExternalOutput").ap()
    layered_kernel(nc, x, args, out)
    r = _run(nc, [arrays], core_ids=[0])
    return r.results[0]["out_0_dram"]
```

```python
from contextlib import ExitStack

import concourse.bass as bass
from concourse import mybir


def layered_kernel(nc, x_in, w, out):
    F32 = mybir.dt.float32
    BF16 = mybir.dt.bfloat16
    ALU = mybir.AluOpType
    ACT = mybir.ActivationFunctionType
    AX = mybir.AxisListType

    B, L, D = x_in.shape
    P = 128
    T = L // P
    KC = D // P
    H, WINDOW = 16, 64
    DH = D // H
    HH = P // DH
    G = 4
    KW = P + WINDOW
    NEG = -1e30
    N_STATES = w["L1_attn_A_log"].shape[1]
    RANK = w["L1_attn_W_dt"].shape[0]
    XD = RANK + 2 * N_STATES
    HID = w["L1_ffn_enc_w"].shape[1]
    MH = HID // P
    E, MD, EH = w["L1_ffn_e_w1"].shape
    EK = EH // P
    Q = 4
    NQ = N_STATES // Q
    LN_EPS = 1e-5
    SCAN_EPS = 1e-12
    UNITS = [(hf, j, t) for hf in range(KC) for j in range(HH // 2) for t in range(T)]
    NU = len(UNITS)
    ZERO_FROM = 110.0

    ctx = ExitStack()
    with ctx:
        def sb(name, shape, dt=F32):
            return ctx.enter_context(nc.sbuf_tensor(name, shape, dt))

        ident = sb("ident", [P, P])
        ident16 = sb("ident16", [P, P], BF16)
        ones = sb("ones", [P, P])
        ones16 = sb("ones16", [P, P], BF16)
        upto = sb("upto", [P, P])
        after = sb("after", [P, P])
        mask = sb("mask", [P, 2, KW], BF16)
        mask0 = sb("mask0", [P, 2, KW], BF16)
        headsel = sb("headsel", [P, HH])
        lower = sb("lower", [P, T * E, E])
        eps1 = sb("eps1", [P, T])
        eps4 = sb("eps4", [P, T])
        mhalf = sb("mhalf", [P, T])
        wqkvT = sb("wqkvT", [P, KC, 3 * D])
        woaT = sb("woaT", [P, 2, KC, D])
        wfused = sb("wfused", [P, KC, D])
        wx = sb("wx", [P, KC, XD])
        wdt = sb("wdt", [RANK, D])
        wo1 = sb("wo1", [P, KC, D])
        wenc = sb("wenc", [P, KC, HID])
        ws2c = sb("ws2c", [P, MH, 2, MD])
        wr1 = sb("wr1", [P, MD])
        wr2 = sb("wr2", [MD + 1, E])
        we1 = sb("we1", [P, E, EH])
        we2 = sb("we2", [P, E, EK, MD])
        wc2s = sb("wc2s", [P, HID])
        wdec = sb("wdec", [P, MH, D])
        decay = sb("decay", [P, N_STATES, D])
        d_all = sb("d_all", [P, D])
        lng_all = sb("lng_all", [P, D])
        bqk = sb("bqk", [P, 2, KC])
        benc = sb("benc", [P, MH])
        bs2c = sb("bs2c", [P, 1])
        br1 = sb("br1", [MD, 1])
        be1 = sb("be1", [P, E, EK])
        bc2s = sb("bc2s", [P, MH])
        BV, BFFN, BDT, BOUT, BOUT1, BDEC, BE2 = range(7)
        biasrow = sb("biasrow", [P, 7, 512], BF16)

        xb = sb("xb", [P, T, D])
        xn = sb("xn", [P, T, D])
        xnT = sb("xnT", [P, KC, L])
        qT = sb("qT", [P, KC, L])
        kT = sb("kT", [P, KC, WINDOW + L])
        vh = sb("vh", [P, T, H, 2 * DH])
        th = sb("th", [P, T, D])
        pr = [sb(f"pr{i}", [P, 2, 2 * P]) for i in range(3)]
        prT = [sb(f"prT{i}", [P, 2, 2, P]) for i in range(2)]
        aT = sb("aT", [P, KC, L])
        x1 = sb("x1", [P, T, D])
        big = sb("big", [P, 8 * 1024])
        qm = [big[:, 2048 * i:2048 * (i + 1)].rearrange("p (h l) -> p h l", h=G) for i in range(2)]
        tmp = [big[:, 1024 * i:1024 * (i + 1)].rearrange("p (q d) -> p q d", q=Q) for i in range(4, 8)]
        e_t, ee_t = tmp[0:2], tmp[2:4]
        f_later = e_t[1]
        stat = [sb(f"stat{i}", [P, T, 6]) for i in range(2)]
        mv = [sb(f"mv{i}", [P, T, 2]) for i in range(2)]
        rstd = [sb(f"rstd{i}", [P, T]) for i in range(2)]
        nmax = sb("nmax", [P, 4, 2])
        psm = sb("psm", [P, 4, 2])
        prc = sb("prc", [P, 4, 2])
        least_a = sb("least_a", [P, NQ])
        least_t = sb("least_t", [P, T - 1])
        past = sb("past", [P, NQ, T - 1])
        first_c = sb("first_c", [P, NQ], mybir.dt.int32)
        xn2 = sb("xn2", [P, T, D])
        xn2T = sb("xn2T", [P, KC, L])
        xdT = sb("xdT", [XD, L])
        bc = sb("bc", [P, T, 2 * N_STATES])
        z = sb("z", [P, T, D])
        az = sb("az", [P, T, D])
        delta, gg = az, z
        dsum = sb("dsum", [P, 2, D])
        tail = sb("tail", [P, T, D])
        fsum = sb("fsum", [P, NQ, Q * D])
        ysum = sb("ysum", [P, T, D])
        late = fsum[:, :, :].rearrange("p a b -> p (a b)")
        hidT = late[:, 0:MH * L].rearrange("p (m l) -> p m l", m=MH)
        eh = [late[:, (MH + EK * i) * L:(MH + EK * (i + 1)) * L].rearrange("p (k l) -> p k l", k=EK) for i in range(2)]
        contT = sb("contT", [P, L])
        rhT = sb("rhT", [MD + 1, L])
        rt = sb("rt", [P, 5, T * E])
        pair = tmp[0][:, 0:2, :].rearrange("p a b -> p (a b)")[:, 0:2 * T * E * E].rearrange("p (a b) -> p a b", a=2)
        rs = sb("rs", [P, 3, T])
        m1 = tmp[2][:, 0:2, :].rearrange("p a (t d) -> p a t d", t=T)
        moe = sb("moe", [P, T, MD])
        moeT = sb("moeT", [P, L])
        ob = tail
        yT = az[:, :, :].rearrange("p t d -> p (t d)").rearrange("p (k l) -> p k l", k=KC)
        td = z

        psall = ctx.enter_context(nc.psum_tensor("psall", [P, 8, 512], F32))
        ps = [psall[:, 2 * i:2 * i + 2, :].rearrange("p a b -> p (a b)") for i in range(4)]
        bank = [psall[:, i, :] for i in range(8)]
        A, O, LB = bank[0:4], bank[4], bank[5:8]
        u_bank = [A[(u + 2) % 4] for u in range(NU)]
        W_LOADS = 76
        C_ALL = 34
        WT_ALL = 83
        PER = {}

        def sem(name, per):
            s = ctx.enter_context(nc.semaphore(name))
            PER[id(s)] = per
            return s

        w_in = sem("w_in", 0)
        cdone = sem("cdone", 0)
        const = sem("const", 0)
        wt_ps = sem("wt_ps", 0)
        wt = sem("wt", 0)
        x_in_s = sem("x_loaded", 16)
        stored = sem("stored", 16)
        passed = sem("passed", 0)
        stats = [sem(f"stats{i}", T) for i in range(3)]
        aggr = [sem(f"aggr{i}", T) for i in range(3)]
        var = [sem(f"var{i}", 1) for i in range(3)]
        rstd_s = [sem(f"rstd{i}", 1) for i in range(3)]
        xn_s = [sem(f"xnorm{i}", T) for i in range(2)]
        xnT_ps = [sem(f"xnT_ps{i}", KC) for i in range(2)]
        xnT_s = [sem(f"xnT{i}", KC) for i in range(2)]
        q_ps = sem("q_ps", KC)
        k_ps = sem("k_ps", KC)
        v_ps = sem("v_ps", 2)
        h_ps = sem("h_ps", 2)
        q_s = sem("q", KC)
        k_s = sem("k", KC)
        v_s = sem("v", 4)
        th_s = sem("th", 2)
        qm_s = sem("qm", 4)
        s_ps = sem("score_ps", NU)
        nmax_s = sem("nmax", NU)
        pexp = sem("pexp", NU)
        prc_s = sem("prc", NU)
        pn = sem("pnorm", NU)
        pT_ps = sem("pT_ps", NU)
        pT_s = sem("pT", NU)
        pv = sem("pv", NU)
        aT_s = sem("aT", KC)
        y0_ps = sem("y0_ps", 2)
        xth = sem("x_plus_tanh", 1)
        x1_s = sem("x1", 2)
        xd_ps = sem("xd_ps", 1)
        xd_s = sem("xd", 1)
        dt_ps = sem("dt_ps", 2)
        bc_ps = sem("bc_ps", 1)
        bc_s = sem("bc", 1)
        z_s = sem("z", 2)
        az_s = sem("az", 1)
        ez_s = sem("ez", 1)
        lz_s = sem("lz", 1)
        delta_s = sem("delta", 1)
        g_s = sem("g", 1)
        dsum_s = sem("dsum", 2)
        yu = sem("yu", 1)
        tail_ps = sem("tail_ps", 2)
        tail_s = sem("tail", 2)
        first_s = sem("first", 6)
        et = sem("et", NQ)
        ee1 = sem("e", NQ)
        ee2 = sem("e_eps", NQ)
        f_s = sem("f", NQ)
        rc_s = sem("rc", NQ)
        sc_ps = sem("scan_ps", NQ * 2)
        xx = sem("xx", NQ * 2)
        ya = sem("yadd", NQ * 3)
        et_l = sem("et_later", 0)
        e_l = sem("e_later", 0)
        ln_l = sem("e_eps_later", 0)
        rc_l = sem("rc_later", 0)
        f_l = sem("f_later", 0)
        ps_l = sem("scan_ps_later", 0)
        x_l = sem("xx_later", 0)
        fs_l = sem("fsum_later", 0)
        y_l = sem("yadd_later", 0)
        yT_ps = sem("yT_ps", KC)
        yT_s = sem("yT", KC)
        y1_ps = sem("y1_ps", 2)
        x2_s = sem("x2", 2)
        enc_ps = sem("enc_ps", MH)
        ts = sem("spikes", MH)
        cont_ps = sem("cont_ps", 1)
        cont_s = sem("cont", 1)
        rh_ps = sem("rh_ps", 1)
        rh_s = sem("rh", 1)
        lg_ps = sem("lg_ps", 1)
        route = sem("route", 11)
        rexp = sem("rexp", 1)
        e1_ps = sem("e1_ps", E * EK)
        eha = sem("eh_a", E)
        ehv = sem("eh_v", E)
        e2_ps = sem("e2_ps", E)
        m1_s = sem("m1", E)
        moe_s = sem("moe", E - 1)
        mT_ps = sem("mT_ps", 1)
        mT_s = sem("mT", 1)
        c2s_ps = sem("c2s_ps", MH)
        tr = sem("rates", MH)
        dec_ps = sem("dec_ps", 2)
        td_s = sem("td", 2)
        n3 = sem("n3", T)
        out_s = sem("out_ready", T)

        experts = [("e1", eha, 1), ("e1", ehv, 1)]
        for e in range(E):
            if e + 1 < E:
                experts += [("e1", eha, e + 2), ("e1", ehv, e + 2)]
            experts.append(("e2", m1_s, e + 1))
        USES = ([("xnT", xnT_s[1], c + 1) for c in range(KC)] + [("xd", xd_s, 1)]
                + [("dt", z_s, 1), ("dt", z_s, 2), ("bc", bc_s, 1)] + [("tail", tail_s, 1), ("tail", tail_s, 2)]
                + [("scan", xx, i + 1) for i in range(2 * NQ)] + [("later", xx, 2 * NQ)] * 2
                + [("yT", yT_s, c + 1) for c in range(KC)] + [("y1", x2_s, 1), ("y1", x2_s, 2)]
                + [("enc", ts, m + 1) for m in range(MH)] + [("cont", cont_s, 1), ("rh", rh_s, 1), ("lg", route, 2)]
                + experts + [("mT", mT_s, 1)] + [("c2s", tr, m + 1) for m in range(MH)]
                + [("dec", td_s, 1), ("dec", td_s, 2)])
        assert len(USES) % 3 == 0

        def lb(name, i):
            u = [k for k, x in enumerate(USES) if x[0] == name][i]
            return LB[u % 3], u

        def eb(e, k):
            return lb("e1", e * EK + k)[0]

        A_STEPS = ["norm", "q", "k", "v", "h"] + list(range(NU)) + ["close"]
        B_STEPS = (["norm", "xT", "xd", "dt", "softplus", "tail", "first", "scan0", "scan1", "scan2", "scan3", "later", "yT", "y1"]
                   + [f"enc{m}" for m in range(MH)] + ["cont", "rh", "lg", "route"] + [f"expert{e}" for e in range(E)]
                   + ["mT"] + [f"c2s{m}" for m in range(MH)] + ["dec0", "dec1", "out"])
        n_a, n_b = len(A_STEPS) - 1, len(B_STEPS)
        SCHEDULE = []
        for i in range(n_a):
            SCHEDULE.append(("a", A_STEPS[i]))
            SCHEDULE += [("b", B_STEPS[k]) for k in range(i * n_b // n_a, (i + 1) * n_b // n_a)]
        SCHEDULE.append(("a", "close"))

        def n0(s, k):
            return k

        def passes(eng, a, b):
            for step in A_STEPS:
                a(step, n0)
            with eng.Fori(0, B - 1) as it:
                for layer, step in SCHEDULE:
                    if layer == "a":
                        a(step, lambda s, k: it * PER[id(s)] + (PER[id(s)] + k))
                    else:
                        b(step, lambda s, k: it * PER[id(s)] + k)
            for step in B_STEPS:
                b(step, lambda s, k: (B - 1) * PER[id(s)] + k)

        block = ctx.enter_context(nc.Block())

        x_v = x_in.rearrange("b (t p) d -> b p t d", p=P)
        o_v = out.rearrange("b (t p) d -> b p t d", p=P)

        wqkv_n = big[:, 0:6 * D].rearrange("p (m c) -> p m c", m=6)
        wo_n = big[:, 6 * D:8 * D].rearrange("p (m c) -> p m c", m=2)
        a1_n = big[:, 8 * D:10 * D].rearrange("p (m c) -> p m c", m=2)
        w_n = big[:, 10 * D:12 * D].rearrange("p (m c) -> p m c", m=2)
        a2_n = big[:, 12 * D:14 * D].rearrange("p (m c) -> p m c", m=2)
        wT = big[:, 14 * D:16 * D].rearrange("p (k c) -> p k c", k=2)
        a12 = big[:, 16 * D:18 * D].rearrange("p (k c) -> p k c", k=2)
        alog = big[:, 18 * D:18 * D + 32].rearrange("p (k n) -> p k n", k=2)
        aexp = big[:, 18 * D + 32:18 * D + 64].rearrange("p (k n) -> p k n", k=2)
        aT16 = big[0:N_STATES, 19 * D:20 * D]
        nsel = big[0:N_STATES, 20 * D:20 * D + N_STATES * P].rearrange("p (n m) -> p n m", n=N_STATES)
        br = fsum[:, :, :].rearrange("p a b -> p (a b)")[:, 0:7 * 512].rearrange("p (k c) -> p k c", k=7)

        ROWS = (0, 32, 64)

        def first_tiles(eng, n):
            eng.wait_ge(first_s, n(first_s, 6))
            eng.sem_inc(passed, 1)
            return [eng.value_load(first_c[P - 1:P, q:q + 1], min_val=0, max_val=T - 1) for q in range(NQ)]

        def later_tiles(eng, c0, done, unit):
            for q in range(NQ):
                with eng.If(c0[q] < T - 1):
                    with eng.Fori(c0[q] + 1, T) as c:
                        unit(q, c, eng.snap(done))
                        eng.reg_add(done, done, 1)
            k = eng.snap(done)
            return k

        @block.sync
        def _(sp):
            def col(v):
                return v.rearrange("(m p) -> p m", p=P)

            def row(v):
                return v.rearrange("(a n) -> a n", a=1)

            sp.wait_ge(const, 7)
            loads = [
                (wqkv_n, w["L0_attn_Wqkv"].rearrange("(m p) c -> p m c", p=P)),
                (wo_n, w["L0_attn_Wout"].rearrange("(m p) c -> p m c", p=P)),
                (a1_n, w["L0_ffn_aux_weight1"].rearrange("(m p) c -> p m c", p=P)),
                (w_n, w["L0_ffn_weight"].rearrange("(m p) c -> p m c", p=P)),
                (a2_n, w["L0_ffn_aux_weight2"].rearrange("(m p) c -> p m c", p=P)),
                (alog, w["L1_attn_A_log"].rearrange("(m p) n -> p m n", p=P)),
                (wx[:, :, :], w["L1_attn_W_x"].rearrange("(k p) n -> p k n", p=P)),
                (wdt[:, :], w["L1_attn_W_dt"]),
                (wo1[:, :, :], w["L1_attn_W_out"].rearrange("(k p) n -> p k n", p=P)),
                (wenc[:, :, :], w["L1_ffn_enc_w"].rearrange("(k p) n -> p k n", p=P)),
                (ws2c[:, :, 0, :], w["L1_ffn_s2c_w"].rearrange("(k p) n -> p k n", p=P)),
                (ws2c[:, :, 1, :], w["L1_ffn_s2c_w"].rearrange("(k p) n -> p k n", p=P)),
                (wr1[0:MD, :], w["L1_ffn_r_w1"]),
                (wr2[0:MD, :], w["L1_ffn_r_w2"]),
                (wr2[MD:MD + 1, :], row(w["L1_ffn_r_b2"])),
                (we1[0:MD, :, :], w["L1_ffn_e_w1"].rearrange("e d h -> d e h")),
                (wc2s[0:MD, :], w["L1_ffn_c2s_w"]),
                (wdec[:, :, :], w["L1_ffn_dec_w"].rearrange("(k p) n -> p k n", p=P)),
                (d_all[:, :], w["L1_attn_D"].partition_broadcast(P)),
                (lng_all[:, :], w["L1_ffn_ln_g"].partition_broadcast(P)),
                (bqk[:, 0, :], col(w["L0_attn_bqkv"][0:D])),
                (bqk[:, 1, :], col(w["L0_attn_bqkv"][D:2 * D])),
                (benc[:, :], col(w["L1_ffn_enc_b"])),
                (bs2c[0:MD, :], w["L1_ffn_s2c_b"].rearrange("(p a) -> p a", a=1)),
                (bs2c[MD:P, :], w["L1_ffn_s2c_b"].rearrange("(p a) -> p a", a=1)),
                (br1[:, :], w["L1_ffn_r_b1"].rearrange("(p a) -> p a", a=1)),
                (bc2s[:, :], col(w["L1_ffn_c2s_b"])),
            ]
            for k in range(EK):
                loads.append((we2[:, :, k, :], w["L1_ffn_e_w2"][:, k * P:(k + 1) * P, :].rearrange("e p d -> p e d")))
                loads.append((be1[:, :, k], w["L1_ffn_e_b1"][:, k * P:(k + 1) * P].rearrange("e p -> p e")))
            for r in ROWS:
                for k, v in ((BV, w["L0_attn_bqkv"][2 * D:3 * D]), (BFFN, w["L0_ffn_bias"]), (BDT, w["L1_attn_b_dt"]),
                             (BOUT, w["L0_attn_bout"]), (BOUT1, w["L1_attn_b_out"]), (BDEC, w["L1_ffn_dec_b"])):
                    for i in range(2):
                        loads.append((br[r:r + 1, k, i * D:(i + 1) * D], row(v)))
                loads.append((br[r:r + 1, BE2, :], w["L1_ffn_e_b2"].rearrange("(a e) d -> a (e d)", a=1)))
                for i in range(2):
                    loads.append((ob[r:r + 1, i, :], row(w["L1_ffn_ln_b"])))
            with nc.allow_non_contiguous_dma("small vectors, once"):
                for dst, src in loads:
                    sp.dma_start(dst, src).then_inc(w_in, 16)
            assert len(loads) == W_LOADS
            sp.sem_inc(stored, 16)
            sp.dma_start(xb[:, :, :], x_v[0]).then_inc(x_in_s, 16)
            with sp.Fori(0, B - 1) as it:
                def n(s, k):
                    return it * PER[id(s)] + k

                after_it = sp.snap(it + 1)
                nxt = x_v[bass.ds(after_it, 1)].rearrange("o p t d -> p (o t) d")
                dst = o_v[bass.ds(it, 1)].rearrange("o p t d -> p (o t) d")
                sp.wait_ge(xth, n(xth, 1))
                sp.sem_inc(passed, 1)
                sp.dma_start(xb[:, :, :], nxt).then_inc(x_in_s, 16)
                sp.wait_ge(out_s, n(out_s, T))
                sp.sem_inc(passed, 1)
                sp.dma_start(dst, ob[:, :, :]).then_inc(stored, 16)
            sp.wait_ge(out_s, B * T)
            sp.dma_start(o_v[B - 1], ob[:, :, :]).then_inc(stored, 16)
            sp.wait_ge(stored, 16 * (B + 1))

        @block.gpsimd
        def _(pool):
            def keep(t, pattern, base, mult, fill, last=const):
                pool.affine_select(out=t, in_=t, compare_op=ALU.is_ge, fill=fill, base=base,
                                   pattern=pattern, channel_multiplier=mult).then_inc(cdone, 1)

            for t in (wr1[:, :], we1[:, :, :], wc2s[:, :], br, kT[:, :, :], vh[:, :, :, :], ob[:, 0:2, :]):
                pool.memset(t, 0.0).then_inc(const, 1)
            sets = ((ident[:, :], 0.0), (ident16[:, :], 0.0), (ones[:, :], 1.0), (ones16[:, :], 1.0), (upto[:, :], 1.0),
                    (after[:, :], 1.0), (mask[:, :, :], 0.0), (mask0[:, :, :], 0.0), (headsel[:, :], 1.0),
                    (lower[:, :, :], 1.0), (eps1[:, :], LN_EPS), (eps4[:, :], 4 * LN_EPS), (mhalf[:, :], -0.5),
                    (biasrow[:, :, :], 0.0), (pr[0][:, :, 0:WINDOW], 0.0), (pr[1][:, :, 0:WINDOW], 0.0), (pr[2][:, :, 0:WINDOW], 0.0),
                    (moeT[:, :], 0.0), (nsel, 1.0), (rhT[:, :], 1.0))
            for t, v in sets:
                pool.memset(t, v).then_inc(cdone, 1)
            pool.wait_ge(cdone, len(sets))
            for m in (ident, ident16):
                pool.affine_select(out=m[:, :], in_=m[:, :], compare_op=ALU.not_equal, fill=1.0, base=0,
                                   pattern=[[-1, P]], channel_multiplier=1).then_inc(cdone, 1)
            keep(upto[:, :], [[1, P]], 0, -1, 0.0)
            keep(after[:, :], [[-1, P]], -1, 1, 0.0)
            keep(lower[:, :, :].rearrange("p (t i) j -> p t i j", t=T), [[0, T], [1, E], [-1, E]], -1, 0, 0.0)
            keep(mask[:, :, :], [[0, 2], [1, KW]], -1, -1, NEG)
            keep(mask0[:, :, :], [[0, 2], [1, KW]], -1, -1, NEG)
            keep(headsel[:, :], [[-DH, HH]], 0, 1, 0.0)
            keep(nsel, [[-1, N_STATES], [0, P]], 0, 1, 0.0)
            c = len(sets) + 9
            pool.wait_ge(cdone, c)
            keep(mask[:, :, :], [[0, 2], [-1, KW]], WINDOW, 1, NEG)
            keep(mask0[:, :, :], [[0, 2], [-1, KW]], WINDOW, 1, NEG)
            keep(headsel[:, :], [[DH, HH]], DH - 1, -1, 0.0)
            keep(nsel, [[1, N_STATES], [0, P]], 0, -1, 0.0)
            pool.wait_ge(cdone, c + 4)
            keep(mask0[:, :, :], [[0, 2], [1, KW]], -WINDOW, 0, NEG)

            pool.wait_ge(w_in, 16 * W_LOADS)
            pool.wait_ge(wt, WT_ALL)
            pool.sem_inc(y_l, 3)
            done = pool.alloc_register("later_pool")
            pool.reg_mov(done, 0)

            def norm(i, eps, n):
                b = min(i, 1)
                pool.wait_ge(aggr[i], n(aggr[i], T))
                pool.tensor_tensor(rstd[b][:, :], mv[b][:, :, 1], eps[:, :], ALU.add).then_inc(var[i], 1)
                pool.wait_ge(var[i], n(var[i], 1))
                pool.tensor_tensor(rstd[b][:, :], rstd[b][:, :], mhalf[:, :], ALU.pow).then_inc(rstd_s[i], 1)

            def queries(g, n):
                hf, a = g // 2, g % 2
                pool.wait_ge(q_s, n(q_s, hf + 1))
                if g >= 2:
                    pool.wait_ge(s_ps, n(s_ps, 8 * (g - 1)))
                pool.tensor_tensor(qm[g % 2], qT[:, hf:hf + 1, :].to_broadcast([P, G, L]),
                                   headsel[:, a * G:(a + 1) * G].unsqueeze(2).to_broadcast([P, G, L]),
                                   ALU.mult).then_inc(qm_s, 1)

            def a(step, n):
                if step == "norm":
                    norm(0, eps1, n)
                elif step == "q":
                    queries(0, n)
                elif step == "k":
                    queries(1, n)
                elif step == "close":
                    pool.wait_ge(th_s, n(th_s, 2))
                    if n is not n0:
                        pool.wait_ge(out_s, n(out_s, 0))
                    pool.tensor_tensor(x1[:, :, :], xb[:, :, :], th[:, :, :], ALU.add).then_inc(xth, 1)
                elif isinstance(step, int):
                    u = step
                    pool.wait_ge(prc_s, n(prc_s, u + 1))
                    p = pr[u % 3][:, :, WINDOW:2 * P]
                    pool.tensor_tensor(p, p, prc[:, u % 4, :].unsqueeze(2).to_broadcast([P, 2, KW]),
                                       ALU.mult).then_inc(pn, 1)
                    if u == 6:
                        queries(2, n)
                    if u == 14:
                        queries(3, n)

            c0 = [None] * NQ

            def b(step, n):
                if step == "norm":
                    norm(1, eps1, n)
                elif step == "xT":
                    pool.wait_ge(xn_s[1], n(xn_s[1], T))
                    pool.tensor_tensor(ysum[:, :, :], xn2[:, :, :], d_all[:, :].unsqueeze(1).to_broadcast([P, T, D]),
                                       ALU.mult).then_inc(yu, 1)
                elif step == "tail":
                    pool.wait_ge(delta_s, n(delta_s, 1))
                    pool.tensor_tensor(dsum[:, 1, :], delta[:, 2, :], delta[:, 3, :], ALU.add).then_inc(dsum_s, 1)
                    pool.wait_ge(dsum_s, n(dsum_s, 1))
                    pool.tensor_tensor(dsum[:, 0, :], delta[:, 1, :], dsum[:, 1, :], ALU.add).then_inc(dsum_s, 1)
                    pool.tensor_tensor(gg[:, :, :], delta[:, :, :], xn2[:, :, :], ALU.mult).then_inc(g_s, 1)
                elif step == "first":
                    c0[:] = first_tiles(pool, n)
                elif step.startswith("scan"):
                    q = int(step[4:])
                    X = ee_t[q % 2]
                    pool.wait_ge(xx, n(xx, 2 * q + 2))
                    pool.tensor_tensor(X[:, 0:2, :], X[:, 0:2, :], X[:, 2:4, :], ALU.add).then_inc(ya, 1)
                    pool.wait_ge(ya, n(ya, 3 * q + 1))
                    pool.tensor_tensor(X[:, 0, :], X[:, 0, :], X[:, 1, :], ALU.add).then_inc(ya, 1)
                    pool.wait_ge(ya, n(ya, 3 * q + 2))
                    pool.sem_inc(passed, 1)
                    y = ysum[:, bass.ds(c0[q], 1), :]
                    pool.tensor_tensor(y, y, X[:, 0:1, :], ALU.add).then_inc(ya, 1)
                elif step == "later":
                    def later(q, c, k):
                        X = ee_t[0]
                        pool.wait_ge(ps_l, k + 1)
                        F = fsum[:, q, :].rearrange("p (a d) -> p a d", a=Q)
                        pool.tensor_tensor(F, F, f_later, ALU.add).then_inc(fs_l, 1)
                        pool.wait_ge(x_l, k + 1)
                        pool.tensor_tensor(X[:, 0:2, :], X[:, 0:2, :], X[:, 2:4, :], ALU.add).then_inc(y_l, 1)
                        pool.wait_ge(y_l, k * 3 + 4)
                        pool.tensor_tensor(X[:, 0, :], X[:, 0, :], X[:, 1, :], ALU.add).then_inc(y_l, 1)
                        pool.wait_ge(y_l, k * 3 + 5)
                        pool.sem_inc(passed, 1)
                        y = ysum[:, bass.ds(c, 1), :]
                        pool.tensor_tensor(y, y, X[:, 0:1, :], ALU.add).then_inc(y_l, 1)

                    later_tiles(pool, c0, done, later)
                elif step.startswith("expert"):
                    e = int(step[6:])
                    if e:
                        pool.wait_ge(m1_s, n(m1_s, e + 1))
                        if e > 1:
                            pool.wait_ge(moe_s, n(moe_s, e - 1))
                        pool.tensor_tensor(moe[:, :, :], moe[:, :, :], m1[:, e % 2, :, :], ALU.add).then_inc(moe_s, 1)
                elif step == "out":
                    norm(2, eps4, n)

            passes(pool, a, b)

        @block.scalar
        def _(act):
            act.wait_ge(w_in, 16 * W_LOADS)
            act.activation(aexp, alog, ACT.Exp).then_inc(wt, 1)
            act.mul(benc[:, :], benc[:, :], 0.5).then_inc(wt, 1)
            act.mul(bc2s[:, :], bc2s[:, :], 0.5).then_inc(wt, 1)
            act.mul(bqk[:, 0, :], bqk[:, 0, :], DH ** -0.5).then_inc(wt, 1)
            act.wait_ge(wt, WT_ALL)
            done = act.alloc_register("later_act")
            act.reg_mov(done, 0)

            def a(step, n):
                if step == "norm":
                    for c in range(KC):
                        act.wait_ge(xnT_ps[0], n(xnT_ps[0], c + 1))
                        act.activation(xnT[:, c, :], A[c], ACT.Copy).then_inc(xnT_s[0], 1)
                elif step == "q":
                    for hf in range(KC):
                        act.wait_ge(q_ps, n(q_ps, hf + 1))
                        act.activation(qT[:, hf, :], A[2 + hf], ACT.Identity, bias=bqk[:, 0, hf:hf + 1],
                                       scale=DH ** -0.5).then_inc(q_s, 1)
                elif step == "k":
                    for hf in range(KC):
                        act.wait_ge(k_ps, n(k_ps, hf + 1))
                        act.activation(kT[:, hf, WINDOW:WINDOW + L], A[hf], ACT.Identity,
                                       bias=bqk[:, 1, hf:hf + 1]).then_inc(k_s, 1)
                elif step == "h":
                    for k in range(2):
                        act.wait_ge(h_ps, n(h_ps, k + 1))
                        act.activation(th[:, 2 * k:2 * k + 2, :].rearrange("p t d -> p (t d)"), A[k], ACT.Tanh).then_inc(th_s, 1)
                    softmax_exp(0, n)
                    softmax_exp(1, n)
                elif step == "close":
                    aT_copy(1, n)
                elif isinstance(step, int):
                    if step + 2 < NU:
                        softmax_exp(step + 2, n)
                    if step == NU // 2:
                        aT_copy(0, n)

            def softmax_exp(u, n):
                act.wait_ge(nmax_s, n(nmax_s, u + 1))
                if u >= 3:
                    act.wait_ge(pT_ps, n(pT_ps, u - 2))
                for i in range(2):
                    last = act.activation(pr[u % 3][:, i, WINDOW:2 * P], u_bank[u][:, KW * i:KW * (i + 1)], ACT.Exp,
                                          bias=nmax[:, u % 4, i:i + 1], accum_out=psm[:, u % 4, i:i + 1])
                last.then_inc(pexp, 1)

            def aT_copy(hf, n):
                act.wait_ge(pv, n(pv, NU // 2 * (hf + 1)))
                act.activation(aT[:, hf, :], O, ACT.Copy).then_inc(aT_s, 1)

            c0 = [None] * NQ

            def rates(name, i, m, ready, sig, bias, n):
                act.wait_ge(ready, n(ready, m + 1))
                act.activation(hidT[:, m, :], lb(name, m)[0], ACT.Tanh, bias=bias[:, m:m + 1], scale=0.5).then_inc(sig, 1)

            def b(step, n):
                if step == "xT":
                    for c in range(KC):
                        act.wait_ge(xnT_ps[1], n(xnT_ps[1], c + 1))
                        act.activation(xn2T[:, c, :], lb("xnT", c)[0], ACT.Copy).then_inc(xnT_s[1], 1)
                elif step == "xd":
                    act.wait_ge(xd_ps, n(xd_ps, 1))
                    act.activation(xdT[:, :], lb("xd", 0)[0][0:XD, :], ACT.Copy).then_inc(xd_s, 1)
                elif step == "dt":
                    act.wait_ge(bc_ps, n(bc_ps, 1))
                    act.activation(bc[:, :, :].rearrange("p t n -> p (t n)"), lb("bc", 0)[0][:, 0:T * 2 * N_STATES],
                                   ACT.Copy).then_inc(bc_s, 1)
                elif step == "softplus":
                    act.wait_ge(z_s, n(z_s, 2))
                    act.activation(az[:, :, :], z[:, :, :], ACT.Abs).then_inc(az_s, 1)
                    act.wait_ge(az_s, n(az_s, 1))
                    act.activation(az[:, :, :], az[:, :, :], ACT.Exp, scale=-1.0).then_inc(ez_s, 1)
                    act.wait_ge(ez_s, n(ez_s, 1))
                    act.activation(az[:, :, :], az[:, :, :], ACT.Ln, bias=1.0).then_inc(lz_s, 1)
                elif step == "first":
                    act.wait_ge(stored, n(stored, 16))
                    for k in range(2):
                        act.wait_ge(tail_ps, n(tail_ps, k + 1))
                        act.activation(tail[:, 2 * k:2 * k + 2, :].rearrange("p t d -> p (t d)"), lb("tail", k)[0],
                                       ACT.Copy).then_inc(tail_s, 1)
                    c0[:] = first_tiles(act, n)
                elif step in ("scan0", "scan2"):
                    q0 = int(step[4:])
                    for q in (q0, q0 + 1):
                        act.wait_ge(et, n(et, q + 1))
                        act.activation(e_t[q % 2], e_t[q % 2], ACT.Exp, scale=-1.0).then_inc(ee1, 1)
                    for q in (q0, q0 + 1):
                        act.wait_ge(ee1, n(ee1, q + 1))
                        if q >= 2:
                            act.wait_ge(ya, n(ya, 3 * (q - 1)))
                        act.activation(ee_t[q % 2], e_t[q % 2], ACT.Ln, bias=SCAN_EPS).then_inc(ee2, 1)
                    for q in (q0, q0 + 1):
                        act.wait_ge(ee2, n(ee2, q + 1))
                        act.activation(ee_t[q % 2], ee_t[q % 2], ACT.Exp, scale=-1.0).then_inc(rc_s, 1)
                elif step == "later":
                    def later(q, c, k):
                        act.wait_ge(et_l, k + 1)
                        act.activation(e_t[0], e_t[0], ACT.Exp, scale=-1.0).then_inc(e_l, 1)
                        act.wait_ge(e_l, k + 1)
                        act.activation(ee_t[0], e_t[0], ACT.Ln, bias=SCAN_EPS).then_inc(ln_l, 1)
                        act.wait_ge(ln_l, k + 1)
                        act.activation(ee_t[0], ee_t[0], ACT.Exp, scale=-1.0).then_inc(rc_l, 1)

                    later_tiles(act, c0, done, later)
                elif step == "yT":
                    for c in range(KC):
                        act.wait_ge(yT_ps, n(yT_ps, c + 1))
                        act.activation(yT[:, c, :], lb("yT", c)[0], ACT.Copy).then_inc(yT_s, 1)
                elif step.startswith("enc"):
                    rates("enc", 0, int(step[3:]), enc_ps, ts, benc, n)
                elif step == "cont":
                    act.wait_ge(cont_ps, n(cont_ps, 1))
                    act.activation(contT[:, :], lb("cont", 0)[0], ACT.Identity, bias=bs2c[:, :], scale=0.5).then_inc(cont_s, 1)
                elif step == "rh":
                    act.wait_ge(rh_ps, n(rh_ps, 1))
                    act.activation(rhT[0:MD, :], lb("rh", 0)[0][0:MD, :], ACT.Relu, bias=br1[:, :]).then_inc(rh_s, 1)
                elif step == "route":
                    act.wait_ge(route, n(route, 2))
                    act.activation(rt[:, 1, :], rt[:, 0, :], ACT.Exp).then_inc(rexp, 1)
                elif step.startswith("expert"):
                    e = int(step[6:])
                    for x in ((0, 1) if e == 0 else (e + 1,)):
                        if x < E:
                            act.wait_ge(e1_ps, n(e1_ps, x * EK + 1))
                            if x >= 2:
                                act.wait_ge(e2_ps, n(e2_ps, x - 1))
                            act.activation(eh[x % 2][:, 0, :], eb(x, 0), ACT.Relu, bias=be1[:, x, 0:1]).then_inc(eha, 1)
                elif step == "mT":
                    act.wait_ge(mT_ps, n(mT_ps, 1))
                    act.activation(moeT[0:MD, :], lb("mT", 0)[0][0:MD, :], ACT.Copy).then_inc(mT_s, 1)
                elif step.startswith("c2s"):
                    rates("c2s", 0, int(step[3:]), c2s_ps, tr, bc2s, n)
                elif step.startswith("dec"):
                    k = int(step[3:])
                    act.wait_ge(dec_ps, n(dec_ps, k + 1))
                    act.activation(td[:, 2 * k:2 * k + 2, :].rearrange("p t d -> p (t d)"), lb("dec", k)[0], ACT.Tanh,
                                   scale=0.25).then_inc(td_s, 1)

            passes(act, a, b)

        @block.vector
        def _(dve):
            dve.wait_ge(w_in, 16 * W_LOADS)
            dve.wait_ge(cdone, C_ALL)
            k = 4
            dve.wait_ge(wt, k)

            def prep(i, out_ap, in_ap):
                dve.wait_ge(wt_ps, i + 1)
                dve.tensor_copy(out_ap, in_ap).then_inc(wt, 1)

            prep(0, wqkvT[:, 0, :], ps[0][:, 0:768])
            prep(1, wqkvT[:, 1, :], ps[1][:, 0:768])
            prep(2, woaT[:, :, :, :].rearrange("p a k c -> p (a k c)"), ps[2][:, :])
            prep(3, wT.rearrange("p k c -> p (k c)"), ps[3][:, 0:512])
            prep(4, a12.rearrange("p k c -> p (k c)"), ps[0][:, 0:512])
            prep(5, wfused[:, :, :].rearrange("p k c -> p (k c)"), ps[1][:, 0:512])
            prep(6, aT16, ps[2][0:N_STATES, 0:D])
            for j in range(4):
                prep(7 + j, decay[:, 4 * j:4 * j + 4, :].rearrange("p n d -> p (n d)"), ps[3 if j % 2 else 0][:, :])
            dve.wait_ge(wt, 4 + 11)
            dve.tensor_reduce(least_a[:, :], decay[:, :, :].rearrange("p (q i) d -> p q (i d)", q=NQ), AX.X,
                              ALU.min).then_inc(wt, 1)
            dve.wait_ge(wt_ps, 12)
            dve.scalar_tensor_tensor(out=bs2c[:, :], in0=ps[1][:, 512:513], scalar=0.5, in1=bs2c[:, :],
                                     op0=ALU.mult, op1=ALU.add).then_inc(wt, 1)
            for i in range(2):
                dve.scalar_tensor_tensor(out=br[:, BDEC, i * D:(i + 1) * D], in0=br[:, BDEC, i * D:(i + 1) * D], scalar=2.0,
                                         in1=ps[1][:, 0:D], op0=ALU.mult, op1=ALU.add).then_inc(wt, 1)
            dve.tensor_tensor(br[:, BOUT1, :], br[:, BOUT1, :], ob[:, 0:2, :].rearrange("p a d -> p (a d)"),
                              ALU.add).then_inc(wt, 1)
            k = 4 + 11 + 5
            dve.wait_ge(wt, k)
            part = [qT[:, :, :].rearrange("p k l -> p (k l)")[:, 256 * i:256 * (i + 1)].bitcast(BF16) for i in range(2)]
            for kk in range(7):
                for j, r in enumerate(ROWS):
                    dve.tensor_copy(part[0], br[:, kk, :]).then_inc(wt, 1)
                    k += 1
                    dve.wait_ge(wt, k)
                    dve.tensor_copy(biasrow[r:r + 1, kk, :], part[0][r:r + 1, :]).then_inc(wt, 1)
                    dve.tensor_tensor(br[:, kk, :], br[:, kk, :], part[0], ALU.subtract).then_inc(wt, 1)
                    k += 2
                    dve.wait_ge(wt, k)
            assert k == WT_ALL, k

            done = dve.alloc_register("later_dve")
            dve.reg_mov(done, 0)

            def norm(i, src, ready, count, n):
                b = min(i, 1)
                for t in range(T):
                    dve.wait_ge(ready, n(ready, count(t)))
                    dve.bn_stats(stat[b][:, t, :], src[:, t, :]).then_inc(stats[i], 1)
                for t in range(T):
                    dve.wait_ge(stats[i], n(stats[i], t + 1))
                    dve.sem_inc(passed, 1)
                    dve.bn_aggr(mv[b][:, t, :], stat[b][:, t, :]).then_inc(aggr[i], 1)

            def normal(i, dst, src, n):
                b = min(i, 1)
                dve.wait_ge(rstd_s[i], n(rstd_s[i], 1))
                for t in range(T):
                    dve.tensor_scalar(dst[:, t, :], src[:, t, :], mv[b][:, t, 0:1], rstd[b][:, t:t + 1], ALU.subtract,
                                      ALU.mult).then_inc(xn_s[i], 1)

            def row_max(u, n):
                dve.wait_ge(s_ps, n(s_ps, u + 1))
                dve.tensor_reduce(nmax[:, u % 4, :], u_bank[u][:, 0:2 * KW].rearrange("p (i k) -> p i k", i=2), AX.X,
                                  ALU.max, negate=True).then_inc(nmax_s, 1)

            def a(step, n):
                if step == "norm":
                    norm(0, xb, x_in_s, lambda t: 16, n)
                    normal(0, xn, xb, n)
                elif step == "v":
                    for k in range(2):
                        dve.wait_ge(v_ps, n(v_ps, k + 1))
                        for par in range(2):
                            vsrc = A[2 + k].rearrange("p (t g b d) -> p t g b d", t=2, g=H // 2, b=2)[:, :, :, par, :]
                            vdst = vh[:, 2 * k:2 * k + 2, :, :].rearrange("p t (g b) (c d) -> p t g b c d", b=2, c=2)
                            dve.tensor_copy(vdst[:, :, :, par, par, :], vsrc).then_inc(v_s, 1)
                elif step == "h":
                    row_max(0, n)
                    row_max(1, n)
                elif step == "close":
                    dve.wait_ge(xth, n(xth, 1))
                    for k in range(2):
                        dve.wait_ge(y0_ps, n(y0_ps, k + 1))
                        x = x1[:, 2 * k:2 * k + 2, :].rearrange("p t d -> p (t d)")
                        dve.tensor_tensor(x, x, A[2 + k], ALU.add).then_inc(x1_s, 1)
                elif isinstance(step, int):
                    u = step
                    t = UNITS[u][2]
                    dve.wait_ge(pexp, n(pexp, u + 1))
                    dve.reciprocal(prc[:, u % 4, :], psm[:, u % 4, :]).then_inc(prc_s, 1)
                    if u + 2 < NU:
                        row_max(u + 2, n)
                    dve.wait_ge(pT_ps, n(pT_ps, u + 1))
                    if u >= 2:
                        dve.wait_ge(pv, n(pv, u - 1))
                    w0 = 1 if t == 0 else 0
                    src = u_bank[u].rearrange("p (i w l) -> p i w l", i=2, w=2)
                    dve.tensor_copy(prT[u % 2][:, :, w0:2, :], src[:, :, w0:2, :]).then_inc(pT_s, 1)

            c0 = [None] * NQ

            def exponents(q, c, dst):
                return dve.tensor_tensor(dst, tail[:, bass.ds(c, 1), :].to_broadcast([P, Q, D]),
                                         decay[:, q * Q:(q + 1) * Q, :], ALU.mult)

            def inputs(q, c, src, dst):
                for i in range(Q):
                    s = q * Q + i
                    last = dve.scalar_tensor_tensor(out=dst[:, i, :], in0=src[:, i, :],
                                                    scalar=bc[:, bass.ds(c, 1), s:s + 1].rearrange("p a n -> p (a n)"),
                                                    in1=gg[:, bass.ds(c, 1), :].rearrange("p a d -> p (a d)"),
                                                    op0=ALU.mult, op1=ALU.mult)
                return last

            def outputs(q, c, i, src, dst):
                for k in range(2):
                    s = N_STATES + q * Q + i + k
                    last = dve.scalar_tensor_tensor(out=dst[:, i + k, :], in0=src[:, k * D:(k + 1) * D],
                                                    scalar=bc[:, bass.ds(c, 1), s:s + 1].rearrange("p a n -> p (a n)"),
                                                    in1=dst[:, i + k, :], op0=ALU.mult, op1=ALU.mult)
                return last

            def b(step, n):
                if step == "norm":
                    norm(1, x1, x1_s, lambda t: t // 2 + 1, n)
                    normal(1, xn2, x1, n)
                elif step == "dt":
                    for k in range(2):
                        dve.wait_ge(dt_ps, n(dt_ps, k + 1))
                        dve.tensor_copy(z[:, 2 * k:2 * k + 2, :].rearrange("p t d -> p (t d)"), lb("dt", k)[0]).then_inc(z_s, 1)
                elif step == "tail":
                    dve.wait_ge(lz_s, n(lz_s, 1))
                    dve.scalar_tensor_tensor(out=delta[:, :, :], in0=z[:, :, :], scalar=0.0, in1=az[:, :, :], op0=ALU.max,
                                             op1=ALU.add).then_inc(delta_s, 1)
                elif step == "first":
                    rows = slice(P - 32, P)
                    dve.wait_ge(tail_s, n(tail_s, 2))
                    dve.tensor_reduce(least_t[rows, :], tail[rows, 0:T - 1, :], AX.X, ALU.min).then_inc(first_s, 1)
                    for c in range(1, T - 1):
                        dve.wait_ge(first_s, n(first_s, c))
                        dve.tensor_tensor(least_t[rows, c:c + 1], least_t[rows, c:c + 1], least_t[rows, c - 1:c],
                                          ALU.min).then_inc(first_s, 1)
                    dve.wait_ge(first_s, n(first_s, T - 1))
                    dve.tensor_tensor(past[rows, :, :], least_t[rows, :].unsqueeze(1).to_broadcast([32, NQ, T - 1]),
                                      least_a[rows, :].unsqueeze(2).to_broadcast([32, NQ, T - 1]), ALU.mult).then_inc(first_s, 1)
                    dve.wait_ge(first_s, n(first_s, T))
                    dve.tensor_scalar(past[rows, :, :], past[rows, :, :], ZERO_FROM, None, ALU.is_gt).then_inc(first_s, 1)
                    dve.wait_ge(first_s, n(first_s, T + 1))
                    with nc.allow_low_precision("counts of at most three"):
                        dve.tensor_reduce(first_c[rows, :], past[rows, :, :], AX.X, ALU.add).then_inc(first_s, 1)
                    c0[:] = first_tiles(dve, n)
                    dve.wait_ge(g_s, n(g_s, 1))
                    dve.wait_ge(bc_s, n(bc_s, 1))
                    for q in range(2):
                        exponents(q, c0[q], e_t[q]).then_inc(et, 1)
                elif step.startswith("scan"):
                    q0 = int(step[4:])
                    F = fsum[:, q0, :].rearrange("p (i d) -> p i d", i=Q)
                    dve.wait_ge(ee1, n(ee1, q0 + 1))
                    inputs(q0, c0[q0], e_t[q0 % 2], F).then_inc(f_s, 1)
                    if q0 + 2 < NQ:
                        dve.wait_ge(f_s, n(f_s, q0 + 1))
                        dve.wait_ge(ee2, n(ee2, q0 + 1))
                        exponents(q0 + 2, c0[q0 + 2], e_t[q0 % 2]).then_inc(et, 1)
                    dve.wait_ge(rc_s, n(rc_s, q0 + 1))
                    for i in range(2):
                        dve.wait_ge(sc_ps, n(sc_ps, 2 * q0 + i + 1))
                        outputs(q0, c0[q0], 2 * i, lb("scan", 2 * q0 + i)[0], ee_t[q0 % 2]).then_inc(xx, 1)
                elif step == "later":
                    def later(q, c, k):
                        dve.wait_ge(y_l, k * 3 + 3)
                        exponents(q, c, e_t[0]).then_inc(et_l, 1)
                        dve.wait_ge(e_l, k + 1)
                        inputs(q, c, e_t[0], f_later).then_inc(f_l, 1)
                        dve.wait_ge(rc_l, k + 1)
                        dve.wait_ge(ps_l, k + 1)
                        for i in range(2):
                            last = outputs(q, c, 2 * i, lb("later", i)[0], ee_t[0])
                        last.then_inc(x_l, 1)

                    dve.wait_ge(ya, n(ya, 3 * NQ))
                    dve.sem_inc(passed, 1)
                    later_tiles(dve, c0, done, later)
                elif step == "y1":
                    for k in range(2):
                        dve.wait_ge(y1_ps, n(y1_ps, k + 1))
                        x = x1[:, 2 * k:2 * k + 2, :].rearrange("p t d -> p (t d)")
                        dve.tensor_tensor(x, x, lb("y1", k)[0], ALU.add).then_inc(x2_s, 1)
                elif step == "route":
                    def after_step(k):
                        dve.wait_ge(route, n(route, k))

                    lg = lb("lg", 0)[0][:, 0:T * E].rearrange("p (t e) -> p t e", t=T)
                    r3 = [rt[:, j, :].rearrange("p (t e) -> p t e", t=T) for j in range(5)]
                    pr3 = [pair[:, j, :].rearrange("p (i e) -> p i e", e=E) for j in range(2)]
                    p4 = [pair[:, j, :].rearrange("p (t i e) -> p t i e", t=T, e=E) for j in range(2)]
                    lj = r3[0].unsqueeze(2).to_broadcast([P, T, E, E])
                    li = r3[0].unsqueeze(3).to_broadcast([P, T, E, E])
                    dve.wait_ge(lg_ps, n(lg_ps, 1))
                    dve.tensor_reduce(rs[:, 0, :], lg, AX.X, ALU.max).then_inc(route, 1)
                    after_step(1)
                    dve.tensor_tensor(r3[0], lg, rs[:, 0, :].unsqueeze(2).to_broadcast([P, T, E]), ALU.subtract).then_inc(route, 1)
                    after_step(2)
                    dve.tensor_tensor(p4[0], lj, li, ALU.is_gt).then_inc(route, 1)
                    dve.tensor_tensor(p4[1], lj, li, ALU.is_equal).then_inc(route, 1)
                    after_step(4)
                    dve.tensor_tensor(pr3[1], pr3[1], lower[:, :, :], ALU.mult).then_inc(route, 1)
                    after_step(5)
                    dve.tensor_tensor(pr3[0], pr3[0], pr3[1], ALU.add).then_inc(route, 1)
                    after_step(6)
                    dve.tensor_reduce(rt[:, 2, :], pr3[0], AX.X, ALU.add).then_inc(route, 1)
                    after_step(7)
                    dve.wait_ge(rexp, n(rexp, 1))
                    dve.scalar_tensor_tensor(out=rt[:, 3, :], in0=rt[:, 2, :], scalar=2.0, in1=rt[:, 1, :], op0=ALU.is_lt,
                                             op1=ALU.mult).then_inc(route, 1)
                    after_step(8)
                    dve.tensor_reduce(rs[:, 1, :], r3[3], AX.X, ALU.add).then_inc(route, 1)
                    after_step(9)
                    dve.reciprocal(rs[:, 2, :], rs[:, 1, :]).then_inc(route, 1)
                    after_step(10)
                    dve.tensor_tensor(r3[4], r3[3], rs[:, 2, :].unsqueeze(2).to_broadcast([P, T, E]), ALU.mult).then_inc(route, 1)
                elif step.startswith("expert"):
                    e = int(step[6:])
                    for x in ((0, 1) if e == 0 else (e + 1,)):
                        if x < E:
                            dve.wait_ge(e1_ps, n(e1_ps, x * EK + 2))
                            if x >= 2:
                                dve.wait_ge(e2_ps, n(e2_ps, x - 1))
                            dve.tensor_scalar(eh[x % 2][:, 1, :], eb(x, 1), be1[:, x, 1:2], 0.0, ALU.add,
                                              ALU.max).then_inc(ehv, 1)
                    dve.wait_ge(e2_ps, n(e2_ps, e + 1))
                    if e == 0:
                        dve.wait_ge(route, n(route, 11))
                    if e >= 3:
                        dve.wait_ge(moe_s, n(moe_s, e - 2))
                    share = rt[:, 4, :].rearrange("p (t e) -> p t e", t=T)[:, :, e:e + 1].to_broadcast([P, T, MD])
                    dst = moe[:, :, :] if e == 0 else m1[:, e % 2, :, :]
                    dve.tensor_tensor(dst, lb("e2", e)[0][:, 0:T * MD].rearrange("p (t d) -> p t d", t=T), share,
                                      ALU.mult).then_inc(m1_s, 1)
                elif step == "out":
                    norm(2, td, td_s, lambda t: t // 2 + 1, n)
                    dve.wait_ge(rstd_s[2], n(rstd_s[2], 1))
                    for t in range(T):
                        dve.scalar_tensor_tensor(out=td[:, t, :], in0=td[:, t, :], scalar=mv[1][:, t, 0:1], in1=lng_all[:, :],
                                                 op0=ALU.subtract, op1=ALU.mult).then_inc(n3, 1)
                    for t in range(T):
                        dve.wait_ge(n3, n(n3, t + 1))
                        dve.scalar_tensor_tensor(out=ob[:, t, :], in0=td[:, t, :], scalar=rstd[1][:, t:t + 1], in1=x1[:, t, :],
                                                 op0=ALU.mult, op1=ALU.add).then_inc(out_s, 1)

            passes(dve, a, b)

        @block.tensor
        def _(pe):
            pe.wait_ge(w_in, 16 * W_LOADS)
            pe.wait_ge(cdone, C_ALL)
            for k in range(KC):
                for m in range(6):
                    mm = pe.transpose(ps[k][:, m * P:(m + 1) * P], wqkv_n[:, m, k * P:(k + 1) * P], ident[:, :])
                mm.then_inc(wt_ps, 1)
            for j, src in enumerate((wo_n, a1_n)):
                for k in range(KC):
                    for m in range(KC):
                        mm = pe.transpose(ps[2][:, 512 * j + k * D + m * P:512 * j + k * D + (m + 1) * P],
                                          src[:, m, k * P:(k + 1) * P], ident[:, :])
            mm.then_inc(wt_ps, 1)
            for k in range(KC):
                for m in range(KC):
                    mm = pe.transpose(ps[3][:, k * D + m * P:k * D + (m + 1) * P], w_n[:, m, k * P:(k + 1) * P], ident[:, :])
            mm.then_inc(wt_ps, 1)
            pe.wait_ge(wt, 4 + 3)
            for m in range(KC):
                for k in range(KC):
                    mm = pe.matmul(ps[0][:, m * D:(m + 1) * D], woaT[:, 1, k, m * P:(m + 1) * P], a2_n[:, k, :],
                                   start=k == 0, stop=k == KC - 1)
            mm.then_inc(wt_ps, 1)
            pe.wait_ge(wt, 4 + 5)
            for m in range(KC):
                for k in range(KC):
                    mm = pe.matmul(ps[1][:, m * D:(m + 1) * D], wT[:, k, m * P:(m + 1) * P], a12[:, k, :],
                                   start=k == 0, stop=k == KC - 1)
            mm.then_inc(wt_ps, 1)
            for k in range(KC):
                mm = pe.transpose(ps[2][0:N_STATES, k * P:(k + 1) * P], aexp[:, k, :], ident[:, :])
            mm.then_inc(wt_ps, 1)
            pe.wait_ge(wt, 4 + 7)
            for j in range(4):
                if j >= 2:
                    pe.wait_ge(wt, 4 + 7 + j - 1)
                for i in range(4):
                    mm = pe.matmul(ps[3 if j % 2 else 0][:, i * D:(i + 1) * D], nsel[:, 4 * j + i, :], aT16,
                                   start=True, stop=True)
                mm.then_inc(wt_ps, 1)
            for k in range(MH):
                pe.matmul(ps[1][:, 0:D], ones[:, :], wdec[:, k, :], start=k == 0, stop=k == MH - 1)
            for k in range(MH):
                mm = pe.matmul(ps[1][:, 512:513], ws2c[:, k, :, :].rearrange("p a d -> p (a d)"), ones[:, 0:1],
                               start=k == 0, stop=k == MH - 1)
            mm.then_inc(wt_ps, 1)
            pe.wait_ge(wt, WT_ALL)

            def half(bk, lhsT, rhs, k_n, k, t0):
                pe.matmul(bk, ones16[:, :], biasrow[:, k, :], start=True, stop=False)
                for t in (t0, t0 + 1):
                    for c in range(k_n):
                        mm = pe.matmul(bk[:, (t - t0) * D:(t - t0 + 1) * D], lhsT[:, c, t * P:(t + 1) * P], rhs[:, c, :],
                                       start=False, stop=c == k_n - 1 and t > t0)
                return mm

            done = pe.alloc_register("later_pe")
            pe.reg_mov(done, 0)

            def scores(u, n):
                hf, j, t = UNITS[u]
                g = hf * 2 + j // 2
                pe.wait_ge(qm_s, n(qm_s, g + 1))
                if u == 0:
                    pe.wait_ge(k_s, n(k_s, KC))
                    pe.wait_ge(v_s, n(v_s, 2))
                elif u == 1:
                    pe.wait_ge(v_s, n(v_s, 4))
                elif u in (2, 3):
                    pe.wait_ge(th_s, n(th_s, u - 1))
                else:
                    pe.wait_ge(pT_s, n(pT_s, u - 3))
                pe.matmul(u_bank[u][:, 0:2 * KW], ident16[:, :], (mask if t else mask0)[:, :, :].rearrange("p a k -> p (a k)"),
                          start=True, stop=False)
                for i in range(2):
                    mm = pe.matmul(u_bank[u][:, KW * i:KW * (i + 1)], qm[g % 2][:, 2 * (j % 2) + i, t * P:(t + 1) * P],
                                   kT[:, hf, t * P:t * P + KW], start=False, stop=i == 1)
                mm.then_inc(s_ps, 1)

            def weighted(u, n):
                hf, j, t = UNITS[u]
                pe.wait_ge(pT_s, n(pT_s, u + 1))
                if u == NU // 2:
                    pe.wait_ge(aT_s, n(aT_s, 1))
                todo = [(i, v) for i in range(2) for v in range(0 if t else 1, 2)]
                for i, v in todo:
                    mm = pe.matmul(O[32 * j:32 * j + 32, t * P:(t + 1) * P], vh[:, t - 1 + v, hf * HH + 2 * j + i, :],
                                   prT[u % 2][:, i, v, :], start=(i, v) == todo[0], stop=(i, v) == todo[-1])
                mm.then_inc(pv, 1)

            def a(step, n):
                if step == "norm":
                    pe.wait_ge(xn_s[0], n(xn_s[0], T))
                    for c in range(KC):
                        for t in range(T):
                            mm = pe.transpose(A[c][:, t * P:(t + 1) * P], xn[:, t, c * P:(c + 1) * P], ident[:, :])
                        mm.then_inc(xnT_ps[0], 1)
                elif step in ("q", "k"):
                    c0, b0, sig = (0, 2, q_ps) if step == "q" else (D, 0, k_ps)
                    pe.wait_ge(xnT_s[0], n(xnT_s[0], KC))
                    for hf in range(KC):
                        for c in range(KC):
                            mm = pe.matmul(A[b0 + hf], wqkvT[:, c, c0 + hf * P:c0 + (hf + 1) * P], xnT[:, c, :],
                                           start=c == 0, stop=c == KC - 1)
                        mm.then_inc(sig, 1)
                elif step == "v":
                    for k in range(2):
                        pe.wait_ge(q_s, n(q_s, k + 1))
                        half(A[2 + k], xnT, wqkvT[:, :, 2 * D:3 * D], KC, BV, 2 * k).then_inc(v_ps, 1)
                elif step == "h":
                    for k in range(2):
                        pe.wait_ge(k_s, n(k_s, k + 1))
                        half(A[k], xnT, wfused, KC, BFFN, 2 * k).then_inc(h_ps, 1)
                    scores(0, n)
                    scores(1, n)
                elif step == "close":
                    weighted(NU - 1, n)
                    pe.wait_ge(aT_s, n(aT_s, 2))
                    for k in range(2):
                        half(A[2 + k], aT, woaT[:, 0, :, :], KC, BOUT, 2 * k).then_inc(y0_ps, 1)
                elif isinstance(step, int):
                    u = step
                    t = UNITS[u][2]
                    if u + 2 < NU:
                        scores(u + 2, n)
                    pe.wait_ge(pn, n(pn, u + 1))
                    for i in range(2):
                        for v in range(0 if t else 1, 2):
                            mm = pe.transpose(u_bank[u][:, (2 * i + v) * P:(2 * i + v + 1) * P],
                                              pr[u % 3][:, i, v * P:(v + 1) * P], ident[:, :])
                    mm.then_inc(pT_ps, 1)
                    if u:
                        weighted(u - 1, n)

            c0s = [None] * NQ

            def use(name, i, n):
                bk, u = lb(name, i)
                if u >= 3:
                    _, s, k = USES[u - 3]
                    pe.wait_ge(s, n(s, k))
                return bk

            def expert_in(e, n):
                for k in range(EK):
                    pe.matmul(use("e1", e * EK + k, n), we1[:, e, k * P:(k + 1) * P], contT[:, :],
                              start=True, stop=True).then_inc(e1_ps, 1)

            def b(step, n):
                if step == "xT":
                    pe.wait_ge(xn_s[1], n(xn_s[1], T))
                    for c in range(KC):
                        bk = use("xnT", c, n)
                        for t in range(T):
                            mm = pe.transpose(bk[:, t * P:(t + 1) * P], xn2[:, t, c * P:(c + 1) * P], ident[:, :])
                        mm.then_inc(xnT_ps[1], 1)
                elif step == "xd":
                    pe.wait_ge(xnT_s[1], n(xnT_s[1], KC))
                    bk = use("xd", 0, n)
                    for c in range(KC):
                        mm = pe.matmul(bk[0:XD, :], wx[:, c, :], xn2T[:, c, :], start=c == 0, stop=c == KC - 1)
                    mm.then_inc(xd_ps, 1)
                elif step == "dt":
                    pe.wait_ge(xd_s, n(xd_s, 1))
                    for k in range(2):
                        bk = use("dt", k, n)
                        pe.matmul(bk, ones16[:, :], biasrow[:, BDT, :], start=True, stop=False)
                        for t in (2 * k, 2 * k + 1):
                            mm = pe.matmul(bk[:, (t - 2 * k) * D:(t - 2 * k + 1) * D], xdT[0:RANK, t * P:(t + 1) * P], wdt[:, :],
                                           start=False, stop=t > 2 * k)
                        mm.then_inc(dt_ps, 1)
                    bk = use("bc", 0, n)
                    pe.sem_inc(passed, 1)
                    for t in range(T):
                        mm = pe.transpose(bk[:, t * 2 * N_STATES:(t + 1) * 2 * N_STATES], xdT[RANK:XD, t * P:(t + 1) * P],
                                          ident[RANK:XD, RANK:XD])
                    mm.then_inc(bc_ps, 1)
                elif step == "first":
                    pe.wait_ge(dsum_s, n(dsum_s, 2))
                    for k in range(2):
                        bk = use("tail", k, n)
                        for c in (2 * k, 2 * k + 1):
                            o = bk[:, (c - 2 * k) * D:(c - 2 * k + 1) * D]
                            later = (dsum[:, 0, :], dsum[:, 1, :], delta[:, 3, :], None)[c]
                            mm = pe.matmul(o, after[:, :], delta[:, c, :], start=True, stop=later is None)
                            if later is not None:
                                mm = pe.matmul(o, ones[:, :], later, start=False, stop=True)
                        mm.then_inc(tail_ps, 1)
                    c0s[:] = first_tiles(pe, n)
                elif step.startswith("scan"):
                    q = int(step[4:])
                    pe.wait_ge(f_s, n(f_s, q + 1))
                    for i in range(2):
                        pe.matmul(use("scan", 2 * q + i, n), upto[:, :], fsum[:, q, 512 * i:512 * (i + 1)],
                                  start=True, stop=True).then_inc(sc_ps, 1)
                elif step == "later":
                    pe.wait_ge(xx, n(xx, 2 * NQ))
                    pe.sem_inc(passed, 1)

                    def later(q, c, k):
                        pe.wait_ge(f_l, k + 1)
                        for i in range(2):
                            o = lb("later", i)[0]
                            pe.matmul(o, ones[:, :], fsum[:, q, 512 * i:512 * (i + 1)], start=True, stop=False)
                            mm = pe.matmul(o, upto[:, :], f_later.rearrange("p q d -> p (q d)")[:, 512 * i:512 * (i + 1)],
                                           start=False, stop=True)
                        mm.then_inc(ps_l, 1)

                    c0s.append(later_tiles(pe, c0s, done, later))
                elif step == "yT":
                    pe.wait_ge(ya, n(ya, 3 * NQ))
                    pe.wait_ge(y_l, c0s.pop() * 3 + 3)
                    for c in range(KC):
                        bk = use("yT", c, n)
                        for t in range(T):
                            mm = pe.transpose(bk[:, t * P:(t + 1) * P], ysum[:, t, c * P:(c + 1) * P], ident[:, :])
                        mm.then_inc(yT_ps, 1)
                elif step == "y1":
                    pe.wait_ge(yT_s, n(yT_s, KC))
                    for k in range(2):
                        half(use("y1", k, n), yT, wo1, KC, BOUT1, 2 * k).then_inc(y1_ps, 1)
                elif step.startswith("enc"):
                    m = int(step[3:])
                    bk = use("enc", m, n)
                    for c in range(KC):
                        mm = pe.matmul(bk, wenc[:, c, m * P:(m + 1) * P], xn2T[:, c, :], start=c == 0, stop=c == KC - 1)
                    mm.then_inc(enc_ps, 1)
                elif step == "cont":
                    bk = use("cont", 0, n)
                    for m in range(MH):
                        pe.wait_ge(ts, n(ts, m + 1))
                        mm = pe.matmul(bk, ws2c[:, m, :, :].rearrange("p a d -> p (a d)"), hidT[:, m, :],
                                       start=m == 0, stop=m == MH - 1)
                    mm.then_inc(cont_ps, 1)
                elif step == "rh":
                    pe.wait_ge(cont_s, n(cont_s, 1))
                    pe.matmul(use("rh", 0, n)[0:MD, :], wr1[:, :], contT[:, :], start=True, stop=True).then_inc(rh_ps, 1)
                elif step == "lg":
                    pe.wait_ge(rh_s, n(rh_s, 1))
                    bk = use("lg", 0, n)
                    for t in range(T):
                        mm = pe.matmul(bk[:, t * E:(t + 1) * E], rhT[:, t * P:(t + 1) * P], wr2[:, :], start=True, stop=True)
                    mm.then_inc(lg_ps, 1)
                elif step == "route":
                    expert_in(0, n)
                elif step.startswith("expert"):
                    e = int(step[6:])
                    if e + 1 < E:
                        expert_in(e + 1, n)
                    pe.wait_ge(eha, n(eha, e + 1))
                    pe.wait_ge(ehv, n(ehv, e + 1))
                    bk = use("e2", e, n)
                    pe.matmul(bk[:, 0:T * MD].rearrange("p (t d) -> p t d", t=T), ones16[:, :],
                              biasrow[:, BE2, e * MD:(e + 1) * MD].unsqueeze(1).to_broadcast([P, T, MD]), start=True, stop=False)
                    for t in range(T):
                        for k in range(EK):
                            mm = pe.matmul(bk[:, t * MD:(t + 1) * MD], eh[e % 2][:, k, t * P:(t + 1) * P], we2[:, e, k, :],
                                           start=False, stop=t == T - 1 and k == EK - 1)
                    mm.then_inc(e2_ps, 1)
                elif step == "mT":
                    pe.wait_ge(moe_s, n(moe_s, E - 1))
                    bk = use("mT", 0, n)
                    pe.sem_inc(passed, 1)
                    for t in range(T):
                        mm = pe.transpose(bk[0:MD, t * P:(t + 1) * P], moe[:, t, :], ident[:, :])
                    mm.then_inc(mT_ps, 1)
                elif step.startswith("c2s"):
                    m = int(step[3:])
                    pe.wait_ge(mT_s, n(mT_s, 1))
                    pe.matmul(use("c2s", m, n), wc2s[:, m * P:(m + 1) * P], moeT[:, :], start=True, stop=True).then_inc(c2s_ps, 1)
                elif step.startswith("dec"):
                    k = int(step[3:])
                    pe.wait_ge(tr, n(tr, MH))
                    half(use("dec", k, n), hidT, wdec, MH, BDEC, 2 * k).then_inc(dec_ps, 1)

            passes(pe, a, b)


def kernel(**inputs):
    import numpy as _np
    import concourse.bacc as _bacc
    from concourse import mybir as _mybir
    from concourse.bass_utils import run_bass_kernel_spmd as _run

    nc = _bacc.Bacc("TRN2", target_bir_lowering=False, num_devices=1)
    arrays, args = {}, {}
    for name in inputs:
        a = _np.ascontiguousarray(inputs[name])
        arrays[f"in_{name}_dram"] = a
        args[name] = nc.dram_tensor(f"in_{name}_dram", a.shape, _mybir.dt.from_np(a.dtype), kind="ExternalInput").ap()
    x = args.pop("L0_attn_x")
    out = nc.dram_tensor("out_0_dram", x.shape, _mybir.dt.float32, kind="ExternalOutput").ap()
    layered_kernel(nc, x, args, out)
    r = _run(nc, [arrays], core_ids=[0])
    return r.results[0]["out_0_dram"]
```

```python
from contextlib import ExitStack

import concourse.bass as bass
from concourse import mybir


def layered_kernel(nc, x_in, w, out):
    F32 = mybir.dt.float32
    BF16 = mybir.dt.bfloat16
    F32R = mybir.dt.float32r
    ALU = mybir.AluOpType
    ACT = mybir.ActivationFunctionType
    AX = mybir.AxisListType

    B, L, D = x_in.shape
    P = 128
    T = L // P
    KC = D // P
    H, WINDOW = 16, 64
    DH = D // H
    HH = P // DH
    G = 2
    AHEAD = 3
    KW = P + WINDOW
    NEG = -1e30
    N_STATES = w["L1_attn_A_log"].shape[1]
    RANK = w["L1_attn_W_dt"].shape[0]
    XD = RANK + 2 * N_STATES
    HID = w["L1_ffn_enc_w"].shape[1]
    MH = HID // P
    E, MD, EH = w["L1_ffn_e_w1"].shape
    EK = EH // P
    Q = 4
    NQ = N_STATES // Q
    LN_EPS = 1e-5
    SCAN_EPS = 1e-12
    UNITS = [(hf, j, t) for hf in range(KC) for j in range(HH // 2) for t in range(T)]
    NU = len(UNITS)
    ZERO_FROM = 110.0

    ctx = ExitStack()
    with ctx:
        def sb(name, shape, dt=F32):
            return ctx.enter_context(nc.sbuf_tensor(name, shape, dt))

        ident = sb("ident", [P, P])
        ident16 = sb("ident16", [P, P], BF16)
        ones = sb("ones", [P, P])
        ones16 = sb("ones16", [P, P], BF16)
        upto = sb("upto", [P, P])
        after = sb("after", [P, P])
        mask = sb("mask", [P, 2, KW], BF16)
        mask0 = sb("mask0", [P, 2, KW], BF16)
        headsel = sb("headsel", [P, HH])
        lower = sb("lower", [P, T * E, E])
        eps1 = sb("eps1", [P, T])
        eps4 = sb("eps4", [P, T])
        mhalf = sb("mhalf", [P, T])
        wqkvT = sb("wqkvT", [P, KC, 3 * D])
        woaT = sb("woaT", [P, 2, KC, D])
        wfused = sb("wfused", [P, KC, D])
        wx = sb("wx", [P, KC, XD])
        wdt = sb("wdt", [RANK, D])
        wo1 = sb("wo1", [P, KC, D])
        wenc = sb("wenc", [P, KC, HID])
        ws2c = sb("ws2c", [P, MH, 2, MD])
        wr1 = sb("wr1", [P, MD], F32R)
        wr2 = sb("wr2", [MD + 1, E])
        we1 = sb("we1", [P, E, EH], F32R)
        we2 = sb("we2", [P, E, EK, MD])
        wc2s = sb("wc2s", [P, HID], F32R)
        wdec = sb("wdec", [P, MH, D])
        decay = sb("decay", [P, N_STATES, D])
        d_all = sb("d_all", [P, D])
        lng_all = sb("lng_all", [P, D])
        bqk = sb("bqk", [P, 2, KC])
        benc = sb("benc", [P, MH])
        bs2c = sb("bs2c", [P, 1])
        br1 = sb("br1", [MD, 1])
        be1 = sb("be1", [P, E, EK])
        bc2s = sb("bc2s", [P, MH])
        BV, BFFN, BDT, BOUT, BOUT1, BDEC, BE2 = range(7)
        biasrow = sb("biasrow", [P, 7, 512], BF16)

        xb = sb("xb", [P, T, D])
        xn = sb("xn", [P, T, D])
        xnT = sb("xnT", [P, KC, L])
        qT = sb("qT", [P, KC, L])
        kT = sb("kT", [P, KC, WINDOW + L])
        vh = sb("vh", [P, T, H, 2 * DH])
        th = sb("th", [P, T, D])
        pr = [sb(f"pr{i}", [P, 2, 2 * P]) for i in range(4)]
        prT = [sb(f"prT{i}", [P, 2, 2, P]) for i in range(2)]
        aT = qT
        x1 = sb("x1", [P, T, D])
        big = sb("big", [P, 6 * 1024])
        qm = [big[:, 1024 * i:1024 * (i + 1)].rearrange("p (h l) -> p h l", h=G) for i in range(2)]
        tmp = [big[:, 1024 * i:1024 * (i + 1)].rearrange("p (q d) -> p q d", q=Q) for i in range(2, 6)]
        e_t, ee_t = tmp[0:2], tmp[2:4]
        f_later = e_t[1]
        stat = [sb(f"stat{i}", [P, T, 6]) for i in range(2)]
        mv = [sb(f"mv{i}", [P, T, 2]) for i in range(2)]
        rstd = [sb(f"rstd{i}", [P, T]) for i in range(2)]
        nmax = sb("nmax", [P, 4, 2])
        psm = sb("psm", [P, 4, 2])
        prc = sb("prc", [P, 4, 2])
        least_a = sb("least_a", [P, NQ])
        least_t = sb("least_t", [P, T - 1])
        past = sb("past", [P, NQ, T - 1])
        first_c = sb("first_c", [P, NQ], mybir.dt.int32)
        xn2 = sb("xn2", [P, T, D])
        xn2T = sb("xn2T", [P, KC, L])
        xdT = ee_t[0].rearrange("p q d -> p (q d)")[0:XD, 0:L]
        bc = sb("bc", [P, T, 2 * N_STATES])
        z = sb("z", [P, T, D])
        az = sb("az", [P, T, D])
        delta, gg = az, z
        dsum = e_t[0][:, 0:2, :]
        tail = sb("tail", [P, T, D])
        fsum = sb("fsum", [P, NQ, Q * D])
        ysum = sb("ysum", [P, T, D])
        hidT = sb("hidT", [P, MH, L])
        eh = [sb("eh0", [P, EK, L]), xnT]
        contT = xn2T[:, 0, :]
        firstT = sb("firstT", [P, L], F32R)
        restT = sb("restT", [P, L], F32R)
        rhT = sb("rhT", [MD + 1, L])
        rt = sb("rt", [P, 5, T * E])
        pair = sb("pair", [P, 2, T * E * E])
        rs = sb("rs", [P, 3, T])
        m1 = sb("m1", [P, 2, T, MD])
        moe = sb("moe", [P, T, MD])
        moeT = contT
        ob = tail
        yT = az[:, :, :].rearrange("p t d -> p (t d)").rearrange("p (k l) -> p k l", k=KC)
        td = z

        psall = ctx.enter_context(nc.psum_tensor("psall", [P, 8, 512], F32))
        ps = [psall[:, 2 * i:2 * i + 2, :].rearrange("p a b -> p (a b)") for i in range(4)]
        bank = [psall[:, i, :] for i in range(8)]
        A, O, LB = bank[0:4], bank[4], bank[5:8]
        u_bank = [A[(u + 2) % 4] for u in range(NU)]
        W_LOADS = 81
        C_ALL = 34
        WT_ALL = 95
        PER = {}

        def sem(name, per):
            s = ctx.enter_context(nc.semaphore(name))
            PER[id(s)] = per
            return s

        w_in = sem("w_in", 0)
        cdone = sem("cdone", 0)
        const = sem("const", 0)
        wt_ps = sem("wt_ps", 0)
        wt = sem("wt", 0)
        x_in_s = sem("x_loaded", 16)
        stored = sem("stored", 16)
        passed = sem("passed", 0)
        stats = [sem(f"stats{i}", T) for i in range(3)]
        aggr = [sem(f"aggr{i}", T) for i in range(3)]
        var = [sem(f"var{i}", 1) for i in range(3)]
        rstd_s = [sem(f"rstd{i}", 1) for i in range(3)]
        xn_s = [sem(f"xnorm{i}", T) for i in range(2)]
        xnT_ps = [sem(f"xnT_ps{i}", KC) for i in range(2)]
        xnT_s = [sem(f"xnT{i}", KC) for i in range(2)]
        q_ps = sem("q_ps", KC)
        k_ps = sem("k_ps", KC)
        v_ps = sem("v_ps", 2)
        h_ps = sem("h_ps", 2)
        q_s = sem("q", KC)
        k_s = sem("k", KC)
        v_s = sem("v", 4)
        th_s = sem("th", 2)
        qm_s = sem("qm", H // G)
        s_ps = sem("score_ps", NU)
        nmax_s = sem("nmax", NU)
        pexp = sem("pexp", NU)
        prc_s = sem("prc", NU)
        pn = sem("pnorm", NU)
        pT_ps = sem("pT_ps", NU)
        pT_s = sem("pT", NU)
        pv = sem("pv", NU)
        aT_s = sem("aT", KC)
        y0_ps = sem("y0_ps", 2)
        xth = sem("x_plus_tanh", 1)
        x1_s = sem("x1_sum", 2)
        x1_c = sem("x1", 1)
        xd_ps = sem("xd_ps", 1)
        xd_s = sem("xd", 1)
        dt_ps = sem("dt_ps", 2)
        bc_ps = sem("bc_ps", 1)
        bc_s = sem("bc", 1)
        z_s = sem("z", 2)
        az_s = sem("az", 1)
        ez_s = sem("ez", 1)
        lz_s = sem("lz", 1)
        delta_s = sem("delta", 1)
        g_s = sem("g", 1)
        dsum_s = sem("dsum", 2)
        yu = sem("yu", 1)
        tail_ps = sem("tail_ps", 2)
        tail_s = sem("tail", 2)
        first_s = sem("first", 6)
        et = sem("et", NQ)
        ee1 = sem("e", NQ)
        ee2 = sem("e_eps", NQ)
        f_s = sem("f", NQ)
        rc_s = sem("rc", NQ)
        sc_ps = sem("scan_ps", NQ * 2)
        xx = sem("xx", NQ * 2)
        ya = sem("yadd", NQ * 3)
        et_l = sem("et_later", 0)
        e_l = sem("e_later", 0)
        ln_l = sem("e_eps_later", 0)
        rc_l = sem("rc_later", 0)
        f_l = sem("f_later", 0)
        ps_l = sem("scan_ps_later", 0)
        x_l = sem("xx_later", 0)
        fs_l = sem("fsum_later", 0)
        y_l = sem("yadd_later", 0)
        yT_ps = sem("yT_ps", KC)
        yT_s = sem("yT", KC)
        y1_ps = sem("y1_ps", 2)
        x2_s = sem("x2", 2)
        enc_ps = sem("enc_ps", MH)
        ts = sem("spikes", MH)
        cont_ps = sem("cont_ps", 1)
        cont_s = sem("cont", 1)
        split_s = sem("split", 4)
        rh_ps = sem("rh_ps", 1)
        rh_s = sem("rh", 1)
        lg_ps = sem("lg_ps", 1)
        route = sem("route", 11)
        rexp = sem("rexp", 1)
        e1_ps = sem("e1_ps", E * EK)
        eha = sem("eh_a", E)
        ehv = sem("eh_v", E)
        e2_ps = sem("e2_ps", E)
        m1_s = sem("m1", E)
        moe_s = sem("moe", E - 1)
        mT_ps = sem("mT_ps", 1)
        mT_s = sem("mT", 1)
        c2s_ps = sem("c2s_ps", MH)
        tr = sem("rates", MH)
        dec_ps = sem("dec_ps", 2)
        td_s = sem("td", 2)
        n3 = sem("n3", T)
        out_s = sem("out_ready", T)

        PLAN = (
            ("xT", []), ("q", []), ("k", ["norm"]), ("v", ["xT", "keep"]), ("h", ["xd", "enc0"]), (0, ["dt"]),
            (1, ["softplus", "enc1", "enc2", "enc3"]), (2, []), (3, ["softplus2"]), (4, ["cont", "delta"]),
            (5, ["g"]), (6, ["split", "tail"]), (7, ["first", "rh"]), (8, ["start", "exp0"]), (9, ["logits", "hid0"]),
            (10, ["in0", "ln0", "route"]), (11, ["sum0", "shares", "rc0"]), (12, ["in1", "out0", "mix0"]),
            (13, ["sum1", "mul0"]), (14, ["exp2"]), (15, ["out1", "hid1"]), (16, ["mix1", "ln2"]),
            (17, ["in2", "hid2", "mul1"]), (18, ["rc2", "in3", "mix2"]), (19, ["mul2"]), (20, []),
            (21, ["sum2", "out2", "hid3"]), (22, []), (23, ["mix3"]), (24, ["mul3", "sum3", "out3"]), (25, ["hid4"]),
            (26, ["later", "mix4"]), (27, ["mul4", "hid5", "yT"]), (28, ["mix5"]), (29, ["mul5", "y1a", "hid6"]),
            (30, ["y1b", "mix6"]), (31, ["mul6", "hid7"]), ("last", ["mix7", "mul7"]),
            ("close", ["mT", "msplit", "c2s0", "c2s1", "c2s2", "c2s3", "dec0", "dec1", "out"]),
        )
        BANKS = {"xT": [("xT", xnT_s[1], c + 1) for c in range(KC)], "xd": [("xd", xd_s, 1)],
                 "dt": [("dt", z_s, 1), ("dt", z_s, 2), ("dt", bc_s, 1)], "tail": [("tail", tail_s, 1), ("tail", tail_s, 2)],
                 "later": [("later", x_l, None)] * 2, "yT": [("yT", yT_s, c + 1) for c in range(KC)],
                 "y1a": [("y1a", x2_s, 1)], "y1b": [("y1b", x2_s, 2)],
                 "cont": [("cont", cont_s, 1)], "rh": [("rh", rh_s, 1)], "logits": [("route", route, 2)], "mT": [("mT", mT_s, 1)]}
        for i in range(NQ):
            BANKS[f"sum{i}"] = [(f"out{i}", xx, 2 * i + 1), (f"out{i}", xx, 2 * i + 2)]
        for i in range(MH):
            BANKS[f"enc{i}"] = [(f"enc{i}", ts, i + 1)]
            BANKS[f"c2s{i}"] = [(f"c2s{i}", tr, i + 1)]
        for i in range(E):
            BANKS[f"hid{i}"] = [(f"hid{i}", eha, i + 1), (f"hid{i}", ehv, i + 1)]
            BANKS[f"mix{i}"] = [(f"mul{i}", m1_s, i + 1)]
        for i in range(2):
            BANKS[f"dec{i}"] = [(f"dec{i}", td_s, i + 1)]

        B_STEPS = [b for _, bs in PLAN for b in bs]
        USES = [(step, i, x) for step in B_STEPS for i, x in enumerate(BANKS.get(step, []))]
        assert sorted(set(x[0] for x in USES)) == sorted(BANKS) and len(USES) % 3 == 0, len(USES)
        for k in range(3, len(USES)):
            assert B_STEPS.index(USES[k - 3][2][0]) <= B_STEPS.index(USES[k][0]), (USES[k - 3][:2], USES[k][:2])

        def lb(step, i):
            u = [k for k, x in enumerate(USES) if x[0:2] == (step, i)][0]
            return LB[u % 3], u

        def n0(s, k):
            return k

        def passes(eng, a, b):
            a("norm", n0)
            for step, _ in PLAN:
                if step == "last":
                    a("norm", lambda s, k: PER[id(s)] + k)
                a(step, n0)
            with eng.Fori(0, B - 1) as it:
                for step, steps in PLAN:
                    if step == "last":
                        with eng.If(it < B - 2):
                            a("norm", lambda s, k: it * PER[id(s)] + (2 * PER[id(s)] + k))
                    a(step, lambda s, k: it * PER[id(s)] + (PER[id(s)] + k))
                    for x in steps:
                        b(x, lambda s, k: it * PER[id(s)] + k)
            for step in B_STEPS:
                b(step, lambda s, k: (B - 1) * PER[id(s)] + k)

        block = ctx.enter_context(nc.Block())

        x_v = x_in.rearrange("b (t p) d -> b p t d", p=P)
        o_v = out.rearrange("b (t p) d -> b p t d", p=P)

        wqkv_n = big[:, 0:6 * D].rearrange("p (m c) -> p m c", m=6)
        wo_n = big[:, 6 * D:8 * D].rearrange("p (m c) -> p m c", m=2)
        a1_n = big[:, 8 * D:10 * D].rearrange("p (m c) -> p m c", m=2)
        w_n = big[:, 10 * D:12 * D].rearrange("p (m c) -> p m c", m=2)
        a2_n = big[:, 12 * D:14 * D].rearrange("p (m c) -> p m c", m=2)
        wT = big[:, 14 * D:16 * D].rearrange("p (k c) -> p k c", k=2)
        a12 = big[:, 16 * D:18 * D].rearrange("p (k c) -> p k c", k=2)
        alog = big[:, 18 * D:18 * D + 32].rearrange("p (k n) -> p k n", k=2)
        aexp = big[:, 18 * D + 32:18 * D + 64].rearrange("p (k n) -> p k n", k=2)
        aT16 = big[0:N_STATES, 19 * D:20 * D]
        nsel = hidT[0:N_STATES, :, :].rearrange("p m l -> p (m l)").rearrange("p (n m) -> p n m", n=N_STATES)
        br = fsum[:, :, :].rearrange("p a b -> p (a b)")[:, 0:7 * 512].rearrange("p (k c) -> p k c", k=7)

        flat = [t[:, :, :].rearrange("p t d -> p (t d)") for t in (xn2, th, ysum)]
        we1_n = [flat[i].rearrange("p (e h) -> p e h", e=E // 2) for i in range(2)]
        wc2s_n = flat[2][:, 0:HID]
        wr1_n = flat[2][:, HID:HID + MD]

        ROWS = (0, 32, 64)

        def first_tiles(eng, n):
            eng.wait_ge(first_s, n(first_s, 6))
            eng.sem_inc(passed, 1)
            return [eng.value_load(first_c[P - 1:P, q:q + 1], min_val=0, max_val=T - 1) for q in range(NQ)]

        def later_tiles(eng, c0, done, unit):
            for q in range(NQ):
                with eng.If(c0[q] < T - 1):
                    with eng.Fori(c0[q] + 1, T) as c:
                        unit(q, c, eng.snap(done))
                        eng.reg_add(done, done, 1)
            k = eng.snap(done)
            return k

        @block.sync
        def _(sp):
            def col(v):
                return v.rearrange("(m p) -> p m", p=P)

            def row(v):
                return v.rearrange("(a n) -> a n", a=1)

            sp.wait_ge(const, 4)
            loads = [
                (wqkv_n, w["L0_attn_Wqkv"].rearrange("(m p) c -> p m c", p=P)),
                (wo_n, w["L0_attn_Wout"].rearrange("(m p) c -> p m c", p=P)),
                (a1_n, w["L0_ffn_aux_weight1"].rearrange("(m p) c -> p m c", p=P)),
                (w_n, w["L0_ffn_weight"].rearrange("(m p) c -> p m c", p=P)),
                (a2_n, w["L0_ffn_aux_weight2"].rearrange("(m p) c -> p m c", p=P)),
                (alog, w["L1_attn_A_log"].rearrange("(m p) n -> p m n", p=P)),
                (wx[:, :, :], w["L1_attn_W_x"].rearrange("(k p) n -> p k n", p=P)),
                (wdt[:, :], w["L1_attn_W_dt"]),
                (wo1[:, :, :], w["L1_attn_W_out"].rearrange("(k p) n -> p k n", p=P)),
                (wenc[:, :, :], w["L1_ffn_enc_w"].rearrange("(k p) n -> p k n", p=P)),
                (ws2c[:, :, 0, :], w["L1_ffn_s2c_w"].rearrange("(k p) n -> p k n", p=P)),
                (ws2c[:, :, 1, :], w["L1_ffn_s2c_w"].rearrange("(k p) n -> p k n", p=P)),
                (wr2[0:MD, :], w["L1_ffn_r_w2"]),
                (wr2[MD:MD + 1, :], row(w["L1_ffn_r_b2"])),
                (wdec[:, :, :], w["L1_ffn_dec_w"].rearrange("(k p) n -> p k n", p=P)),
                (d_all[:, :], w["L1_attn_D"].partition_broadcast(P)),
                (lng_all[:, :], w["L1_ffn_ln_g"].partition_broadcast(P)),
                (bqk[:, 0, :], col(w["L0_attn_bqkv"][0:D])),
                (bqk[:, 1, :], col(w["L0_attn_bqkv"][D:2 * D])),
                (benc[:, :], col(w["L1_ffn_enc_b"])),
                (bs2c[0:MD, :], w["L1_ffn_s2c_b"].rearrange("(p a) -> p a", a=1)),
                (bs2c[MD:P, :], w["L1_ffn_s2c_b"].rearrange("(p a) -> p a", a=1)),
                (br1[:, :], w["L1_ffn_r_b1"].rearrange("(p a) -> p a", a=1)),
                (bc2s[:, :], col(w["L1_ffn_c2s_b"])),
            ]
            for rows in (slice(0, MD), slice(MD, P)):
                for i in range(2):
                    loads.append((we1_n[i][rows, :, :], w["L1_ffn_e_w1"][i * E // 2:(i + 1) * E // 2].rearrange("e d h -> d e h")))
                loads.append((wc2s_n[rows, :], w["L1_ffn_c2s_w"]))
                loads.append((wr1_n[rows, :], w["L1_ffn_r_w1"]))
            for k in range(EK):
                loads.append((we2[:, :, k, :], w["L1_ffn_e_w2"][:, k * P:(k + 1) * P, :].rearrange("e p d -> p e d")))
                loads.append((be1[:, :, k], w["L1_ffn_e_b1"][:, k * P:(k + 1) * P].rearrange("e p -> p e")))
            for r in ROWS:
                for k, v in ((BV, w["L0_attn_bqkv"][2 * D:3 * D]), (BFFN, w["L0_ffn_bias"]), (BDT, w["L1_attn_b_dt"]),
                             (BOUT, w["L0_attn_bout"]), (BOUT1, w["L1_attn_b_out"]), (BDEC, w["L1_ffn_dec_b"])):
                    for i in range(2):
                        loads.append((br[r:r + 1, k, i * D:(i + 1) * D], row(v)))
                loads.append((br[r:r + 1, BE2, :], w["L1_ffn_e_b2"].rearrange("(a e) d -> a (e d)", a=1)))
                for i in range(2):
                    loads.append((ob[r:r + 1, i, :], row(w["L1_ffn_ln_b"])))
            with nc.allow_non_contiguous_dma("small vectors, once"):
                for dst, src in loads:
                    sp.dma_start(dst, src).then_inc(w_in, 16)
            assert len(loads) == W_LOADS
            sp.sem_inc(stored, 16)
            sp.dma_start(xb[:, :, :], x_v[0]).then_inc(x_in_s, 16)
            sp.wait_ge(xth, 1)
            sp.dma_start(xb[:, :, :], x_v[1]).then_inc(x_in_s, 16)
            with sp.Fori(0, B - 2) as it:
                def n(s, k):
                    return it * PER[id(s)] + k

                after_next = sp.snap(it + 2)
                nxt = x_v[bass.ds(after_next, 1)].rearrange("o p t d -> p (o t) d")
                dst = o_v[bass.ds(it, 1)].rearrange("o p t d -> p (o t) d")
                sp.wait_ge(xth, n(xth, 2))
                sp.sem_inc(passed, 1)
                sp.dma_start(xb[:, :, :], nxt).then_inc(x_in_s, 16)
                sp.wait_ge(out_s, n(out_s, T))
                sp.sem_inc(passed, 1)
                sp.dma_start(dst, ob[:, :, :]).then_inc(stored, 16)
            for i in (B - 2, B - 1):
                sp.wait_ge(out_s, (i + 1) * T)
                sp.dma_start(o_v[i], ob[:, :, :]).then_inc(stored, 16)
            sp.wait_ge(stored, 16 * (B + 1))

        @block.gpsimd
        def _(pool):
            def keep(t, pattern, base, mult, fill, last=const):
                pool.affine_select(out=t, in_=t, compare_op=ALU.is_ge, fill=fill, base=base,
                                   pattern=pattern, channel_multiplier=mult).then_inc(cdone, 1)

            for t in (br, kT[:, :, :], vh[:, :, :, :], ob[:, 0:2, :]):
                pool.memset(t, 0.0).then_inc(const, 1)
            sets = ((ident[:, :], 0.0), (ident16[:, :], 0.0), (ones[:, :], 1.0), (ones16[:, :], 1.0), (upto[:, :], 1.0),
                    (after[:, :], 1.0), (mask[:, :, :], 0.0), (mask0[:, :, :], 0.0), (headsel[:, :], 1.0),
                    (lower[:, :, :], 1.0), (eps1[:, :], LN_EPS), (eps4[:, :], 4 * LN_EPS), (mhalf[:, :], -0.5),
                    (biasrow[:, :, :], 0.0), (pr[0][:, :, 0:WINDOW], 0.0), (pr[1][:, :, 0:WINDOW], 0.0), (pr[2][:, :, 0:WINDOW], 0.0), (pr[3][:, :, 0:WINDOW], 0.0),
                    (nsel, 1.0), (rhT[:, :], 1.0))
            for t, v in sets:
                pool.memset(t, v).then_inc(cdone, 1)
            pool.wait_ge(cdone, len(sets))
            for m in (ident, ident16):
                pool.affine_select(out=m[:, :], in_=m[:, :], compare_op=ALU.not_equal, fill=1.0, base=0,
                                   pattern=[[-1, P]], channel_multiplier=1).then_inc(cdone, 1)
            keep(upto[:, :], [[1, P]], 0, -1, 0.0)
            keep(after[:, :], [[-1, P]], -1, 1, 0.0)
            keep(lower[:, :, :].rearrange("p (t i) j -> p t i j", t=T), [[0, T], [1, E], [-1, E]], -1, 0, 0.0)
            keep(mask[:, :, :], [[0, 2], [1, KW]], -1, -1, NEG)
            keep(mask0[:, :, :], [[0, 2], [1, KW]], -1, -1, NEG)
            keep(headsel[:, :], [[-DH, HH]], 0, 1, 0.0)
            keep(nsel, [[-1, N_STATES], [0, P]], 0, 1, 0.0)
            c = len(sets) + 9
            pool.wait_ge(cdone, c)
            keep(mask[:, :, :], [[0, 2], [-1, KW]], WINDOW, 1, NEG)
            keep(mask0[:, :, :], [[0, 2], [-1, KW]], WINDOW, 1, NEG)
            keep(headsel[:, :], [[DH, HH]], DH - 1, -1, 0.0)
            keep(nsel, [[1, N_STATES], [0, P]], 0, -1, 0.0)
            pool.wait_ge(cdone, c + 4)
            keep(mask0[:, :, :], [[0, 2], [1, KW]], -WINDOW, 0, NEG)

            pool.wait_ge(w_in, 16 * W_LOADS)
            pool.wait_ge(wt, WT_ALL)
            pool.sem_inc(y_l, 3)
            pool.sem_inc(fs_l, 1)
            done = pool.alloc_register("later_pool")
            pool.reg_mov(done, 0)

            def norm(i, eps, n):
                b = min(i, 1)
                pool.wait_ge(aggr[i], n(aggr[i], T))
                pool.tensor_tensor(rstd[b][:, :], mv[b][:, :, 1], eps[:, :], ALU.add).then_inc(var[i], 1)
                pool.wait_ge(var[i], n(var[i], 1))
                pool.tensor_tensor(rstd[b][:, :], rstd[b][:, :], mhalf[:, :], ALU.pow).then_inc(rstd_s[i], 1)

            def queries(g, n):
                hf, a = g // (HH // G), g % (HH // G)
                pool.wait_ge(q_s, n(q_s, hf + 1))
                if g >= 2:
                    pool.wait_ge(s_ps, n(s_ps, T * (g - 1)))
                pool.tensor_tensor(qm[g % 2], qT[:, hf:hf + 1, :].to_broadcast([P, G, L]),
                                   headsel[:, a * G:(a + 1) * G].unsqueeze(2).to_broadcast([P, G, L]),
                                   ALU.mult).then_inc(qm_s, 1)

            def a(step, n):
                if step == "norm":
                    norm(0, eps1, n)
                elif step == "q":
                    queries(0, n)
                elif step == "k":
                    queries(1, n)
                elif step == "h":
                    normalise(0, n)
                    normalise(1, n)
                elif isinstance(step, int):
                    u = step
                    if u == 0:
                        pool.wait_ge(th_s, n(th_s, 2))
                        pool.tensor_tensor(th[:, :, :], xb[:, :, :], th[:, :, :], ALU.add).then_inc(xth, 1)
                    if u + 2 < NU:
                        normalise(u + 2, n)
                    if u % T == 1 and u // T + 2 < H // G:
                        queries(u // T + 2, n)

            def normalise(u, n):
                pool.wait_ge(prc_s, n(prc_s, u + 1))
                p = pr[u % 4][:, :, WINDOW:2 * P]
                pool.tensor_tensor(p, p, prc[:, u % 4, :].unsqueeze(2).to_broadcast([P, 2, KW]), ALU.mult).then_inc(pn, 1)

            c0 = [None] * NQ

            def b(step, n):
                if step == "norm":
                    norm(1, eps1, n)
                elif step == "xT":
                    pool.wait_ge(xn_s[1], n(xn_s[1], T))
                    pool.tensor_tensor(ysum[:, :, :], xn2[:, :, :], d_all[:, :].unsqueeze(1).to_broadcast([P, T, D]),
                                       ALU.mult).then_inc(yu, 1)
                elif step == "delta":
                    pool.wait_ge(delta_s, n(delta_s, 1))
                    pool.tensor_tensor(dsum[:, 1, :], delta[:, 2, :], delta[:, 3, :], ALU.add).then_inc(dsum_s, 1)
                    pool.wait_ge(dsum_s, n(dsum_s, 1))
                    pool.tensor_tensor(dsum[:, 0, :], delta[:, 1, :], dsum[:, 1, :], ALU.add).then_inc(dsum_s, 1)
                elif step == "g":
                    pool.tensor_tensor(gg[:, :, :], delta[:, :, :], xn2[:, :, :], ALU.mult).then_inc(g_s, 1)
                elif step == "start":
                    c0[:] = first_tiles(pool, n)
                elif step in ("out0", "out1", "out2", "out3"):
                    q = int(step[3:])
                    X = ee_t[q % 2]
                    pool.wait_ge(xx, n(xx, 2 * q + 2))
                    pool.tensor_tensor(X[:, 0:2, :], X[:, 0:2, :], X[:, 2:4, :], ALU.add).then_inc(ya, 1)
                    pool.wait_ge(ya, n(ya, 3 * q + 1))
                    pool.tensor_tensor(X[:, 0, :], X[:, 0, :], X[:, 1, :], ALU.add).then_inc(ya, 1)
                    pool.wait_ge(ya, n(ya, 3 * q + 2))
                    pool.sem_inc(passed, 1)
                    y = ysum[:, bass.ds(c0[q], 1), :]
                    pool.tensor_tensor(y, y, X[:, 0:1, :], ALU.add).then_inc(ya, 1)
                elif step == "later":
                    def later(q, c, k):
                        X = ee_t[0]
                        pool.wait_ge(ps_l, k + 1)
                        F = fsum[:, q, :].rearrange("p (a d) -> p a d", a=Q)
                        pool.tensor_tensor(F, F, f_later, ALU.add).then_inc(fs_l, 1)
                        pool.wait_ge(x_l, k + 2)
                        pool.tensor_tensor(X[:, 0:2, :], X[:, 0:2, :], X[:, 2:4, :], ALU.add).then_inc(y_l, 1)
                        pool.wait_ge(y_l, k * 3 + 4)
                        pool.tensor_tensor(X[:, 0, :], X[:, 0, :], X[:, 1, :], ALU.add).then_inc(y_l, 1)
                        pool.wait_ge(y_l, k * 3 + 5)
                        pool.sem_inc(passed, 1)
                        y = ysum[:, bass.ds(c, 1), :]
                        pool.tensor_tensor(y, y, X[:, 0:1, :], ALU.add).then_inc(y_l, 1)

                    later_tiles(pool, c0, done, later)
                elif step.startswith("mul"):
                    e = int(step[3:])
                    if e:
                        pool.wait_ge(m1_s, n(m1_s, e + 1))
                        if e > 1:
                            pool.wait_ge(moe_s, n(moe_s, e - 1))
                        pool.tensor_tensor(moe[:, :, :], moe[:, :, :], m1[:, e % 2, :, :], ALU.add).then_inc(moe_s, 1)
                elif step == "out":
                    norm(2, eps4, n)

            passes(pool, a, b)

        @block.scalar
        def _(act):
            act.wait_ge(w_in, 16 * W_LOADS)
            act.activation(aexp, alog, ACT.Exp).then_inc(wt, 1)
            act.mul(benc[:, :], benc[:, :], 0.5).then_inc(wt, 1)
            act.mul(bc2s[:, :], bc2s[:, :], 0.5).then_inc(wt, 1)
            act.mul(bqk[:, 0, :], bqk[:, 0, :], DH ** -0.5).then_inc(wt, 1)
            act.wait_ge(wt, WT_ALL)
            done = act.alloc_register("later_act")
            act.reg_mov(done, 0)

            def a(step, n):
                if step == "xT":
                    for c in range(KC):
                        act.wait_ge(xnT_ps[0], n(xnT_ps[0], c + 1))
                        act.activation(xnT[:, c, :], A[c], ACT.Copy).then_inc(xnT_s[0], 1)
                elif step == "q":
                    for hf in range(KC):
                        act.wait_ge(q_ps, n(q_ps, hf + 1))
                        act.activation(qT[:, hf, :], A[2 + hf], ACT.Identity, bias=bqk[:, 0, hf:hf + 1],
                                       scale=DH ** -0.5).then_inc(q_s, 1)
                elif step == "k":
                    for hf in range(KC):
                        act.wait_ge(k_ps, n(k_ps, hf + 1))
                        act.activation(kT[:, hf, WINDOW:WINDOW + L], A[hf], ACT.Identity,
                                       bias=bqk[:, 1, hf:hf + 1]).then_inc(k_s, 1)
                elif step == "h":
                    if n is not n0:
                        act.wait_ge(x1_c, n(x1_c, 0))
                    for k in range(2):
                        act.wait_ge(h_ps, n(h_ps, k + 1))
                        act.activation(th[:, 2 * k:2 * k + 2, :].rearrange("p t d -> p (t d)"), A[k], ACT.Tanh).then_inc(th_s, 1)
                    for u in range(AHEAD):
                        softmax_exp(u, n)
                elif step == "last":
                    aT_copy(1, n)
                elif isinstance(step, int):
                    if step + AHEAD < NU:
                        softmax_exp(step + AHEAD, n)
                    if step == NU // 2:
                        aT_copy(0, n)

            def softmax_exp(u, n):
                act.wait_ge(nmax_s, n(nmax_s, u + 1))
                if u >= 4:
                    act.wait_ge(pT_ps, n(pT_ps, u - 3))
                for i in range(2):
                    last = act.activation(pr[u % 4][:, i, WINDOW:2 * P], u_bank[u][:, KW * i:KW * (i + 1)], ACT.Exp,
                                          bias=nmax[:, u % 4, i:i + 1], accum_out=psm[:, u % 4, i:i + 1])
                last.then_inc(pexp, 1)

            def aT_copy(hf, n):
                act.wait_ge(pv, n(pv, NU // 2 * (hf + 1)))
                act.activation(aT[:, hf, :], O, ACT.Copy).then_inc(aT_s, 1)

            c0 = [None] * NQ

            def rates(step, m, ready, sig, bias, n):
                act.wait_ge(ready, n(ready, m + 1))
                act.activation(hidT[:, m, :], lb(step, 0)[0], ACT.Tanh, bias=bias[:, m:m + 1], scale=0.5).then_inc(sig, 1)

            def b(step, n):
                if step == "xT":
                    for c in range(KC):
                        act.wait_ge(xnT_ps[1], n(xnT_ps[1], c + 1))
                        act.activation(xn2T[:, c, :], lb("xT", c)[0], ACT.Copy).then_inc(xnT_s[1], 1)
                elif step == "keep":
                    act.wait_ge(xn_s[1], n(xn_s[1], T))
                    act.activation(x1[:, :, :], th[:, :, :], ACT.Copy).then_inc(x1_c, 1)
                elif step == "xd":
                    act.wait_ge(xd_ps, n(xd_ps, 1))
                    act.activation(xdT[:, :], lb("xd", 0)[0][0:XD, :], ACT.Copy).then_inc(xd_s, 1)
                elif step == "dt":
                    act.wait_ge(bc_ps, n(bc_ps, 1))
                    act.activation(bc[:, :, :].rearrange("p t n -> p (t n)"), lb("dt", 2)[0][:, 0:T * 2 * N_STATES],
                                   ACT.Copy).then_inc(bc_s, 1)
                elif step == "softplus":
                    act.wait_ge(z_s, n(z_s, 2))
                    act.activation(az[:, :, :], z[:, :, :], ACT.Abs).then_inc(az_s, 1)
                    act.wait_ge(az_s, n(az_s, 1))
                    act.activation(az[:, :, :], az[:, :, :], ACT.Exp, scale=-1.0).then_inc(ez_s, 1)
                elif step == "softplus2":
                    act.wait_ge(ez_s, n(ez_s, 1))
                    act.activation(az[:, :, :], az[:, :, :], ACT.Ln, bias=1.0).then_inc(lz_s, 1)
                elif step == "tail":
                    act.wait_ge(stored, n(stored, 16))
                    for k in range(2):
                        act.wait_ge(tail_ps, n(tail_ps, k + 1))
                        act.activation(tail[:, 2 * k:2 * k + 2, :].rearrange("p t d -> p (t d)"), lb("tail", k)[0],
                                       ACT.Copy).then_inc(tail_s, 1)
                elif step in ("exp0", "exp2"):
                    q0 = int(step[3:])
                    for q in (q0, q0 + 1):
                        act.wait_ge(et, n(et, q + 1))
                        act.activation(e_t[q % 2], e_t[q % 2], ACT.Exp, scale=-1.0).then_inc(ee1, 1)
                elif step in ("ln0", "ln2"):
                    q0 = int(step[2:])
                    for q in (q0, q0 + 1):
                        act.wait_ge(ee1, n(ee1, q + 1))
                        if q >= 2:
                            act.wait_ge(ya, n(ya, 3 * (q - 1)))
                        act.activation(ee_t[q % 2], e_t[q % 2], ACT.Ln, bias=SCAN_EPS).then_inc(ee2, 1)
                elif step in ("rc0", "rc2"):
                    q0 = int(step[2:])
                    for q in (q0, q0 + 1):
                        act.wait_ge(ee2, n(ee2, q + 1))
                        act.activation(ee_t[q % 2], ee_t[q % 2], ACT.Exp, scale=-1.0).then_inc(rc_s, 1)
                elif step == "later":
                    def later(q, c, k):
                        act.wait_ge(et_l, k + 1)
                        act.activation(e_t[0], e_t[0], ACT.Exp, scale=-1.0).then_inc(e_l, 1)
                        act.wait_ge(e_l, k + 1)
                        act.activation(ee_t[0], e_t[0], ACT.Ln, bias=SCAN_EPS).then_inc(ln_l, 1)
                        act.wait_ge(ln_l, k + 1)
                        act.activation(ee_t[0], ee_t[0], ACT.Exp, scale=-1.0).then_inc(rc_l, 1)

                    c0[:] = first_tiles(act, n)
                    later_tiles(act, c0, done, later)
                elif step == "yT":
                    for c in range(KC):
                        act.wait_ge(yT_ps, n(yT_ps, c + 1))
                        act.activation(yT[:, c, :], lb("yT", c)[0], ACT.Copy).then_inc(yT_s, 1)
                elif step.startswith("enc"):
                    rates(step, int(step[3:]), enc_ps, ts, benc, n)
                elif step == "cont":
                    act.wait_ge(cont_ps, n(cont_ps, 1))
                    act.activation(contT, lb("cont", 0)[0], ACT.Identity, bias=bs2c[:, :], scale=0.5).then_inc(cont_s, 1)
                elif step == "rh":
                    act.wait_ge(rh_ps, n(rh_ps, 1))
                    act.activation(rhT[0:MD, :], lb("rh", 0)[0][0:MD, :], ACT.Relu, bias=br1[:, :]).then_inc(rh_s, 1)
                elif step == "route":
                    act.wait_ge(route, n(route, 2))
                    act.activation(rt[:, 1, :], rt[:, 0, :], ACT.Exp).then_inc(rexp, 1)
                elif step.startswith("hid"):
                    x = int(step[3:])
                    act.wait_ge(e1_ps, n(e1_ps, x * EK + 1))
                    if x >= 2:
                        act.wait_ge(e2_ps, n(e2_ps, x - 1))
                    act.activation(eh[x % 2][:, 0, :], lb(step, 0)[0], ACT.Relu, bias=be1[:, x, 0:1]).then_inc(eha, 1)
                elif step == "mT":
                    act.wait_ge(mT_ps, n(mT_ps, 1))
                    act.activation(moeT, lb("mT", 0)[0], ACT.Copy).then_inc(mT_s, 1)
                elif step.startswith("c2s"):
                    rates(step, int(step[3:]), c2s_ps, tr, bc2s, n)
                elif step.startswith("dec"):
                    k = int(step[3:])
                    act.wait_ge(dec_ps, n(dec_ps, k + 1))
                    act.activation(td[:, 2 * k:2 * k + 2, :].rearrange("p t d -> p (t d)"), lb(step, 0)[0], ACT.Tanh,
                                   scale=0.25).then_inc(td_s, 1)

            passes(act, a, b)

        @block.vector
        def _(dve):
            dve.wait_ge(w_in, 16 * W_LOADS)
            dve.wait_ge(cdone, C_ALL)
            k = 4
            dve.wait_ge(wt, k)

            def prep(i, out_ap, in_ap):
                dve.wait_ge(wt_ps, i + 1)
                dve.tensor_copy(out_ap, in_ap).then_inc(wt, 1)

            prep(0, wqkvT[:, 0, :], ps[0][:, 0:768])
            prep(1, wqkvT[:, 1, :], ps[1][:, 0:768])
            prep(2, woaT[:, :, :, :].rearrange("p a k c -> p (a k c)"), ps[2][:, :])
            prep(3, wT.rearrange("p k c -> p (k c)"), ps[3][:, 0:512])
            prep(4, a12.rearrange("p k c -> p (k c)"), ps[0][:, 0:512])
            prep(5, wfused[:, :, :].rearrange("p k c -> p (k c)"), ps[1][:, 0:512])
            prep(6, aT16, ps[2][0:N_STATES, 0:D])
            for j in range(4):
                prep(7 + j, decay[:, 4 * j:4 * j + 4, :].rearrange("p n d -> p (n d)"), ps[3 if j % 2 else 0][:, :])
            dve.wait_ge(wt, 4 + 11)
            dve.tensor_reduce(least_a[:, :], decay[:, :, :].rearrange("p (q i) d -> p q (i d)", q=NQ), AX.X,
                              ALU.min).then_inc(wt, 1)
            dve.wait_ge(wt_ps, 12)
            dve.scalar_tensor_tensor(out=bs2c[:, :], in0=ps[1][:, 512:513], scalar=0.5, in1=bs2c[:, :],
                                     op0=ALU.mult, op1=ALU.add).then_inc(wt, 1)
            for i in range(2):
                dve.scalar_tensor_tensor(out=br[:, BDEC, i * D:(i + 1) * D], in0=br[:, BDEC, i * D:(i + 1) * D], scalar=2.0,
                                         in1=ps[1][:, 0:D], op0=ALU.mult, op1=ALU.add).then_inc(wt, 1)
            dve.tensor_tensor(br[:, BOUT1, :], br[:, BOUT1, :], ob[:, 0:2, :].rearrange("p a d -> p (a d)"),
                              ALU.add).then_inc(wt, 1)
            k = 4 + 11 + 5
            dve.wait_ge(wt, k)
            part = [qT[:, :, :].rearrange("p k l -> p (k l)")[:, 256 * i:256 * (i + 1)].bitcast(BF16) for i in range(2)]
            for kk in range(7):
                for j, r in enumerate(ROWS):
                    dve.tensor_copy(part[0], br[:, kk, :]).then_inc(wt, 1)
                    k += 1
                    dve.wait_ge(wt, k)
                    dve.tensor_copy(biasrow[r:r + 1, kk, :], part[0][r:r + 1, :]).then_inc(wt, 1)
                    dve.tensor_tensor(br[:, kk, :], br[:, kk, :], part[0], ALU.subtract).then_inc(wt, 1)
                    k += 2
                    dve.wait_ge(wt, k)
            for dst, src in ((we1[:, 0:E // 2, :].rearrange("p e h -> p (e h)"), flat[0]),
                             (we1[:, E // 2:E, :].rearrange("p e h -> p (e h)"), flat[1]), (wc2s[:, :], wc2s_n), (wr1[:, :], wr1_n)):
                first = x1[:, :, :].rearrange("p t d -> p (t d)")[:, 0:src.shape[1]]
                dve.tensor_copy(first.bitcast(F32R), src).then_inc(wt, 1)
                k += 1
                dve.wait_ge(wt, k)
                dve.tensor_copy(dst[0:MD, :], first[0:MD, :]).then_inc(wt, 1)
                dve.tensor_tensor(dst[MD:P, :], src[MD:P, :], first[MD:P, :], ALU.subtract).then_inc(wt, 1)
                k += 2
                dve.wait_ge(wt, k)
            assert k == WT_ALL, k

            dve.sem_inc(x_l, 1)
            done = dve.alloc_register("later_dve")
            dve.reg_mov(done, 0)

            def norm(i, src, ready, count, n):
                b = min(i, 1)
                for t in range(T):
                    dve.wait_ge(ready, n(ready, count(t)))
                    dve.bn_stats(stat[b][:, t, :], src[:, t, :]).then_inc(stats[i], 1)
                for t in range(T):
                    dve.wait_ge(stats[i], n(stats[i], t + 1))
                    dve.sem_inc(passed, 1)
                    dve.bn_aggr(mv[b][:, t, :], stat[b][:, t, :]).then_inc(aggr[i], 1)

            def normal(i, dst, src, n):
                b = min(i, 1)
                dve.wait_ge(rstd_s[i], n(rstd_s[i], 1))
                for t in range(T):
                    dve.tensor_scalar(dst[:, t, :], src[:, t, :], mv[b][:, t, 0:1], rstd[b][:, t:t + 1], ALU.subtract,
                                      ALU.mult).then_inc(xn_s[i], 1)

            def row_max(u, n):
                dve.wait_ge(s_ps, n(s_ps, u + 1))
                dve.tensor_reduce(nmax[:, u % 4, :], u_bank[u][:, 0:2 * KW].rearrange("p (i k) -> p i k", i=2), AX.X,
                                  ALU.max, negate=True).then_inc(nmax_s, 1)

            def a(step, n):
                if step == "norm":
                    norm(0, xb, x_in_s, lambda t: 16, n)
                    normal(0, xn, xb, n)
                elif step == "v":
                    for k in range(2):
                        dve.wait_ge(v_ps, n(v_ps, k + 1))
                        for par in range(2):
                            vsrc = A[2 + k].rearrange("p (t g b d) -> p t g b d", t=2, g=H // 2, b=2)[:, :, :, par, :]
                            vdst = vh[:, 2 * k:2 * k + 2, :, :].rearrange("p t (g b) (c d) -> p t g b c d", b=2, c=2)
                            dve.tensor_copy(vdst[:, :, :, par, par, :], vsrc).then_inc(v_s, 1)
                elif step == "h":
                    for u in range(AHEAD):
                        row_max(u, n)
                    for u in range(2):
                        sums(u, n)
                elif step == "close":
                    for k in range(2):
                        dve.wait_ge(y0_ps, n(y0_ps, k + 1))
                        x = th[:, 2 * k:2 * k + 2, :].rearrange("p t d -> p (t d)")
                        dve.tensor_tensor(x, x, A[2 + k], ALU.add).then_inc(x1_s, 1)
                elif isinstance(step, int):
                    u = step
                    t = UNITS[u][2]
                    if u + 2 < NU:
                        sums(u + 2, n)
                    dve.wait_ge(pT_ps, n(pT_ps, u + 1))
                    if u >= 2:
                        dve.wait_ge(pv, n(pv, u - 1))
                    w0 = 1 if t == 0 else 0
                    src = u_bank[u].rearrange("p (i w l) -> p i w l", i=2, w=2)
                    dve.tensor_copy(prT[u % 2][:, :, w0:2, :], src[:, :, w0:2, :]).then_inc(pT_s, 1)
                    if u + AHEAD < NU:
                        row_max(u + AHEAD, n)

            def sums(u, n):
                dve.wait_ge(pexp, n(pexp, u + 1))
                dve.reciprocal(prc[:, u % 4, :], psm[:, u % 4, :]).then_inc(prc_s, 1)

            c0 = [None] * NQ

            def exponents(q, c, dst):
                return dve.tensor_tensor(dst, tail[:, bass.ds(c, 1), :].to_broadcast([P, Q, D]),
                                         decay[:, q * Q:(q + 1) * Q, :], ALU.mult)

            def inputs(q, c, src, dst):
                for i in range(Q):
                    s = q * Q + i
                    last = dve.scalar_tensor_tensor(out=dst[:, i, :], in0=src[:, i, :],
                                                    scalar=bc[:, bass.ds(c, 1), s:s + 1].rearrange("p a n -> p (a n)"),
                                                    in1=gg[:, bass.ds(c, 1), :].rearrange("p a d -> p (a d)"),
                                                    op0=ALU.mult, op1=ALU.mult)
                return last

            def outputs(q, c, i, src, dst):
                for k in range(2):
                    s = N_STATES + q * Q + i + k
                    last = dve.scalar_tensor_tensor(out=dst[:, i + k, :], in0=src[:, k * D:(k + 1) * D],
                                                    scalar=bc[:, bass.ds(c, 1), s:s + 1].rearrange("p a n -> p (a n)"),
                                                    in1=dst[:, i + k, :], op0=ALU.mult, op1=ALU.mult)
                return last

            def split(ready, j, n):
                dve.wait_ge(ready, n(ready, 1))
                dve.tensor_copy(firstT[:, :], contT).then_inc(split_s, 1)
                dve.wait_ge(split_s, n(split_s, j + 1))
                dve.tensor_tensor(restT[:, :], contT, firstT[:, :].bitcast(F32), ALU.subtract).then_inc(split_s, 1)

            def b(step, n):
                if step == "split":
                    split(cont_s, 0, n)
                elif step == "msplit":
                    split(mT_s, 2, n)
                elif step == "norm":
                    norm(1, th, x1_s, lambda t: t // 2 + 1, n)
                    normal(1, xn2, th, n)
                elif step == "dt":
                    for k in range(2):
                        dve.wait_ge(dt_ps, n(dt_ps, k + 1))
                        dve.tensor_copy(z[:, 2 * k:2 * k + 2, :].rearrange("p t d -> p (t d)"), lb("dt", k)[0]).then_inc(z_s, 1)
                elif step == "delta":
                    dve.wait_ge(lz_s, n(lz_s, 1))
                    dve.scalar_tensor_tensor(out=delta[:, :, :], in0=z[:, :, :], scalar=0.0, in1=az[:, :, :], op0=ALU.max,
                                             op1=ALU.add).then_inc(delta_s, 1)
                elif step == "first":
                    rows = slice(P - 32, P)
                    dve.wait_ge(tail_s, n(tail_s, 2))
                    dve.tensor_reduce(least_t[rows, :], tail[rows, 0:T - 1, :], AX.X, ALU.min).then_inc(first_s, 1)
                    for c in range(1, T - 1):
                        dve.wait_ge(first_s, n(first_s, c))
                        dve.tensor_tensor(least_t[rows, c:c + 1], least_t[rows, c:c + 1], least_t[rows, c - 1:c],
                                          ALU.min).then_inc(first_s, 1)
                    dve.wait_ge(first_s, n(first_s, T - 1))
                    dve.tensor_tensor(past[rows, :, :], least_t[rows, :].unsqueeze(1).to_broadcast([32, NQ, T - 1]),
                                      least_a[rows, :].unsqueeze(2).to_broadcast([32, NQ, T - 1]), ALU.mult).then_inc(first_s, 1)
                    dve.wait_ge(first_s, n(first_s, T))
                    dve.tensor_scalar(past[rows, :, :], past[rows, :, :], ZERO_FROM, None, ALU.is_gt).then_inc(first_s, 1)
                    dve.wait_ge(first_s, n(first_s, T + 1))
                    with nc.allow_low_precision("counts of at most three"):
                        dve.tensor_reduce(first_c[rows, :], past[rows, :, :], AX.X, ALU.add).then_inc(first_s, 1)
                elif step == "start":
                    c0[:] = first_tiles(dve, n)
                elif step == "exp0":
                    dve.wait_ge(g_s, n(g_s, 1))
                    dve.wait_ge(bc_s, n(bc_s, 1))
                    for q in range(2):
                        exponents(q, c0[q], e_t[q]).then_inc(et, 1)
                elif step in ("in0", "in1", "in2", "in3"):
                    q = int(step[2:])
                    F = fsum[:, q, :].rearrange("p (i d) -> p i d", i=Q)
                    dve.wait_ge(ee1, n(ee1, q + 1))
                    inputs(q, c0[q], e_t[q % 2], F).then_inc(f_s, 1)
                    if q + 2 < NQ:
                        dve.wait_ge(f_s, n(f_s, q + 1))
                        dve.wait_ge(ee2, n(ee2, q + 1))
                        exponents(q + 2, c0[q + 2], e_t[q % 2]).then_inc(et, 1)
                elif step in ("out0", "out1", "out2", "out3"):
                    q = int(step[3:])
                    dve.wait_ge(rc_s, n(rc_s, q + 1))
                    for i in range(2):
                        dve.wait_ge(sc_ps, n(sc_ps, 2 * q + i + 1))
                        outputs(q, c0[q], 2 * i, lb(f"sum{q}", i)[0], ee_t[q % 2]).then_inc(xx, 1)
                elif step == "later":
                    def later(q, c, k):
                        dve.wait_ge(y_l, k * 3 + 3)
                        exponents(q, c, e_t[0]).then_inc(et_l, 1)
                        dve.wait_ge(e_l, k + 1)
                        inputs(q, c, e_t[0], f_later).then_inc(f_l, 1)
                        dve.wait_ge(rc_l, k + 1)
                        dve.wait_ge(ps_l, k + 1)
                        for i in range(2):
                            last = outputs(q, c, 2 * i, lb("later", i)[0], ee_t[0])
                        last.then_inc(x_l, 1)

                    dve.wait_ge(ya, n(ya, 3 * NQ))
                    dve.sem_inc(passed, 1)
                    later_tiles(dve, c0, done, later)
                elif step in ("y1a", "y1b"):
                    k = ("y1a", "y1b").index(step)
                    dve.wait_ge(x1_c, n(x1_c, 1))
                    dve.wait_ge(y1_ps, n(y1_ps, k + 1))
                    x = x1[:, 2 * k:2 * k + 2, :].rearrange("p t d -> p (t d)")
                    dve.tensor_tensor(x, x, lb(step, 0)[0], ALU.add).then_inc(x2_s, 1)
                elif step in ("route", "shares"):
                    lg = lb("logits", 0)[0][:, 0:T * E].rearrange("p (t e) -> p t e", t=T)
                    r3 = [rt[:, j, :].rearrange("p (t e) -> p t e", t=T) for j in range(5)]
                    pr3 = [pair[:, j, :].rearrange("p (i e) -> p i e", e=E) for j in range(2)]
                    p4 = [pair[:, j, :].rearrange("p (t i e) -> p t i e", t=T, e=E) for j in range(2)]
                    lj = r3[0].unsqueeze(2).to_broadcast([P, T, E, E])
                    li = r3[0].unsqueeze(3).to_broadcast([P, T, E, E])

                    def after_step(k):
                        dve.wait_ge(route, n(route, k))

                if step == "route":
                    dve.wait_ge(lg_ps, n(lg_ps, 1))
                    dve.tensor_reduce(rs[:, 0, :], lg, AX.X, ALU.max).then_inc(route, 1)
                    after_step(1)
                    dve.tensor_tensor(r3[0], lg, rs[:, 0, :].unsqueeze(2).to_broadcast([P, T, E]), ALU.subtract).then_inc(route, 1)
                    after_step(2)
                    dve.tensor_tensor(p4[0], lj, li, ALU.is_gt).then_inc(route, 1)
                    dve.tensor_tensor(p4[1], lj, li, ALU.is_equal).then_inc(route, 1)
                    after_step(4)
                    dve.tensor_tensor(pr3[1], pr3[1], lower[:, :, :], ALU.mult).then_inc(route, 1)
                    after_step(5)
                    dve.tensor_tensor(pr3[0], pr3[0], pr3[1], ALU.add).then_inc(route, 1)
                    after_step(6)
                    dve.tensor_reduce(rt[:, 2, :], pr3[0], AX.X, ALU.add).then_inc(route, 1)
                elif step == "shares":
                    after_step(7)
                    dve.wait_ge(rexp, n(rexp, 1))
                    dve.scalar_tensor_tensor(out=rt[:, 3, :], in0=rt[:, 2, :], scalar=2.0, in1=rt[:, 1, :], op0=ALU.is_lt,
                                             op1=ALU.mult).then_inc(route, 1)
                    after_step(8)
                    dve.tensor_reduce(rs[:, 1, :], r3[3], AX.X, ALU.add).then_inc(route, 1)
                    after_step(9)
                    dve.reciprocal(rs[:, 2, :], rs[:, 1, :]).then_inc(route, 1)
                    after_step(10)
                    dve.tensor_tensor(r3[4], r3[3], rs[:, 2, :].unsqueeze(2).to_broadcast([P, T, E]), ALU.mult).then_inc(route, 1)
                elif step.startswith("hid"):
                    x = int(step[3:])
                    dve.wait_ge(e1_ps, n(e1_ps, x * EK + 2))
                    if x >= 2:
                        dve.wait_ge(e2_ps, n(e2_ps, x - 1))
                    dve.tensor_scalar(eh[x % 2][:, 1, :], lb(step, 1)[0], be1[:, x, 1:2], 0.0, ALU.add,
                                      ALU.max).then_inc(ehv, 1)
                elif step.startswith("mul"):
                    e = int(step[3:])
                    dve.wait_ge(e2_ps, n(e2_ps, e + 1))
                    if e == 0:
                        dve.wait_ge(route, n(route, 11))
                    if e >= 3:
                        dve.wait_ge(moe_s, n(moe_s, e - 2))
                    share = rt[:, 4, :].rearrange("p (t e) -> p t e", t=T)[:, :, e:e + 1].to_broadcast([P, T, MD])
                    dst = moe[:, :, :] if e == 0 else m1[:, e % 2, :, :]
                    dve.tensor_tensor(dst, lb(f"mix{e}", 0)[0][:, 0:T * MD].rearrange("p (t d) -> p t d", t=T), share,
                                      ALU.mult).then_inc(m1_s, 1)
                elif step == "out":
                    norm(2, td, td_s, lambda t: t // 2 + 1, n)
                    dve.wait_ge(rstd_s[2], n(rstd_s[2], 1))
                    for t in range(T):
                        dve.scalar_tensor_tensor(out=td[:, t, :], in0=td[:, t, :], scalar=mv[1][:, t, 0:1], in1=lng_all[:, :],
                                                 op0=ALU.subtract, op1=ALU.mult).then_inc(n3, 1)
                    for t in range(T):
                        dve.wait_ge(n3, n(n3, t + 1))
                        dve.scalar_tensor_tensor(out=ob[:, t, :], in0=td[:, t, :], scalar=rstd[1][:, t:t + 1], in1=x1[:, t, :],
                                                 op0=ALU.mult, op1=ALU.add).then_inc(out_s, 1)

            passes(dve, a, b)

        @block.tensor
        def _(pe):
            pe.wait_ge(w_in, 16 * W_LOADS)
            pe.wait_ge(cdone, C_ALL)
            for k in range(KC):
                for m in range(6):
                    mm = pe.transpose(ps[k][:, m * P:(m + 1) * P], wqkv_n[:, m, k * P:(k + 1) * P], ident[:, :])
                mm.then_inc(wt_ps, 1)
            for j, src in enumerate((wo_n, a1_n)):
                for k in range(KC):
                    for m in range(KC):
                        mm = pe.transpose(ps[2][:, 512 * j + k * D + m * P:512 * j + k * D + (m + 1) * P],
                                          src[:, m, k * P:(k + 1) * P], ident[:, :])
            mm.then_inc(wt_ps, 1)
            for k in range(KC):
                for m in range(KC):
                    mm = pe.transpose(ps[3][:, k * D + m * P:k * D + (m + 1) * P], w_n[:, m, k * P:(k + 1) * P], ident[:, :])
            mm.then_inc(wt_ps, 1)
            pe.wait_ge(wt, 4 + 3)
            for m in range(KC):
                for k in range(KC):
                    mm = pe.matmul(ps[0][:, m * D:(m + 1) * D], woaT[:, 1, k, m * P:(m + 1) * P], a2_n[:, k, :],
                                   start=k == 0, stop=k == KC - 1)
            mm.then_inc(wt_ps, 1)
            pe.wait_ge(wt, 4 + 5)
            for m in range(KC):
                for k in range(KC):
                    mm = pe.matmul(ps[1][:, m * D:(m + 1) * D], wT[:, k, m * P:(m + 1) * P], a12[:, k, :],
                                   start=k == 0, stop=k == KC - 1)
            mm.then_inc(wt_ps, 1)
            for k in range(KC):
                mm = pe.transpose(ps[2][0:N_STATES, k * P:(k + 1) * P], aexp[:, k, :], ident[:, :])
            mm.then_inc(wt_ps, 1)
            pe.wait_ge(wt, 4 + 7)
            for j in range(4):
                if j >= 2:
                    pe.wait_ge(wt, 4 + 7 + j - 1)
                for i in range(4):
                    mm = pe.matmul(ps[3 if j % 2 else 0][:, i * D:(i + 1) * D], nsel[:, 4 * j + i, :], aT16,
                                   start=True, stop=True)
                mm.then_inc(wt_ps, 1)
            for k in range(MH):
                pe.matmul(ps[1][:, 0:D], ones[:, :], wdec[:, k, :], start=k == 0, stop=k == MH - 1)
            for k in range(MH):
                mm = pe.matmul(ps[1][:, 512:513], ws2c[:, k, :, :].rearrange("p a d -> p (a d)"), ones[:, 0:1],
                               start=k == 0, stop=k == MH - 1)
            mm.then_inc(wt_ps, 1)
            pe.wait_ge(wt, WT_ALL)

            def half(bk, lhsT, rhs, k_n, k, t0):
                pe.matmul(bk, ones16[:, :], biasrow[:, k, :], start=True, stop=False)
                for t in (t0, t0 + 1):
                    for c in range(k_n):
                        mm = pe.matmul(bk[:, (t - t0) * D:(t - t0 + 1) * D], lhsT[:, c, t * P:(t + 1) * P], rhs[:, c, :],
                                       start=False, stop=c == k_n - 1 and t > t0)
                return mm

            def two_parts(bk, weights):
                pe.matmul(bk, weights, firstT[:, :], start=True, stop=False)
                return pe.matmul(bk, weights, restT[:, :], start=False, stop=True)

            done = pe.alloc_register("later_pe")
            pe.reg_mov(done, 0)

            def scores(u, n):
                hf, j, t = UNITS[u]
                g = u // T
                pe.wait_ge(qm_s, n(qm_s, g + 1))
                if u == 0:
                    pe.wait_ge(k_s, n(k_s, KC))
                    pe.wait_ge(v_s, n(v_s, 2))
                elif u == 1:
                    pe.wait_ge(v_s, n(v_s, 4))
                elif u in (2, 3):
                    pe.wait_ge(th_s, n(th_s, u - 1))
                else:
                    pe.wait_ge(pT_s, n(pT_s, u - 3))
                pe.matmul(u_bank[u][:, 0:2 * KW], ident16[:, :], (mask if t else mask0)[:, :, :].rearrange("p a k -> p (a k)"),
                          start=True, stop=False)
                for i in range(2):
                    mm = pe.matmul(u_bank[u][:, KW * i:KW * (i + 1)], qm[g % 2][:, i, t * P:(t + 1) * P],
                                   kT[:, hf, t * P:t * P + KW], start=False, stop=i == 1)
                mm.then_inc(s_ps, 1)

            def weighted(u, n):
                hf, j, t = UNITS[u]
                pe.wait_ge(pT_s, n(pT_s, u + 1))
                if u == NU // 2:
                    pe.wait_ge(aT_s, n(aT_s, 1))
                todo = [(i, v) for i in range(2) for v in range(0 if t else 1, 2)]
                for i, v in todo:
                    mm = pe.matmul(O[32 * j:32 * j + 32, t * P:(t + 1) * P], vh[:, t - 1 + v, hf * HH + 2 * j + i, :],
                                   prT[u % 2][:, i, v, :], start=(i, v) == todo[0], stop=(i, v) == todo[-1])
                mm.then_inc(pv, 1)

            def a(step, n):
                if step == "xT":
                    pe.wait_ge(xn_s[0], n(xn_s[0], T))
                    for c in range(KC):
                        for t in range(T):
                            mm = pe.transpose(A[c][:, t * P:(t + 1) * P], xn[:, t, c * P:(c + 1) * P], ident[:, :])
                        mm.then_inc(xnT_ps[0], 1)
                elif step in ("q", "k"):
                    c0, b0, sig = (0, 2, q_ps) if step == "q" else (D, 0, k_ps)
                    if step == "q" and n is not n0:
                        pe.wait_ge(x1_s, n(x1_s, 0))
                    for c in range(KC):
                        pe.wait_ge(xnT_s[0], n(xnT_s[0], c + 1))
                        for hf in range(KC):
                            mm = pe.matmul(A[b0 + hf], wqkvT[:, c, c0 + hf * P:c0 + (hf + 1) * P], xnT[:, c, :],
                                           start=c == 0, stop=c == KC - 1)
                            if c == KC - 1:
                                mm.then_inc(sig, 1)
                elif step == "v":
                    for k in range(2):
                        pe.wait_ge(q_s, n(q_s, k + 1))
                        half(A[2 + k], xnT, wqkvT[:, :, 2 * D:3 * D], KC, BV, 2 * k).then_inc(v_ps, 1)
                elif step == "h":
                    for k in range(2):
                        pe.wait_ge(k_s, n(k_s, k + 1))
                        half(A[k], xnT, wfused, KC, BFFN, 2 * k).then_inc(h_ps, 1)
                    for u in range(AHEAD):
                        scores(u, n)
                elif step == "last":
                    weighted(NU - 1, n)
                elif step == "close":
                    pe.wait_ge(aT_s, n(aT_s, 2))
                    for k in range(2):
                        half(A[2 + k], aT, woaT[:, 0, :, :], KC, BOUT, 2 * k).then_inc(y0_ps, 1)
                elif isinstance(step, int):
                    u = step
                    t = UNITS[u][2]
                    pe.wait_ge(pn, n(pn, u + 1))
                    for i in range(2):
                        for v in range(0 if t else 1, 2):
                            mm = pe.transpose(u_bank[u][:, (2 * i + v) * P:(2 * i + v + 1) * P],
                                              pr[u % 4][:, i, v * P:(v + 1) * P], ident[:, :])
                    mm.then_inc(pT_ps, 1)
                    if u + AHEAD < NU:
                        scores(u + AHEAD, n)
                    if u:
                        weighted(u - 1, n)

            c0s = [None] * NQ
            later_units = []

            def use(step, i, n):
                bk, u = lb(step, i)
                if u >= 3:
                    _, s, k = USES[u - 3][2]
                    if s is x_l:
                        pe.wait_ge(x_l, later_units[0] + 1)
                        pe.sem_inc(passed, 1)
                    else:
                        pe.wait_ge(s, n(s, k))
                return bk

            def b(step, n):
                if step == "xT":
                    pe.wait_ge(xn_s[1], n(xn_s[1], T))
                    for c in range(KC):
                        bk = use("xT", c, n)
                        for t in range(T):
                            mm = pe.transpose(bk[:, t * P:(t + 1) * P], xn2[:, t, c * P:(c + 1) * P], ident[:, :])
                        mm.then_inc(xnT_ps[1], 1)
                elif step == "xd":
                    pe.wait_ge(xnT_s[1], n(xnT_s[1], KC))
                    bk = use("xd", 0, n)
                    for c in range(KC):
                        mm = pe.matmul(bk[0:XD, :], wx[:, c, :], xn2T[:, c, :], start=c == 0, stop=c == KC - 1)
                    mm.then_inc(xd_ps, 1)
                elif step == "dt":
                    pe.wait_ge(xd_s, n(xd_s, 1))
                    for k in range(2):
                        bk = use("dt", k, n)
                        pe.matmul(bk, ones16[:, :], biasrow[:, BDT, :], start=True, stop=False)
                        for t in (2 * k, 2 * k + 1):
                            mm = pe.matmul(bk[:, (t - 2 * k) * D:(t - 2 * k + 1) * D], xdT[0:RANK, t * P:(t + 1) * P], wdt[:, :],
                                           start=False, stop=t > 2 * k)
                        mm.then_inc(dt_ps, 1)
                    bk = use("dt", 2, n)
                    pe.sem_inc(passed, 1)
                    for t in range(T):
                        mm = pe.transpose(bk[:, t * 2 * N_STATES:(t + 1) * 2 * N_STATES], xdT[RANK:XD, t * P:(t + 1) * P],
                                          ident[RANK:XD, RANK:XD])
                    mm.then_inc(bc_ps, 1)
                elif step == "tail":
                    pe.wait_ge(dsum_s, n(dsum_s, 2))
                    for k in range(2):
                        bk = use("tail", k, n)
                        two = slice(2 * k, 2 * k + 2)
                        pe.matmul(bk, after[:, :], delta[:, two, :].rearrange("p t d -> p (t d)"), start=True, stop=False)
                        if k == 0:
                            mm = pe.matmul(bk, ones[:, :], dsum[:, :, :].rearrange("p t d -> p (t d)"), start=False, stop=True)
                        else:
                            mm = pe.matmul(bk[:, 0:D], ones[:, :], delta[:, 3, :], start=False, stop=True)
                        mm.then_inc(tail_ps, 1)
                elif step.startswith("sum"):
                    q = int(step[3:])
                    pe.wait_ge(f_s, n(f_s, q + 1))
                    for i in range(2):
                        pe.matmul(use(step, i, n), upto[:, :], fsum[:, q, 512 * i:512 * (i + 1)],
                                  start=True, stop=True).then_inc(sc_ps, 1)
                elif step == "later":
                    c0s[:] = first_tiles(pe, n)
                    for i in range(2):
                        use("later", i, n)
                    pe.wait_ge(xx, n(xx, 2 * NQ))
                    pe.sem_inc(passed, 1)

                    def later(q, c, k):
                        pe.wait_ge(x_l, k + 1)
                        pe.wait_ge(fs_l, k + 1)
                        for i in range(2):
                            pe.matmul(lb("later", i)[0], ones[:, :], fsum[:, q, 512 * i:512 * (i + 1)], start=True, stop=False)
                        pe.wait_ge(f_l, k + 1)
                        for i in range(2):
                            mm = pe.matmul(lb("later", i)[0], upto[:, :], f_later.rearrange("p q d -> p (q d)")[:, 512 * i:512 * (i + 1)],
                                           start=False, stop=True)
                        mm.then_inc(ps_l, 1)

                    later_units[:] = [later_tiles(pe, c0s, done, later)]
                elif step == "yT":
                    pe.wait_ge(ya, n(ya, 3 * NQ))
                    pe.wait_ge(y_l, later_units[0] * 3 + 3)
                    for c in range(KC):
                        bk = use("yT", c, n)
                        for t in range(T):
                            mm = pe.transpose(bk[:, t * P:(t + 1) * P], ysum[:, t, c * P:(c + 1) * P], ident[:, :])
                        mm.then_inc(yT_ps, 1)
                elif step in ("y1a", "y1b"):
                    k = ("y1a", "y1b").index(step)
                    pe.wait_ge(yT_s, n(yT_s, KC))
                    pe.sem_inc(passed, 1)
                    half(use(step, 0, n), yT, wo1, KC, BOUT1, 2 * k).then_inc(y1_ps, 1)
                elif step.startswith("enc"):
                    m = int(step[3:])
                    bk = use(step, 0, n)
                    for c in range(KC):
                        mm = pe.matmul(bk, wenc[:, c, m * P:(m + 1) * P], xn2T[:, c, :], start=c == 0, stop=c == KC - 1)
                    mm.then_inc(enc_ps, 1)
                elif step == "cont":
                    bk = use("cont", 0, n)
                    pe.sem_inc(passed, 1)
                    for m in range(MH):
                        pe.wait_ge(ts, n(ts, m + 1))
                        mm = pe.matmul(bk, ws2c[:, m, :, :].rearrange("p a d -> p (a d)"), hidT[:, m, :],
                                       start=m == 0, stop=m == MH - 1)
                    mm.then_inc(cont_ps, 1)
                elif step == "rh":
                    pe.wait_ge(split_s, n(split_s, 2))
                    two_parts(use("rh", 0, n)[0:MD, :], wr1[:, :]).then_inc(rh_ps, 1)
                elif step == "logits":
                    pe.wait_ge(rh_s, n(rh_s, 1))
                    bk = use("logits", 0, n)
                    for t in range(T):
                        mm = pe.matmul(bk[:, t * E:(t + 1) * E], rhT[:, t * P:(t + 1) * P], wr2[:, :], start=True, stop=True)
                    mm.then_inc(lg_ps, 1)
                elif step.startswith("hid"):
                    e = int(step[3:])
                    for k in range(EK):
                        two_parts(use(step, k, n), we1[:, e, k * P:(k + 1) * P]).then_inc(e1_ps, 1)
                elif step.startswith("mix"):
                    e = int(step[3:])
                    bk = use(step, 0, n)
                    pe.sem_inc(passed, 1)
                    pe.wait_ge(eha, n(eha, e + 1))
                    pe.wait_ge(ehv, n(ehv, e + 1))
                    pe.matmul(bk[:, 0:T * MD].rearrange("p (t d) -> p t d", t=T), ones16[:, :],
                              biasrow[:, BE2, e * MD:(e + 1) * MD].unsqueeze(1).to_broadcast([P, T, MD]), start=True, stop=False)
                    for t in range(T):
                        for k in range(EK):
                            mm = pe.matmul(bk[:, t * MD:(t + 1) * MD], eh[e % 2][:, k, t * P:(t + 1) * P], we2[:, e, k, :],
                                           start=False, stop=t == T - 1 and k == EK - 1)
                    mm.then_inc(e2_ps, 1)
                elif step == "mT":
                    pe.wait_ge(moe_s, n(moe_s, E - 1))
                    bk = use("mT", 0, n)
                    pe.sem_inc(passed, 1)
                    for t in range(T):
                        for rows in (slice(0, MD), slice(MD, P)):
                            mm = pe.matmul(bk[rows, t * P:(t + 1) * P], moe[:, t, :], ident[:, :],
                                           start=True, stop=True)
                    mm.then_inc(mT_ps, 1)
                elif step.startswith("c2s"):
                    m = int(step[3:])
                    pe.wait_ge(split_s, n(split_s, 4))
                    two_parts(use(step, 0, n), wc2s[:, m * P:(m + 1) * P]).then_inc(c2s_ps, 1)
                elif step.startswith("dec"):
                    k = int(step[3:])
                    pe.wait_ge(tr, n(tr, MH))
                    half(use(step, 0, n), hidT, wdec, MH, BDEC, 2 * k).then_inc(dec_ps, 1)

            passes(pe, a, b)


def kernel(**inputs):
    import numpy as _np
    import concourse.bacc as _bacc
    from concourse import mybir as _mybir
    from concourse.bass_utils import run_bass_kernel_spmd as _run

    nc = _bacc.Bacc("TRN2", target_bir_lowering=False, num_devices=1)
    arrays, args = {}, {}
    for name in inputs:
        a = _np.ascontiguousarray(inputs[name])
        arrays[f"in_{name}_dram"] = a
        args[name] = nc.dram_tensor(f"in_{name}_dram", a.shape, _mybir.dt.from_np(a.dtype), kind="ExternalInput").ap()
    x = args.pop("L0_attn_x")
    out = nc.dram_tensor("out_0_dram", x.shape, _mybir.dt.float32, kind="ExternalOutput").ap()
    layered_kernel(nc, x, args, out)
    r = _run(nc, [arrays], core_ids=[0])
    return r.results[0]["out_0_dram"]
```
